# Optimizing a Trainium2 kernel written in Bass

```python
import numpy as np
import jax
import jax.numpy as jnp

def _softmax(x, axis=-1):
    return jax.nn.softmax(x, axis=axis)

def _gelu(x):
    return jax.nn.gelu(x, approximate=True)

def _silu(x):
    return jax.nn.silu(x)

def _sigmoid(x):
    return jax.nn.sigmoid(x)

def _layernorm(x, axis=-1, eps=1e-05):
    m = jnp.mean(x, axis=axis, keepdims=True)
    v = jnp.var(x, axis=axis, keepdims=True)
    return (x - m) / jnp.sqrt(v + eps)

def _scatter_add(tgt, idx, src, axis=0):
    return tgt.at[idx].add(src)

def _segment_sum(src, seg, n):
    return jax.ops.segment_sum(src, seg, n)
kernel_name = 'mk_xattn_ffn_d2_seqx_r8_a09938'

def setup_inputs(seed: int=0):
    np.random.seed(seed)
    _w = jnp.asarray

    def _rec_inputs():
        import jax
        import jax.numpy as jnp
        _rk = jax.random.key(seed)
        x = -0.0001538 + 1 * jax.random.normal(jax.random.fold_in(_rk, 1), (32, 128, 128), jnp.float32)
        _lenS = 128 - jax.random.randint(jax.random.fold_in(_rk, 7), (32,), 0, max(1, 128 // 4) + 1, jnp.int32)
        _lenS2 = 128 - jax.random.randint(jax.random.fold_in(_rk, 8), (32,), 0, max(1, 128 // 4) + 1, jnp.int32)
        _ctx_1024P = jax.random.normal(jax.random.fold_in(_rk, 11), (32, 16, 128), jnp.float32)
        _ctx_1024c = jax.random.dirichlet(jax.random.fold_in(_rk, 511), 0.3 * jnp.ones((16,), jnp.float32), (32, 128))
        _ctx_1024t = jnp.einsum('bsk,bkd->bsd', _ctx_1024c, _ctx_1024P)
        _ctx_1024t = _ctx_1024t * jax.lax.rsqrt(jnp.mean(jnp.square(_ctx_1024t)) + 1e-12) * 0.953939
        ctx_1024 = -0.000191848 + 0.999787 * (_ctx_1024t + 0.3 * jax.random.normal(jax.random.fold_in(_rk, 611), (32, 128, 128), jnp.float32))
        return (x, ctx_1024)
    x, ctx_1024 = _rec_inputs()

    def _L0_xattn_setup():
        import jax, jax.numpy as jnp
        import numpy as np
        EMBED_DIM = 128
        NUM_HEADS = 16
        THETA = 10000.0

        def apply_rope(x):
            B, T, C = x.shape
            freqs = 1.0 / THETA ** (jnp.arange(0, C, 2, dtype=jnp.float32) / C)
            t = jnp.arange(T, dtype=jnp.float32)
            ang = jnp.outer(t, freqs)
            cosv, sinv = (jnp.cos(ang), jnp.sin(ang))
            xr = x.reshape(B, T, C // 2, 2)
            real = xr[..., 0] * cosv - xr[..., 1] * sinv
            imag = xr[..., 0] * sinv + xr[..., 1] * cosv
            return jnp.stack([real, imag], axis=-1).reshape(B, T, C)
        k = jax.random.key(seed)
        ks = jax.random.split(k, 7)
        B, T, C = (8, 96, EMBED_DIM)
        w_scale = 1.0 / np.sqrt(C)
        return {'query': jax.random.normal(ks[0], (B, T, C), jnp.float32), 'key': jax.random.normal(ks[1], (B, T, C), jnp.float32), 'value': jax.random.normal(ks[2], (B, T, C), jnp.float32), 'Wq': jax.random.normal(ks[3], (C, C), jnp.float32) * w_scale, 'Wk': jax.random.normal(ks[4], (C, C), jnp.float32) * w_scale, 'Wv': jax.random.normal(ks[5], (C, C), jnp.float32) * w_scale, 'Wo': jax.random.normal(ks[6], (C, C), jnp.float32) * w_scale}
    _L0_xattn_all = _L0_xattn_setup()
    _L0_xattn_in = {k: v for k, v in _L0_xattn_all.items() if k in ('Wq', 'Wk', 'Wv', 'Wo')}
    del _L0_xattn_all

    def _L0_ffn_setup():
        import jax, jax.numpy as jnp
        import numpy as np
        D, H, O, E, TOPK = (128, 512, 128, 8, 2)
        B, S = (4, 128)
        key = jax.random.key(seed)
        ks = jax.random.split(key, 12)
        std = 0.02
        return {'hidden_states': jax.random.normal(ks[0], (B, S, D), dtype=jnp.float32), 'norm_weight': jnp.ones((D,), dtype=jnp.float32), 'router_w': jax.random.normal(ks[1], (E, D), dtype=jnp.float32) * std, 'sw1': jax.random.normal(ks[2], (D, H), dtype=jnp.float32) * (1.0 / np.sqrt(D)), 'sb1': jnp.zeros((H,), dtype=jnp.float32), 'sw2': jax.random.normal(ks[3], (H, O), dtype=jnp.float32) * (1.0 / np.sqrt(H)), 'sb2': jnp.zeros((O,), dtype=jnp.float32), 'ew1': jax.random.normal(ks[4], (E, D, H), dtype=jnp.float32) * (1.0 / np.sqrt(D)), 'eb1': jnp.zeros((E, H), dtype=jnp.float32), 'ew2': jax.random.normal(ks[5], (E, H, O), dtype=jnp.float32) * (1.0 / np.sqrt(H)), 'eb2': jnp.zeros((E, O), dtype=jnp.float32)}
    _L0_ffn_all = _L0_ffn_setup()
    _L0_ffn_in = {k: v for k, v in _L0_ffn_all.items() if k in ('norm_weight', 'router_w', 'sw1', 'sb1', 'sw2', 'sb2', 'ew1', 'eb1', 'ew2', 'eb2')}
    del _L0_ffn_all

    def _L1_xattn_setup():
        import jax, jax.numpy as jnp
        import numpy as np
        D_MODEL = 128
        N_HEADS = 16
        HEAD_DIM = D_MODEL // N_HEADS
        key = jax.random.key(seed)
        k1, k2, k3, k4, k5, k6 = jax.random.split(key, 6)
        B, T_q, T_kv = (4, 128, 512)
        s = 1.0 / np.sqrt(D_MODEL)
        return {'query': jax.random.normal(k1, (B, T_q, D_MODEL), dtype=jnp.float32), 'kv_source': jax.random.normal(k2, (B, T_kv, D_MODEL), dtype=jnp.float32), 'w_q': jax.random.normal(k3, (D_MODEL, D_MODEL), dtype=jnp.float32) * s, 'w_k': jax.random.normal(k4, (D_MODEL, D_MODEL), dtype=jnp.float32) * s, 'w_v': jax.random.normal(k5, (D_MODEL, D_MODEL), dtype=jnp.float32) * s, 'w_o': jax.random.normal(k6, (D_MODEL, D_MODEL), dtype=jnp.float32) * s}
    _L1_xattn_all = _L1_xattn_setup()
    _L1_xattn_in = {k: v for k, v in _L1_xattn_all.items() if k in ('w_q', 'w_k', 'w_v', 'w_o')}
    del _L1_xattn_all

    def _L1_ffn_setup():
        import jax, jax.numpy as jnp
        import numpy as np
        B, T, D, E, H = (8, 256, 128, 8, 32)
        LN_EPS = 1e-05
        key = jax.random.key(seed)
        ks = jax.random.split(key, 4)
        return {'x': jax.random.normal(ks[0], (B, T, D), dtype=jnp.float32), 'Wg': jax.random.normal(ks[1], (E, D), dtype=jnp.float32) * 0.02, 'ln_scale': jnp.ones((E, D), dtype=jnp.float32), 'ln_bias': jnp.zeros((E, D), dtype=jnp.float32), 'W1': jax.random.normal(ks[2], (E, D, H), dtype=jnp.float32) * 0.02, 'b1': jnp.zeros((E, H), dtype=jnp.float32), 'W2': jax.random.normal(ks[3], (E, H, D), dtype=jnp.float32) * 0.02, 'b2': jnp.zeros((E, D), dtype=jnp.float32)}
    _L1_ffn_all = _L1_ffn_setup()
    _L1_ffn_in = {k: v for k, v in _L1_ffn_all.items() if k in ('Wg', 'ln_scale', 'ln_bias', 'W1', 'b1', 'W2', 'b2')}
    del _L1_ffn_all
    return {'x': x, 'ctx_1024': ctx_1024, 'L0_xattn_Wq': _L0_xattn_in['Wq'], 'L0_xattn_Wk': _L0_xattn_in['Wk'], 'L0_xattn_Wv': _L0_xattn_in['Wv'], 'L0_xattn_Wo': _L0_xattn_in['Wo'], 'L0_ffn_norm_weight': _L0_ffn_in['norm_weight'], 'L0_ffn_router_w': _L0_ffn_in['router_w'], 'L0_ffn_sw1': _L0_ffn_in['sw1'], 'L0_ffn_sb1': _L0_ffn_in['sb1'], 'L0_ffn_sw2': _L0_ffn_in['sw2'], 'L0_ffn_sb2': _L0_ffn_in['sb2'], 'L0_ffn_ew1': _L0_ffn_in['ew1'], 'L0_ffn_eb1': _L0_ffn_in['eb1'], 'L0_ffn_ew2': _L0_ffn_in['ew2'], 'L0_ffn_eb2': _L0_ffn_in['eb2'], 'L1_xattn_w_q': _L1_xattn_in['w_q'], 'L1_xattn_w_k': _L1_xattn_in['w_k'], 'L1_xattn_w_v': _L1_xattn_in['w_v'], 'L1_xattn_w_o': _L1_xattn_in['w_o'], 'L1_ffn_Wg': _L1_ffn_in['Wg'], 'L1_ffn_ln_scale': _L1_ffn_in['ln_scale'], 'L1_ffn_ln_bias': _L1_ffn_in['ln_bias'], 'L1_ffn_W1': _L1_ffn_in['W1'], 'L1_ffn_b1': _L1_ffn_in['b1'], 'L1_ffn_W2': _L1_ffn_in['W2'], 'L1_ffn_b2': _L1_ffn_in['b2']}

def reference(x, ctx_1024, L0_xattn_Wq, L0_xattn_Wk, L0_xattn_Wv, L0_xattn_Wo, L0_ffn_norm_weight, L0_ffn_router_w, L0_ffn_sw1, L0_ffn_sb1, L0_ffn_sw2, L0_ffn_sb2, L0_ffn_ew1, L0_ffn_eb1, L0_ffn_ew2, L0_ffn_eb2, L1_xattn_w_q, L1_xattn_w_k, L1_xattn_w_v, L1_xattn_w_o, L1_ffn_Wg, L1_ffn_ln_scale, L1_ffn_ln_bias, L1_ffn_W1, L1_ffn_b1, L1_ffn_W2, L1_ffn_b2):
    import jax
    import jax.numpy as jnp

    def _L0_xattn_ref(query, key, value, Wq, Wk, Wv, Wo):
        import jax, jax.numpy as jnp
        import numpy as np
        EMBED_DIM = 128
        NUM_HEADS = 16
        THETA = 10000.0

        def apply_rope(x):
            B, T, C = x.shape
            freqs = 1.0 / THETA ** (jnp.arange(0, C, 2, dtype=jnp.float32) / C)
            t = jnp.arange(T, dtype=jnp.float32)
            ang = jnp.outer(t, freqs)
            cosv, sinv = (jnp.cos(ang), jnp.sin(ang))
            xr = x.reshape(B, T, C // 2, 2)
            real = xr[..., 0] * cosv - xr[..., 1] * sinv
            imag = xr[..., 0] * sinv + xr[..., 1] * cosv
            return jnp.stack([real, imag], axis=-1).reshape(B, T, C)
        B, T, C = query.shape
        H = NUM_HEADS
        D = C // H
        q = jnp.einsum('btc,oc->bto', query, Wq)
        k = jnp.einsum('btc,oc->bto', key, Wk)
        v = jnp.einsum('btc,oc->bto', value, Wv)
        q = apply_rope(q)
        k = apply_rope(k)
        q = q.reshape(B, T, H, D).transpose(0, 2, 1, 3)
        k = k.reshape(B, T, H, D).transpose(0, 2, 1, 3)
        v = v.reshape(B, T, H, D).transpose(0, 2, 1, 3)
        scale = 1.0 / jnp.sqrt(jnp.asarray(D, dtype=q.dtype))
        scores = jnp.einsum('bhqd,bhkd->bhqk', q, k) * scale
        attn = jax.nn.softmax(scores, axis=-1)
        y = jnp.einsum('bhqk,bhkd->bhqd', attn, v)
        y = y.transpose(0, 2, 1, 3).reshape(B, T, C)
        return jnp.einsum('btc,oc->bto', y, Wo)

    def _L0_ffn_ref(hidden_states, norm_weight, router_w, sw1, sb1, sw2, sb2, ew1, eb1, ew2, eb2):
        import jax, jax.numpy as jnp
        import numpy as np
        D, H, O, E, TOPK = (128, 512, 128, 8, 2)
        B, S = (4, 128)
        b, s, d = hidden_states.shape
        var = jnp.mean(jnp.square(hidden_states), axis=-1, keepdims=True)
        normed = hidden_states * jax.lax.rsqrt(var + 1e-08) * norm_weight
        shared = jnp.maximum(normed @ sw1 + sb1, 0.0) @ sw2 + sb2
        flat = normed.reshape(-1, d)
        T = flat.shape[0]
        probs = jax.nn.sigmoid(flat @ router_w.T)
        scores, idx = jax.lax.top_k(probs, TOPK)
        w = scores / (jnp.sum(scores, axis=-1, keepdims=True) + 1e-06)
        comb = jnp.zeros((T, E), dtype=flat.dtype)
        comb = comb.at[jnp.arange(T)[:, None], idx].add(w)
        h = jnp.maximum(jnp.einsum('td,edh->teh', flat, ew1) + eb1[None, :, :], 0.0)
        eo = jnp.einsum('teh,eho->teo', h, ew2) + eb2[None, :, :]
        routed = jnp.einsum('teo,te->to', eo, comb)
        return shared + routed.reshape(b, s, -1)

    def _L1_xattn_ref(query, kv_source, w_q, w_k, w_v, w_o):
        import jax, jax.numpy as jnp
        import numpy as np
        D_MODEL = 128
        N_HEADS = 16
        HEAD_DIM = D_MODEL // N_HEADS
        B, T_q, _ = query.shape
        T_kv = kv_source.shape[1]
        q = (query @ w_q.T).reshape(B, T_q, N_HEADS, HEAD_DIM)
        k = (kv_source @ w_k.T).reshape(B, T_kv, N_HEADS, HEAD_DIM)
        v = (kv_source @ w_v.T).reshape(B, T_kv, N_HEADS, HEAD_DIM)
        scale = HEAD_DIM ** (-0.5)
        attn = jax.nn.softmax(jnp.einsum('bqhd,bkhd->bhqk', q, k) * scale, axis=-1)
        out = jnp.einsum('bhqk,bkhd->bqhd', attn, v).reshape(B, T_q, D_MODEL)
        return out @ w_o.T

    def _L1_ffn_ref(x, Wg, ln_scale, ln_bias, W1, b1, W2, b2):
        import jax, jax.numpy as jnp
        import numpy as np
        B, T, D, E, H = (8, 256, 128, 8, 32)
        LN_EPS = 1e-05
        Bs, Ts, Ds = x.shape
        xt = x.reshape(Bs * Ts, Ds)
        logits = xt @ Wg.T
        top1 = jnp.argmax(logits, axis=-1)
        mu = jnp.mean(xt, axis=-1, keepdims=True)
        var = jnp.mean(jnp.square(xt - mu), axis=-1, keepdims=True)
        xhat = (xt - mu) * jax.lax.rsqrt(var + LN_EPS)
        n_experts = Wg.shape[0]

        def body(y, p):
            s_e, b_e, w1, bb1, w2, bb2, eid = p
            h = jax.nn.gelu((xhat * s_e + b_e) @ w1 + bb1, approximate=False)
            out = h @ w2 + bb2
            mask = (top1 == eid)[:, None].astype(out.dtype)
            return (y + mask * out, None)
        y0 = jnp.zeros_like(xt)
        y, _ = jax.lax.scan(body, y0, (ln_scale, ln_bias, W1, b1, W2, b2, jnp.arange(n_experts)))
        return y.reshape(Bs, Ts, Ds)
    x = x + _L0_xattn_ref(_layernorm(x, axis=-1), ctx_1024, ctx_1024, L0_xattn_Wq, L0_xattn_Wk, L0_xattn_Wv, L0_xattn_Wo)
    x = x + _L0_ffn_ref(_layernorm(x, axis=-1), L0_ffn_norm_weight, L0_ffn_router_w, L0_ffn_sw1, L0_ffn_sb1, L0_ffn_sw2, L0_ffn_sb2, L0_ffn_ew1, L0_ffn_eb1, L0_ffn_ew2, L0_ffn_eb2)
    x = x + _L1_xattn_ref(_layernorm(x, axis=-1), ctx_1024, L1_xattn_w_q, L1_xattn_w_k, L1_xattn_w_v, L1_xattn_w_o)
    x = x + _L1_ffn_ref(_layernorm(x, axis=-1), L1_ffn_Wg, L1_ffn_ln_scale, L1_ffn_ln_bias, L1_ffn_W1, L1_ffn_b1, L1_ffn_W2, L1_ffn_b2)
    return x

_drawn_inputs = setup_inputs


def setup_inputs(seed=0):
    import zlib

    import numpy as np

    out = dict(_drawn_inputs(seed))
    spreads = {'L0_ffn_norm_weight': (1.0, 0.2),
     'L0_ffn_sb1': (0.0, 0.1),
     'L0_ffn_sb2': (0.0, 0.1),
     'L0_ffn_eb1': (0.0, 0.1),
     'L0_ffn_eb2': (0.0, 0.1),
     'L1_ffn_ln_scale': (1.0, 0.6),
     'L1_ffn_ln_bias': (0.0, 0.8),
     'L1_ffn_b1': (0.0, 0.8),
     'L1_ffn_b2': (0.0, 0.1)}
    factors = {'L1_ffn_W1': 6.396, 'L1_ffn_W2': 5.876}
    for name, (base, spread) in spreads.items():
        noise = np.random.default_rng([zlib.crc32(name.encode()), seed]).standard_normal(out[name].shape)
        drawn = base * np.exp(spread * noise) if base else spread * noise
        out[name] = jnp.asarray(drawn.astype(out[name].dtype))
    for name, factor in factors.items():
        out[name] = (out[name] * factor).astype(out[name].dtype)
    return out
```

```python
from contextlib import ExitStack

import numpy as np

import concourse.bass as bass
from concourse import mybir

P = 128
B = 32
H, D = 16, 8
BLK = 8
GB = 4
G = B // GB
GT = GB * P
E0, HID = 8, 512
NE = E0 + 1
HB = HID // P
E1, H1 = 8, 32
SLOTS = 4
RING = 4
Q_TERMS = (0, 0, 0, 1, 1, 2)
K_TERMS = (0, 1, 2, 0, 1, 0)
TERM_ROWS = 8 * len(Q_TERMS)
SCORE_ROWS = TERM_ROWS + 3
CONSTS = 6
SCALE = float(1.0 / np.sqrt(np.float32(D)))
EPS_LN, EPS_RMS, EPS_TOP = 1e-5, 1e-8, 1e-6

ALU = mybir.AluOpType
ACT = mybir.ActivationFunctionType
F32 = mybir.dt.float32
BF16 = mybir.dt.bfloat16
U32 = mybir.dt.uint32
AX = mybir.AxisListType.X


def wait(eng, sem, value):
    if not (isinstance(value, int) and value <= 0):
        eng.wait_ge(sem, value)


def group_steps(eng, step):
    step(0, 0)
    step(0, 1)
    with eng.Fori(1, G // 2 - 1) as i:
        step(i, 0)
        step(i, 1)
    step(G // 2 - 1, 0)
    step(G // 2 - 1, 1)


def has_group(i, par, ahead):
    return not isinstance(i, int) or 2 * i + par + ahead < G


def batch_steps(eng, step):
    for k in range(RING):
        step(0, k)
    with eng.Fori(1, B // RING - 1) as i:
        for k in range(RING):
            step(i, k)
    for k in range(RING + 3):
        step(B // RING - 1 + k // RING, k % RING)


def has_batch(i, k, off):
    return not isinstance(i, int) or 0 <= RING * i + k + off < B


class Kernel:
    def __init__(self, nc, ins, out):
        self.nc, self.ins, self.out = nc, ins, out
        self.ctx = ExitStack()
        self.open_sems = []

    def sb(self, name, shape, dtype=F32):
        return self.ctx.enter_context(self.nc.sbuf_tensor(name, shape, dtype))

    def sem(self, name):
        self.open_sems.append(self.nc.alloc_semaphore(name=name))
        return self.open_sems[-1]

    def renew_semaphores(self):
        self.nc.clear_and_free_semaphores(self.open_sems)
        self.open_sems = []
        self.nc.all_engine_barrier()

    def wait_apart(self, eng, *counts):
        counts = [(sem, value if isinstance(value, int) else eng.to_reg(value)) for sem, value in counts]
        eng.wait_ge(self.const_done, CONSTS)
        for sem, value in counts:
            wait(eng, sem, value)

    def sems(self, prefix, names):
        return {n: self.sem(f"{prefix}_{n}") for n in names.split()}

    def build(self):
        nc = self.nc
        with self.ctx:
            self.x = self.sb("x", [P, B, P])
            self.v = self.sb("v", [P, B, P])
            self.parts = [self.sb(f"{n}_parts", [P, 3, B * P], BF16) for n in "qk"]
            self.big = self.sb("big", [P, 2 * SLOTS * BLK * GT // 2])
            big16 = self.big[:].bitcast(BF16).rearrange("p (w s n) -> p w s n", w=2, s=SLOTS)
            self.stack = [big16[:, w] for w in range(2)]
            self.scratch = self.sb("scratch", [P, RING * 2 * BLK * P // 2])
            sc = self.scratch[:]
            self.c_in = sc[:, 0:2 * GT].rearrange("p (r n) -> p r n", r=2)
            self.cT = sc[:, 2 * GT:4 * GT].rearrange("p (r n) -> p r n", r=2)
            self.xT = sc[:, 4 * GT:6 * GT].rearrange("p (r n) -> p r n", r=2)
            self.xn = sc[:, 6 * GT:7 * GT]
            self.hat = sc[:, 7 * GT:8 * GT]
            st = sc.bitcast(BF16).rearrange("p (r w b t) -> p r w b t", r=RING, w=2, b=BLK)
            self.q_st = [st[:, r, 0] for r in range(RING)]
            self.k_st = [st[:, r, 1] for r in range(RING)]
            self.temp = self.sb("temp", [P, 4, GT])
            self.attn_w = self.sb("attn_w", [P, 6, P])
            self.rope_t = self.sb("rope_t", [P, 2, P])
            self.ident = self.sb("ident", [P, P])
            self.ident16 = self.sb("ident16", [P, P], BF16)
            self.half = self.sb("half", [P, 8])
            self.iota8 = self.sb("iota8", [P, 8])
            self.psum = self.ctx.enter_context(nc.psum_tensor("psum", [P, 8, 512], F32))
            self.consts()
            self.attention(0)
            self.ffn0()
            self.renew_semaphores()
            self.attention(1)
            self.ffn1()

    def consts(self):
        nc = self.nc
        done = self.const_done = nc.alloc_semaphore(name="const_done")
        ii = self.sb("iota_int", [P, 8], mybir.dt.int32)
        with nc.Block() as block:
            @block.gpsimd
            def _(pool):
                nc.gpsimd.memset(self.ident[:], 0.0).then_inc(done, 1)
                pool.wait_ge(done, 1)
                nc.gpsimd.affine_select(out=self.ident[:], in_=self.ident[:], compare_op=ALU.not_equal, fill=1.0,
                                        base=0, pattern=[[-1, P]], channel_multiplier=1).then_inc(done, 1)
                nc.gpsimd.iota(ii[:], pattern=[[1, 8]], base=0, channel_multiplier=0).then_inc(done, 1)
                pool.wait_ge(done, 3)
                nc.gpsimd.tensor_copy(self.ident16[:], self.ident[:]).then_inc(done, 1)
                nc.gpsimd.tensor_copy(self.iota8[:], ii[:]).then_inc(done, 1)
                nc.gpsimd.memset(self.half[:], -0.5).then_inc(done, 1)

    def transpose_in(self, pe, bank, src, **kw):
        for j in range(GB):
            last = self.nc.tensor.transpose(self.psum[:, bank, j * P:(j + 1) * P], src[:, j * P:(j + 1) * P],
                                            self.ident[:])
        return last

    def attention(self, l):
        nc, ps = self.nc, self.psum
        rope = l == 0
        s = self.sems(f"a{l}", """w_in ones_set stats mv veps rstd xn xn_tr c_tr xT cT q_mm qs_mm k_mm ks_mm v_mm
            t1 t2 rot high rest mid low v_out stacked pv_zero p1 negmax split_a split_b split_c split nm_tr nm_out
            p2 exps v_st pv u_out u_tr den y y_tr yT o_mm x_add""")
        x_in = [self.sem(f"a{l}_x_in{r}") for r in range(2)]
        c_in = [self.sem(f"a{l}_c_in{r}") for r in range(2)]
        staged = [self.sem(f"a{l}_staged{r}") for r in range(RING)]
        nm_rows = [self.sem(f"a{l}_nm_rows{r}") for r in range(2)]

        with ExitStack() as local:
            def sb(name, shape, dtype=F32):
                return local.enter_context(nc.sbuf_tensor(f"a{l}_{name}", shape, dtype))

            bn = sb("bn", [P, GB, 6])
            mv = sb("mv", [P, GB, 2])
            veps = sb("veps", [P, GB])
            rstd = sb("rstd", [P, GB])
            negmax = sb("negmax", [P, 2, 2, BLK])
            nm_rest = sb("nm_rest", [P, 2, BLK])
            nm_parts = sb("nm_parts", [P, 2, 2, 3, BLK], BF16)
            nm_T = sb("nm_T", [TERM_ROWS, 2, P], BF16)
            v_st = sb("v_st", [P, 2, H, D + 1])
            u = sb("u", [P, 4, P])
            rden = sb("rden", [P, H])
            y = sb("y", [P, P])
            yT = sb("yT", [P, P])
            w_q, w_qs, w_k, w_ks, w_v, w_o = (self.attn_w[:, n] for n in range(6))
            t1, t2, rot, rest = (self.temp[:, n] for n in range(4))
            cos4 = self.rope_t[:, 0:1].to_broadcast([P, GB, P])
            sin4 = self.rope_t[:, 1:2].to_broadcast([P, GB, P])
            pt = self.temp[:].rearrange("p (r a) n -> p r (a n)", r=2).rearrange("p r (a b t) -> p r a b t", a=2, b=4)
            XN_BANK, C_BANK, Q_BANK, QS_BANK, K_BANK, KS_BANK, V_BANK = range(7)
            P1_BANK, P2_BANK, PV_BANK, TAIL_BANK = 0, 2, 6, 7
            tail16 = ps[:, TAIL_BANK].bitcast(BF16)

            def four(ap):
                return ap.rearrange("p (b t) -> p b t", b=GB)

            with nc.Block() as block:
                @block.sync
                def _(sp):
                    sp.dma_start(self.attn_w[:], self.ins[f"attn_w{l}"]).then_inc(s["w_in"], 16)
                    if rope:
                        sp.dma_start(self.rope_t[:], self.ins["rope"]).then_inc(s["w_in"], 16)

                    def stack(g, slot, first):
                        sp.wait_ge(s["high"], 2 * g + 2)
                        sp.wait_ge(s["mid"], 2 * g + 2)
                        sp.wait_ge(s["low"], 2 * g + 2)
                        if first:
                            sp.wait_ge(s["ones_set"], g + 1)
                        else:
                            self.wait_apart(sp, *((staged[r], 32 * (g - SLOTS + 1)) for r in range(RING)))
                        wait(sp, s["stacked"], 16 * 24 * g)
                        for w, terms in enumerate((Q_TERMS, K_TERMS)):
                            for par in range(2):
                                for t, part in enumerate(terms):
                                    r0 = 64 * par + 8 * t
                                    sp.dma_start(self.stack[w][r0:r0 + 8, slot],
                                                 self.parts[w][64 * par:64 * par + 64, part, bass.ts(g, GT)],
                                                 ).then_inc(s["stacked"], 16)

                    for g in range(SLOTS):
                        stack(g, g, True)
                    with sp.Fori(SLOTS, G) as g:
                        stack(g, g - SLOTS, False)

                @block.gpsimd
                def _(pool):
                    def ones(g):
                        for w in range(2):
                            last = nc.gpsimd.memset(self.stack[w][:, g].bitcast(F32),
                                                    float(np.array([0x3F803F80], np.uint32).view(np.float32)[0]))
                        last.then_inc(s["ones_set"], 1)

                    def inverse_std(g):
                        self.wait_apart(pool, (s["mv"], g + 1))
                        nc.gpsimd.tensor_scalar(veps[:], mv[:, :, 1], EPS_LN, None, ALU.add).then_inc(s["veps"], 1)
                        pool.wait_ge(s["veps"], g + 1)
                        nc.gpsimd.tensor_tensor(rstd[:], veps[:], self.half[:, 0:GB], ALU.pow).then_inc(s["rstd"], 1)

                    def low(n, w, g):
                        pool.wait_ge(s["mid"], n + 1)
                        nc.gpsimd.tensor_tensor(self.parts[w][:, 2, bass.ts(g, GT)], rest,
                                                self.parts[w][:, 1, bass.ts(g, GT)], ALU.subtract).then_inc(s["low"], 1)

                    ones(0)
                    inverse_std(0)

                    def project(i, par):
                        g = 2 * i + par
                        if has_group(i, par, 1):
                            inverse_std(g + 1)
                        low(2 * g, 0, g)
                        low(2 * g + 1, 1, g)

                    group_steps(pool, project)
                    for g in range(1, SLOTS):
                        ones(g)
                    for r in range(2):
                        last = nc.gpsimd.memset(v_st[:, r, :, D:D + 1], 1.0)
                    last.then_inc(s["v_st"], 1)
                    pool.wait_ge(s["v_out"], G)

                    def step(i, k):
                        b = 4 * i + k
                        p1, p2 = has_batch(i, k, 0), has_batch(i, k, -2)
                        if has_batch(i, k, -1):
                            r = (k - 1) % 2
                            self.wait_apart(pool, (s["nm_out"], b))
                            for par in range(2):
                                pool.dma_start(self.q_st[(k - 1) % RING][64 * par + TERM_ROWS:64 * par + SCORE_ROWS]
                                               .rearrange("p b t -> p (b t)"),
                                               nm_T[24 * par:24 * par + 24, r]).then_inc(nm_rows[r], 16)
                        if p2:
                            self.wait_apart(pool, (s["pv"], 2 * (b - 3)))
                            nc.gpsimd.tensor_copy(v_st[:, k % 2, :, 0:D],
                                                  self.v[:, b - 2].rearrange("p (h d) -> p h d", h=H),
                                                  ).then_inc(s["v_st"], 1)
                        if p1:
                            r = k % 2
                            self.wait_apart(pool, (s["negmax"], 2 * b + 2), (s["nm_tr"], b - 1))
                            nc.gpsimd.tensor_copy(nm_parts[:, r, :, 0], negmax[:, r]).then_inc(s["split_a"], 1)
                            pool.wait_ge(s["split_a"], b + 1)
                            nc.gpsimd.tensor_tensor(nm_rest[:], negmax[:, r], nm_parts[:, r, :, 0],
                                                    ALU.subtract).then_inc(s["split_b"], 1)
                            self.wait_apart(pool, (s["split_b"], b + 1))
                            nc.gpsimd.tensor_copy(nm_parts[:, r, :, 1], nm_rest[:]).then_inc(s["split_c"], 1)
                            pool.wait_ge(s["split_c"], b + 1)
                            nc.gpsimd.tensor_tensor(nm_parts[:, r, :, 2], nm_rest[:], nm_parts[:, r, :, 1],
                                                    ALU.subtract).then_inc(s["split"], 1)

                    batch_steps(pool, step)

                @block.scalar
                def _(act):
                    def load(g, par):
                        if l == 0:
                            act.dma_start(self.x[:, bass.ts(g, GB)], self.ins["x"][:, bass.ts(g, GB)],
                                          ).then_inc(x_in[par], 16)
                        act.dma_start(four(self.c_in[:, par]), self.ins["ctx"][:, bass.ts(g, GB)],
                                      ).then_inc(c_in[par], 16)

                    def inputs(g, par):
                        act.wait_ge(s["xn_tr"], g + 1)
                        wait(act, s["q_mm"], g - 1)
                        if rope:
                            wait(act, s["qs_mm"], g - 1)
                        nc.scalar.activation(self.xT[:, par], ps[:, XN_BANK], ACT.Copy).then_inc(s["xT"], 1)
                        act.wait_ge(s["c_tr"], g + 1)
                        wait(act, s["v_mm"], g - 1)
                        nc.scalar.activation(self.cT[:, par], ps[:, C_BANK], ACT.Copy).then_inc(s["cT"], 1)

                    def split(n, w, g):
                        src = rot if rope else ps[:, (Q_BANK, K_BANK)[w]]
                        act.wait_ge(s["rot"] if rope else s[("q_mm", "k_mm")[w]], n + 1 if rope else g + 1)
                        nc.scalar.activation(self.parts[w][:, 0, bass.ts(g, GT)], src, ACT.Copy).then_inc(s["high"], 1)
                        act.wait_ge(s["rest"], n + 1)
                        nc.scalar.activation(self.parts[w][:, 1, bass.ts(g, GT)], rest, ACT.Copy).then_inc(s["mid"], 1)

                    load(0, 0)
                    load(1, 1)
                    inputs(0, 0)

                    def project(i, par):
                        g = 2 * i + par
                        if has_group(i, par, 2):
                            act.wait_ge(s["c_tr"], g + 1)
                            load(g + 2, par)
                        if has_group(i, par, 1):
                            inputs(g + 1, 1 - par)
                        split(2 * g, 0, g)
                        split(2 * g + 1, 1, g)
                        act.wait_ge(s["v_mm"], g + 1)
                        nc.scalar.activation(self.v[:, bass.ts(g, GB)], four(ps[:, V_BANK]), ACT.Copy,
                                             ).then_inc(s["v_out"], 1)

                    group_steps(act, project)

                    def stage(i, k):
                        act.wait_ge(s["stacked"], 16 * 24 * (i + 1))
                        slot = i % SLOTS
                        for w, dst in enumerate((self.q_st, self.k_st)):
                            act.dma_start(dst[k], self.stack[w][:, slot].rearrange("p (b j t) -> p j b t", b=BLK,
                                          j=GB)[:, k]).then_inc(staged[k], 16)

                    act.wait_ge(s["v_mm"], G)
                    act.wait_ge(s["low"], 2 * G)
                    stage(0, 0)
                    stage(0, 1)

                    def step(i, k):
                        b = 4 * i + k
                        p1, p2 = has_batch(i, k, 0), has_batch(i, k, -2)
                        if has_batch(i, k, -1):
                            r = (k - 1) % 2
                            act.wait_ge(s["nm_tr"], b)
                            if has_batch(i, k, -3):
                                act.wait_ge(nm_rows[r], 32 * (2 * i + (k - 3) // 2 + 1))
                            nc.scalar.activation(nm_T[:, r], tail16[0:TERM_ROWS, 0:P], ACT.Copy).then_inc(s["nm_out"], 1)

                        def exp(unit):
                            n = 2 * (b - 2) + unit
                            act.wait_ge(s["p2"], n + 1)
                            wait(act, s["pv"], n - 1)
                            nc.scalar.activation(pt[:, unit].rearrange("p a b t -> p (a b t)"),
                                                 ps[:, P2_BANK + 2 * unit:P2_BANK + 2 * unit + 2]
                                                 .rearrange("p a n -> p (a n)"),
                                                 ACT.Exp, scale=SCALE).then_inc(s["exps"], 1)

                        if p2:
                            exp(0)
                        if has_batch(i, k, -3):
                            act.wait_ge(s["y_tr"], b - 2)
                            wait(act, s["o_mm"], b - 3)
                            nc.scalar.activation(yT[:], ps[:, TAIL_BANK, 0:P], ACT.Copy).then_inc(s["yT"], 1)
                        if p2:
                            exp(1)
                        if has_batch(i, k, 2):
                            stage(i + (k + 2) // 4, (k + 2) % 4)
                        if p2:
                            act.wait_ge(s["pv"], 2 * (b - 2) + 2)
                            wait(act, s["u_tr"], b - 2)
                            nc.scalar.activation(u[:], four(ps[:, PV_BANK]), ACT.Copy).then_inc(s["u_out"], 1)

                    batch_steps(act, step)

                @block.vector
                def _(dve):
                    def norm(g, par, loads):
                        if l == 0:
                            dve.wait_ge(x_in[par], 16 * loads)
                        for j in range(GB):
                            last = nc.vector.bn_stats(bn[:, j], self.x[:, 4 * g + j])
                        last.then_inc(s["stats"], 1)
                        self.wait_apart(dve, (s["stats"], g + 1), (s["rstd"], g))
                        for j in range(GB):
                            last = nc.vector.bn_aggr(mv[:, j], bn[:, j])
                        last.then_inc(s["mv"], 1)
                        dve.wait_ge(s["mv"], g + 1)
                        dve.wait_ge(s["rstd"], g + 1)
                        wait(dve, s["xn_tr"], g)
                        for j in range(GB):
                            last = nc.vector.tensor_scalar(self.xn[:, j * P:(j + 1) * P], self.x[:, 4 * g + j],
                                                           mv[:, j, 0:1], rstd[:, j:j + 1], ALU.subtract, ALU.mult)
                        last.then_inc(s["xn"], 1)

                    def remainder(n, w, g):
                        mm, mms = (("q_mm", "qs_mm"), ("k_mm", "ks_mm"))[w]
                        banks = ((Q_BANK, QS_BANK), (K_BANK, KS_BANK))[w]
                        if rope:
                            dve.wait_ge(s[mm], g + 1)
                            nc.vector.tensor_tensor(four(t1), four(ps[:, banks[0]]), cos4, ALU.mult).then_inc(s["t1"], 1)
                            dve.wait_ge(s[mms], g + 1)
                            nc.vector.tensor_tensor(four(t2), four(ps[:, banks[1]]), sin4, ALU.mult).then_inc(s["t2"], 1)
                            dve.wait_ge(s["t1"], n + 1)
                            dve.wait_ge(s["t2"], n + 1)
                            wait(dve, s["high"], n)
                            nc.vector.tensor_tensor(rot, t1, t2, ALU.add).then_inc(s["rot"], 1)
                            dve.wait_ge(s["rot"], n + 1)
                        src = rot if rope else ps[:, banks[0]]
                        dve.wait_ge(s["high"], n + 1)
                        wait(dve, s["low"], n)
                        nc.vector.tensor_tensor(rest, src, self.parts[w][:, 0, bass.ts(g, GT)],
                                                ALU.subtract).then_inc(s["rest"], 1)

                    dve.wait_ge(s["w_in"], 32 if rope else 16)
                    norm(0, 0, 1)

                    def project(i, par):
                        g = 2 * i + par
                        if has_group(i, par, 1):
                            norm(g + 1, 1 - par, i + (par + 1) // 2 + 1)
                        remainder(2 * g, 0, g)
                        remainder(2 * g + 1, 1, g)

                    group_steps(dve, project)
                    dve.wait_ge(s["v_out"], G)
                    nc.vector.memset(ps[:, PV_BANK], 0.0).then_inc(s["pv_zero"], 1)

                    def step(i, k):
                        b = 4 * i + k
                        r = k % 2

                        def maxima(unit):
                            dve.wait_ge(s["p1"], 2 * b + unit + 1)
                            if unit == 0:
                                wait(dve, s["split"], b - 1)
                            nc.vector.tensor_reduce(negmax[:, r, :, 4 * unit:4 * unit + 4],
                                                    ps[:, P1_BANK:P1_BANK + 2].rearrange("p a (b t) -> p a b t", b=4),
                                                    AX, ALU.max, negate=True).then_inc(s["negmax"], 1)

                        if has_batch(i, k, 0):
                            maxima(0)
                        if has_batch(i, k, -3):
                            dve.wait_ge(s["u_tr"], b - 2)
                            sums = ps[:, TAIL_BANK].rearrange("p (h n) -> p h n", h=H)
                            nc.vector.reciprocal(rden[:], sums[:, :, D]).then_inc(s["den"], 1)
                            dve.wait_ge(s["den"], b - 2)
                            wait(dve, s["y_tr"], b - 3)
                            nc.vector.tensor_tensor(y[:].rearrange("p (h d) -> p h d", h=H), sums[:, :, 0:D],
                                                    rden[:].unsqueeze(2).to_broadcast([P, H, D]),
                                                    ALU.mult).then_inc(s["y"], 1)
                        if has_batch(i, k, 0):
                            maxima(1)
                        if has_batch(i, k, -3):
                            dve.wait_ge(s["o_mm"], b - 2)
                            nc.vector.tensor_tensor(self.x[:, b - 3], ps[:, TAIL_BANK, P:2 * P], self.x[:, b - 3],
                                                    ALU.add).then_inc(s["x_add"], 1)

                    batch_steps(dve, step)

                @block.tensor
                def _(pe):
                    def transposes(g, par, loads):
                        pe.wait_ge(s["xn"], g + 1)
                        wait(pe, s["xT"], g)
                        self.transpose_in(pe, XN_BANK, self.xn).then_inc(s["xn_tr"], 1)
                        pe.wait_ge(c_in[par], 16 * loads)
                        wait(pe, s["cT"], g)
                        self.transpose_in(pe, C_BANK, self.c_in[:, par]).then_inc(s["c_tr"], 1)

                    def project_one(bank, weight, rhs, done):
                        nc.tensor.matmul(ps[:, bank], weight, rhs, start=True, stop=True).then_inc(s[done], 1)

                    pe.wait_ge(s["w_in"], 32 if rope else 16)
                    transposes(0, 0, 1)

                    def project(i, par):
                        g = 2 * i + par
                        pe.wait_ge(s["xT"], g + 1)
                        wait(pe, s["rest"], 2 * g)
                        project_one(Q_BANK, w_q, self.xT[:, par], "q_mm")
                        if rope:
                            project_one(QS_BANK, w_qs, self.xT[:, par], "qs_mm")
                        if has_group(i, par, 1):
                            transposes(g + 1, 1 - par, i + (par + 1) // 2 + 1)
                        pe.wait_ge(s["cT"], g + 1)
                        project_one(K_BANK, w_k, self.cT[:, par], "k_mm")
                        if rope:
                            project_one(KS_BANK, w_ks, self.cT[:, par], "ks_mm")
                        wait(pe, s["v_out"], g)
                        for j in range(GB):
                            last = nc.tensor.matmul(ps[:, V_BANK, j * P:(j + 1) * P], self.cT[:, par, j * P:(j + 1) * P],
                                                    w_v, start=True, stop=True)
                        last.then_inc(s["v_mm"], 1)

                    group_steps(pe, project)
                    pe.wait_ge(s["rest"], 2 * G)
                    pe.wait_ge(s["pv_zero"], 1)

                    def step(i, k):
                        b = 4 * i + k
                        r2 = (k - 2) % RING

                        def scores(bank, unit, stat, mov, rows):
                            for j in range(4):
                                for par in range(2):
                                    r0, blk = 64 * par, 4 * unit + j
                                    last = nc.tensor.matmul(ps[:, bank + par, j * P:(j + 1) * P],
                                                            stat[r0:r0 + rows, blk], mov[r0:r0 + rows, blk],
                                                            start=True, stop=True)
                            return last

                        def p1(unit):
                            if unit == 0:
                                pe.wait_ge(staged[k], 32 * (i + 1))
                            wait(pe, s["negmax"], 2 * b + unit)
                            scores(P1_BANK, unit, self.q_st[k], self.k_st[k], TERM_ROWS).then_inc(s["p1"], 1)

                        def p2(unit):
                            if unit == 0:
                                pe.wait_ge(nm_rows[k % 2], 32 * (2 * i + (k - 2) // 2 + 1))
                            wait(pe, s["exps"], 2 * (b - 3) + unit + 1)
                            scores(P2_BANK + 2 * unit, unit, self.k_st[r2], self.q_st[r2], SCORE_ROWS
                                   ).then_inc(s["p2"], 1)

                        def pv(unit):
                            n = 2 * (b - 2) + unit
                            if unit == 0:
                                pe.wait_ge(s["v_st"], b)
                                wait(pe, s["u_out"], b - 2)
                            pe.wait_ge(s["exps"], n + 1)
                            for par in range(2):
                                for j in range(4):
                                    last = nc.tensor.matmul(ps[32 * j:32 * j + D + 1, PV_BANK,
                                                               (2 * par + unit) * P:(2 * par + unit + 1) * P],
                                                            v_st[:, k % 2, 8 * par + 4 * unit + j],
                                                            pt[:, unit, par, j], start=True, stop=True,
                                                            tile_position=(0, 32 * j))
                            last.then_inc(s["pv"], 1)

                        if has_batch(i, k, 0):
                            p1(0)
                        if has_batch(i, k, -1):
                            self.wait_apart(pe, (s["split"], b), (s["x_add"], b - 3))
                            nc.tensor.transpose(tail16[0:TERM_ROWS, 0:P],
                                                nm_parts[:, (k - 1) % 2].rearrange("p a n b -> p (a n b)"),
                                                self.ident16[:]).then_inc(s["nm_tr"], 1)
                        if has_batch(i, k, -2):
                            p2(0)
                        if has_batch(i, k, -3):
                            pe.wait_ge(s["u_out"], b - 2)
                            if has_batch(i, k, -1):
                                pe.wait_ge(s["nm_out"], b)
                            wait(pe, s["x_add"], b - 3)
                            for n in range(4):
                                last = nc.tensor.transpose(ps[:, TAIL_BANK, n * P:(n + 1) * P], u[:, n], self.ident[:])
                            last.then_inc(s["u_tr"], 1)
                        if has_batch(i, k, 0):
                            p1(1)
                        if has_batch(i, k, -2):
                            pv(0)
                        if has_batch(i, k, -3):
                            pe.wait_ge(s["y"], b - 2)
                            nc.tensor.transpose(ps[:, TAIL_BANK, 0:P], y[:], self.ident[:]).then_inc(s["y_tr"], 1)
                        if has_batch(i, k, -2):
                            p2(1)
                        if has_batch(i, k, -3):
                            pe.wait_ge(s["yT"], b - 2)
                            nc.tensor.matmul(ps[:, TAIL_BANK, P:2 * P], yT[:], w_o, start=True, stop=True
                                             ).then_inc(s["o_mm"], 1)
                        if has_batch(i, k, -2):
                            pv(1)

                    batch_steps(pe, step)

    def ffn0(self):
        nc, ps = self.nc, self.psum
        s = self.sems("f0", """w1_in w2_in small_in stats mv veps rstd hat sq sveps srstd xn xn_tr xT logit_mm prob
            top8 idx idxf m0 m1 mask picked total rtot comb comb_tr combT up relu down acc""")
        UP_BANK, DOWN_BANK, T_BANK, MISC_BANK = 0, 4, 6, 7
        w1 = self.big[:, 0:NE * HID].rearrange("p (e n) -> p e n", e=NE)
        w2 = self.big[:, NE * HID:2 * NE * HID].rearrange("p (e b n) -> p e b n", e=NE, b=HB)
        hid = self.big[:, 2 * NE * HID:2 * NE * HID + 2 * HB * GT].rearrange("p (r b n) -> p r b n", r=2, b=HB)

        with ExitStack() as local:
            def sb(name, shape, dtype=F32):
                return local.enter_context(nc.sbuf_tensor(f"f0_{name}", shape, dtype))

            b1 = sb("b1", [P, NE * HB])
            b2 = sb("b2", [NE, P])
            rw = sb("rw", [P, E0])
            nw = sb("nw", [P, 1])
            bn = sb("bn", [P, GB, 6])
            mv = sb("mv", [P, GB, 2])
            veps = sb("veps", [P, GB])
            rstd = sb("rstd", [P, GB])
            sq = sb("sq", [P, GB])
            sveps = sb("sveps", [P, GB])
            srstd = sb("srstd", [P, GB])
            prob = sb("prob", [P, GB, E0])
            top8 = sb("top8", [P, GB, E0])
            idx = sb("idx", [P, GB, E0], U32)
            idxf = sb("idxf", [P, GB, 2])
            m0 = sb("m0", [P, GB, E0])
            m1 = sb("m1", [P, GB, E0])
            mask = sb("mask", [P, GB, E0])
            picked = sb("picked", [P, GB, E0])
            total = sb("total", [P, GB])
            rtot = sb("rtot", [P, GB])
            comb = sb("comb", [P, 2, GB, NE])
            combT = sb("combT", [NE, 2, GT])
            hat, xn, xT = self.hat, self.xn, self.xT

            def cols(ap, j):
                return ap[:, j * P:(j + 1) * P]

            def eight(ap):
                return ap.to_broadcast([P, GB, E0])

            with nc.Block() as block:
                @block.sync
                def _(sp):
                    for dst, name in ((b1, "f0_b1"), (b2, "f0_b2"), (rw, "f0_rw"), (nw, "f0_nw")):
                        sp.dma_start(dst[:], self.ins[name]).then_inc(s["small_in"], 16)
                    sp.dma_start(w1, self.ins["f0_w1"]).then_inc(s["w1_in"], 16)
                    sp.dma_start(w2, self.ins["f0_w2"]).then_inc(s["w2_in"], 16)

                @block.gpsimd
                def _(pool):
                    def roots(g):
                        self.wait_apart(pool, (s["mv"], g + 1))
                        nc.gpsimd.tensor_scalar(veps[:], mv[:, :, 1], EPS_LN, None, ALU.add).then_inc(s["veps"], 1)
                        pool.wait_ge(s["veps"], g + 1)
                        nc.gpsimd.tensor_tensor(rstd[:], veps[:], self.half[:, 0:GB], ALU.pow).then_inc(s["rstd"], 1)
                        self.wait_apart(pool, (s["sq"], g + 1))
                        nc.gpsimd.tensor_scalar(sveps[:], sq[:], 1.0 / P, EPS_RMS, ALU.mult, ALU.add,
                                                ).then_inc(s["sveps"], 1)
                        pool.wait_ge(s["sveps"], g + 1)
                        nc.gpsimd.tensor_tensor(srstd[:], sveps[:], self.half[:, 0:GB], ALU.pow,
                                                ).then_inc(s["srstd"], 1)

                    with pool.Fori(0, G) as g:
                        roots(g)

                @block.scalar
                def _(act):
                    def squares(g):
                        act.wait_ge(s["hat"], g + 1)
                        wait(act, s["srstd"], g)
                        for j in range(GB):
                            last = nc.scalar.activation(cols(xn, j), cols(hat, j), ACT.Square,
                                                        accum_out=sq[:, j:j + 1])
                        last.then_inc(s["sq"], 1)

                    def copy_xT(g, par):
                        act.wait_ge(s["xn_tr"], g + 1)
                        wait(act, s["up"], NE * HB * (g - 1))
                        nc.scalar.activation(xT[:, par], ps[:, T_BANK], ACT.Copy, scale=nw[:, 0:1]
                                             ).then_inc(s["xT"], 1)

                    def probs(g):
                        act.wait_ge(s["logit_mm"], g + 1)
                        wait(act, s["comb"], g)
                        nc.scalar.activation(prob[:], ps[:, MISC_BANK, 0:GB * E0].rearrange("p (j e) -> p j e", j=GB),
                                             ACT.Sigmoid).then_inc(s["prob"], 1)

                    def copy_combT(g, par):
                        act.wait_ge(s["comb_tr"], g + 1)
                        wait(act, s["down"], NE * (g - 1))
                        nc.scalar.activation(combT[:, par], ps[0:NE, MISC_BANK], ACT.Copy).then_inc(s["combT"], 1)

                    act.wait_ge(s["small_in"], 64)
                    squares(0)
                    copy_xT(0, 0)
                    probs(0)
                    copy_combT(0, 0)

                    def step(i, par):
                        g = 2 * i + par
                        for e in range(NE):
                            n = NE * g + e
                            for hb in range(HB):
                                act.wait_ge(s["up"], HB * n + hb + 1)
                                if hb == 0:
                                    wait(act, s["down"], n - 1)
                                nc.scalar.activation(hid[:, (par + e) % 2, hb], ps[:, UP_BANK + hb], ACT.Relu,
                                                     bias=b1[:, HB * e + hb:HB * e + hb + 1]).then_inc(s["relu"], 1)
                            if has_group(i, par, 1):
                                if e == 1:
                                    squares(g + 1)
                                if e == 4:
                                    copy_xT(g + 1, 1 - par)
                                if e == 6:
                                    probs(g + 1)
                                if e == 8:
                                    copy_combT(g + 1, 1 - par)

                    group_steps(act, step)

                @block.vector
                def _(dve):
                    def norm1(g):
                        for j in range(GB):
                            last = nc.vector.bn_stats(bn[:, j], self.x[:, 4 * g + j])
                        last.then_inc(s["stats"], 1)
                        self.wait_apart(dve, (s["stats"], g + 1), (s["rstd"], g))
                        for j in range(GB):
                            last = nc.vector.bn_aggr(mv[:, j], bn[:, j])
                        last.then_inc(s["mv"], 1)
                        dve.wait_ge(s["mv"], g + 1)
                        dve.wait_ge(s["rstd"], g + 1)
                        wait(dve, s["sq"], g)
                        for j in range(GB):
                            last = nc.vector.tensor_scalar(cols(hat, j), self.x[:, 4 * g + j], mv[:, j, 0:1],
                                                           rstd[:, j:j + 1], ALU.subtract, ALU.mult)
                        last.then_inc(s["hat"], 1)

                    def norm2(g):
                        dve.wait_ge(s["hat"], g + 1)
                        dve.wait_ge(s["sq"], g + 1)
                        dve.wait_ge(s["srstd"], g + 1)
                        wait(dve, s["xn_tr"], g)
                        for j in range(GB):
                            last = nc.vector.tensor_scalar(cols(xn, j), cols(hat, j), srstd[:, j:j + 1], None,
                                                           ALU.mult)
                        last.then_inc(s["xn"], 1)

                    def route(g, par):
                        self.wait_apart(dve, (s["prob"], g + 1))
                        for j in range(GB):
                            last = nc.vector.max(top8[:, j], prob[:, j])
                        last.then_inc(s["top8"], 1)
                        self.wait_apart(dve, (s["top8"], g + 1))
                        for j in range(GB):
                            last = nc.vector.max_index(idx[:, j], top8[:, j], prob[:, j])
                        last.then_inc(s["idx"], 1)
                        dve.wait_ge(s["idx"], g + 1)
                        nc.vector.tensor_copy(idxf[:], idx[:, :, 0:2]).then_inc(s["idxf"], 1)
                        dve.wait_ge(s["idxf"], g + 1)
                        iota = self.iota8[:].unsqueeze(1).to_broadcast([P, GB, E0])
                        nc.vector.tensor_tensor(m0[:], iota, eight(idxf[:, :, 0:1]), ALU.is_equal).then_inc(s["m0"], 1)
                        nc.vector.tensor_tensor(m1[:], iota, eight(idxf[:, :, 1:2]), ALU.is_equal).then_inc(s["m1"], 1)
                        dve.wait_ge(s["m0"], g + 1)
                        dve.wait_ge(s["m1"], g + 1)
                        nc.vector.tensor_tensor(mask[:], m0[:], m1[:], ALU.add).then_inc(s["mask"], 1)
                        dve.wait_ge(s["mask"], g + 1)
                        nc.vector.tensor_tensor(picked[:], mask[:], prob[:], ALU.mult).then_inc(s["picked"], 1)
                        nc.vector.scalar_tensor_tensor(total[:], top8[:, :, 0], EPS_TOP, top8[:, :, 1], ALU.add,
                                                       ALU.add).then_inc(s["total"], 1)
                        dve.wait_ge(s["total"], g + 1)
                        nc.vector.reciprocal(rtot[:], total[:]).then_inc(s["rtot"], 1)
                        dve.wait_ge(s["rtot"], g + 1)
                        dve.wait_ge(s["picked"], g + 1)
                        wait(dve, s["comb_tr"], g - 1)
                        nc.vector.tensor_tensor(comb[:, par, :, 0:E0], picked[:], eight(rtot[:].unsqueeze(2)),
                                                ALU.mult).then_inc(s["comb"], 1)

                    def accumulate(n, g, par, e):
                        dve.wait_ge(s["down"], n + 1)
                        bank = DOWN_BANK + (par + e) % 2
                        for j in range(GB):
                            if e < E0:
                                last = nc.vector.scalar_tensor_tensor(
                                    self.x[:, 4 * g + j], ps[:, bank, j * P:(j + 1) * P], comb[:, par, j, e:e + 1],
                                    self.x[:, 4 * g + j], ALU.mult, ALU.add)
                            else:
                                last = nc.vector.tensor_tensor(self.x[:, 4 * g + j], ps[:, bank, j * P:(j + 1) * P],
                                                               self.x[:, 4 * g + j], ALU.add)
                        last.then_inc(s["acc"], 1)

                    for r in range(2):
                        last = nc.vector.memset(comb[:, r, :, E0:NE], 1.0)
                    last.then_inc(s["comb"], 1)
                    dve.wait_ge(s["small_in"], 64)
                    norm1(0)
                    norm2(0)
                    route(0, 0)

                    def step(i, par):
                        g = 2 * i + par
                        for e in range(NE):
                            if has_group(i, par, 1):
                                if e == 0:
                                    norm1(g + 1)
                                if e == 2:
                                    norm2(g + 1)
                                if e == 7:
                                    route(g + 1, 1 - par)
                            wait(dve, s["acc"], NE * g + e)
                            accumulate(NE * g + e, g, par, e)

                    group_steps(dve, step)

                @block.tensor
                def _(pe):
                    def transposes(g):
                        pe.wait_ge(s["xn"], g + 1)
                        wait(pe, s["xT"], g)
                        self.transpose_in(pe, T_BANK, xn).then_inc(s["xn_tr"], 1)

                    def logits(g, par):
                        pe.wait_ge(s["xT"], g + 1)
                        wait(pe, s["combT"], g)
                        for j in range(GB):
                            last = nc.tensor.matmul(ps[:, MISC_BANK, j * E0:(j + 1) * E0], cols(xT[:, par], j), rw[:],
                                                    start=True, stop=True)
                        last.then_inc(s["logit_mm"], 1)

                    def comb_transpose(g, par):
                        pe.wait_ge(s["comb"], g + 2)
                        pe.wait_ge(s["prob"], g + 1)
                        for j in range(GB):
                            last = nc.tensor.transpose(ps[0:NE, MISC_BANK, j * P:(j + 1) * P], comb[:, par, j],
                                                       self.ident[:])
                        last.then_inc(s["comb_tr"], 1)

                    def up(n, par, e):
                        for hb in range(HB):
                            wait(pe, s["relu"], HB * (n - 1) + hb + 1)
                            nc.tensor.matmul(ps[:, UP_BANK + hb], w1[:, e, hb * P:(hb + 1) * P], xT[:, par],
                                             start=True, stop=True).then_inc(s["up"], 1)

                    def down(n, par, e, combT_ready=None):
                        wait(pe, s["acc"], n - 1)
                        if e == E0:
                            pe.wait_ge(s["combT"], combT_ready)
                        for j in range(GB):
                            out = ps[:, DOWN_BANK + (par + e) % 2, j * P:(j + 1) * P]
                            if e == E0:
                                nc.tensor.matmul(out, combT[:, par, j * P:(j + 1) * P], b2[:], start=True, stop=False)
                            for hb in range(HB):
                                if j == 0:
                                    pe.wait_ge(s["relu"], HB * n + hb + 1)
                                last = nc.tensor.matmul(out, hid[:, (par + e) % 2, hb, j * P:(j + 1) * P],
                                                        w2[:, e, hb], start=(e < E0 and hb == 0), stop=(hb == HB - 1))
                        last.then_inc(s["down"], 1)

                    pe.wait_ge(s["small_in"], 64)
                    transposes(0)
                    logits(0, 0)
                    comb_transpose(0, 0)
                    pe.wait_ge(s["w1_in"], 16)
                    pe.wait_ge(s["w2_in"], 16)

                    def step(i, par):
                        g = 2 * i + par
                        for e in range(NE):
                            n = NE * g + e
                            up(n, par, e)
                            if has_group(i, par, 1):
                                if e == 4:
                                    transposes(g + 1)
                                if e == 6:
                                    logits(g + 1, 1 - par)
                                if e == 8:
                                    comb_transpose(g + 1, 1 - par)
                            if e > 0:
                                down(n - 1, par, e - 1)
                        down(NE * g + NE - 1, par, E0, g + 1)

                    group_steps(pe, step)

    def ffn1(self):
        nc, ps = self.nc, self.psum
        s = self.sems("f1", """w_in w_folded fold_mm bias expand stats mv veps rstd xt xstats xmv xveps xrstd xh
            xt_tr xh_tr xtT xhT logit_mm logit top8 idx idxf mask mask_tr maskT mask16 up gelu spread hm down out
            out_dma""")
        XT_BANK, XH_BANK, UP_BANK, SPREAD_BANK, DOWN_BANK, MISC_BANK = 0, 1, 2, 4, 6, 7
        NB1 = E1 * H1 // P
        xt, xh = self.xn, self.hat
        xtT, xhT = self.xT, self.cT

        with ExitStack() as local:
            def sb(name, shape, dtype=F32):
                return local.enter_context(nc.sbuf_tensor(f"f1_{name}", shape, dtype))

            w1 = sb("w1", [P, E1, H1])
            w1s = sb("w1s", [P, E1, H1])
            lns = sb("lns", [P, E1])
            lnb = sb("lnb", [P, E1])
            b1 = sb("b1", [P, NB1])
            b1e = sb("b1e", [P, NB1])
            w2 = sb("w2", [P, NB1, P])
            b2 = sb("b2", [E1, P])
            wg = sb("wg", [P, E1])
            expand = sb("expand", [E1, NB1 * P])
            expand16 = sb("expand16", [E1, NB1 * P], BF16)
            bn = sb("bn", [P, 2, GB, 6])
            mv = sb("mv", [P, 2, GB, 2])
            veps = sb("veps", [P, 2, GB])
            rstd = sb("rstd", [P, 2, GB])
            logit = sb("logit", [P, GB, E1])
            top8 = sb("top8", [P, GB, E1])
            idx = sb("idx", [P, GB, E1], U32)
            idxf = sb("idxf", [P, GB, 1])
            mask = sb("mask", [P, GB, E1])
            maskT = sb("maskT", [E1, GT])
            mask16 = sb("mask16", [E1, GT], BF16)
            hg = sb("hg", [P, 2, NB1, GT])
            hm = sb("hm", [P, NB1, GT])

            def cols(ap, j):
                return ap[:, j * P:(j + 1) * P]

            with nc.Block() as block:
                @block.sync
                def _(sp):
                    pairs = ((w1, "f1_w1"), (lns, "f1_lns"), (lnb, "f1_lnb"), (b1, "f1_b1"), (w2, "f1_w2"),
                             (b2, "f1_b2"), (wg, "f1_wg"), (expand, "f1_expand"))
                    for dst, name in pairs:
                        sp.dma_start(dst[:], self.ins[name]).then_inc(s["w_in"], 16)
                    with sp.Fori(0, G) as g:
                        sp.wait_ge(s["out"], g + 1)
                        sp.dma_start(self.out[:, bass.ts(g, GB)], self.x[:, bass.ts(g, GB)]).then_inc(s["out_dma"], 16)
                    sp.wait_ge(s["out_dma"], 16 * G)

                @block.gpsimd
                def _(pool):
                    def inverse_std(g, which, ready, add, done):
                        self.wait_apart(pool, (s[ready], g + 1))
                        nc.gpsimd.tensor_scalar(veps[:, which], mv[:, which, :, 1], EPS_LN, None, ALU.add,
                                                ).then_inc(s[add], 1)
                        pool.wait_ge(s[add], g + 1)
                        nc.gpsimd.tensor_tensor(rstd[:, which], veps[:, which], self.half[:, 0:GB], ALU.pow,
                                                ).then_inc(s[done], 1)

                    with pool.Fori(0, G) as g:
                        inverse_std(g, 0, "mv", "veps", "rstd")
                        inverse_std(g, 1, "xmv", "xveps", "xrstd")

                @block.scalar
                def _(act):
                    def inputs(g):
                        act.wait_ge(s["xt_tr"], g + 1)
                        wait(act, s["logit_mm"], g)
                        nc.scalar.activation(xtT[:, 0], ps[:, XT_BANK], ACT.Copy).then_inc(s["xtT"], 1)
                        act.wait_ge(s["xh_tr"], g + 1)
                        wait(act, s["up"], 2 * g)
                        nc.scalar.activation(xhT[:, 0], ps[:, XH_BANK], ACT.Copy).then_inc(s["xhT"], 1)

                    def gelu(g, par):
                        wait(act, s["hm"], 2 * (g - 1))
                        for blk in range(NB1):
                            act.wait_ge(s["up"], 2 * g + blk + 1)
                            nc.scalar.activation(hg[:, par, blk], ps[:, UP_BANK + blk], ACT.Gelu,
                                                 bias=b1e[:, blk:blk + 1]).then_inc(s["gelu"], 1)

                    def masks(g):
                        act.wait_ge(s["mask_tr"], g + 1)
                        wait(act, s["down"], g)
                        nc.scalar.activation(maskT[:], ps[0:E1, MISC_BANK], ACT.Copy).then_inc(s["maskT"], 1)
                        wait(act, s["spread"], g)
                        nc.scalar.activation(mask16[:], ps[0:E1, MISC_BANK], ACT.Copy).then_inc(s["mask16"], 1)

                    act.wait_ge(s["w_in"], 16 * 8)
                    nc.scalar.activation(expand16[:], expand[:], ACT.Copy).then_inc(s["expand"], 1)
                    inputs(0)
                    act.wait_ge(s["bias"], 1)
                    gelu(0, 0)

                    def step(i, par):
                        g = 2 * i + par
                        if has_group(i, par, 1):
                            inputs(g + 1)
                        masks(g)
                        if has_group(i, par, 1):
                            gelu(g + 1, 1 - par)

                    group_steps(act, step)

                @block.vector
                def _(dve):
                    def norm(g, which, src, dst, stats, mvs, ready, read, done):
                        for j in range(GB):
                            last = nc.vector.bn_stats(bn[:, which, j], src[j])
                        last.then_inc(s[stats], 1)
                        self.wait_apart(dve, (s[stats], g + 1), (s[ready], g))
                        for j in range(GB):
                            last = nc.vector.bn_aggr(mv[:, which, j], bn[:, which, j])
                        last.then_inc(s[mvs], 1)
                        dve.wait_ge(s[mvs], g + 1)
                        dve.wait_ge(s[ready], g + 1)
                        wait(dve, s[read], g)
                        for j in range(GB):
                            last = nc.vector.tensor_scalar(cols(dst, j), src[j], mv[:, which, j, 0:1],
                                                           rstd[:, which, j:j + 1], ALU.subtract, ALU.mult)
                        last.then_inc(s[done], 1)

                    def norms(g):
                        norm(g, 0, [self.x[:, 4 * g + j] for j in range(GB)], xt, "stats", "mv", "rstd", "xt_tr", "xt")
                        dve.wait_ge(s["xt"], g + 1)
                        norm(g, 1, [cols(xt, j) for j in range(GB)], xh, "xstats", "xmv", "xrstd", "xh_tr", "xh")

                    def route(g):
                        dve.wait_ge(s["logit_mm"], g + 1)
                        nc.vector.tensor_copy(logit[:], ps[:, MISC_BANK, 0:GB * E1].rearrange("p (j e) -> p j e", j=GB),
                                              ).then_inc(s["logit"], 1)
                        self.wait_apart(dve, (s["logit"], g + 1))
                        for j in range(GB):
                            last = nc.vector.max(top8[:, j], logit[:, j])
                        last.then_inc(s["top8"], 1)
                        self.wait_apart(dve, (s["top8"], g + 1))
                        for j in range(GB):
                            last = nc.vector.max_index(idx[:, j], top8[:, j], logit[:, j])
                        last.then_inc(s["idx"], 1)
                        dve.wait_ge(s["idx"], g + 1)
                        nc.vector.tensor_copy(idxf[:], idx[:, :, 0:1]).then_inc(s["idxf"], 1)
                        dve.wait_ge(s["idxf"], g + 1)
                        wait(dve, s["mask_tr"], g)
                        nc.vector.tensor_tensor(mask[:], self.iota8[:].unsqueeze(1).to_broadcast([P, GB, E1]),
                                                idxf[:].to_broadcast([P, GB, E1]), ALU.is_equal).then_inc(s["mask"], 1)

                    dve.wait_ge(s["w_in"], 16 * 8)
                    for e in range(E1):
                        last = nc.vector.tensor_scalar(w1s[:, e], w1[:, e], lns[:, e:e + 1], None, ALU.mult)
                    last.then_inc(s["w_folded"], 1)
                    norms(0)
                    dve.wait_ge(s["fold_mm"], 1)
                    nc.vector.tensor_tensor(b1e[:], ps[:, DOWN_BANK, 0:NB1], b1[:], ALU.add).then_inc(s["bias"], 1)
                    route(0)
                    norms(1)

                    def step(i, par):
                        g = 2 * i + par
                        dve.wait_ge(s["spread"], g + 1)
                        wait(dve, s["down"], g)
                        for blk in range(NB1):
                            dve.wait_ge(s["gelu"], 2 * g + blk + 1)
                            nc.vector.tensor_tensor(hm[:, blk], hg[:, par, blk], ps[:, SPREAD_BANK + blk],
                                                    ALU.mult).then_inc(s["hm"], 1)
                        if has_group(i, par, 1):
                            route(g + 1)
                        dve.wait_ge(s["down"], g + 1)
                        nc.vector.tensor_tensor(self.x[:, bass.ts(g, GB)],
                                                ps[:, DOWN_BANK].rearrange("p (j n) -> p j n", j=GB),
                                                self.x[:, bass.ts(g, GB)], ALU.add).then_inc(s["out"], 1)
                        if has_group(i, par, 2):
                            norms(g + 2)

                    group_steps(dve, step)

                @block.tensor
                def _(pe):
                    def transposes(g):
                        pe.wait_ge(s["xt"], g + 1)
                        wait(pe, s["xtT"], g)
                        self.transpose_in(pe, XT_BANK, xt).then_inc(s["xt_tr"], 1)
                        pe.wait_ge(s["xh"], g + 1)
                        wait(pe, s["xhT"], g)
                        self.transpose_in(pe, XH_BANK, xh).then_inc(s["xh_tr"], 1)

                    def logits(g):
                        pe.wait_ge(s["xtT"], g + 1)
                        wait(pe, s["mask16"], g)
                        for j in range(GB):
                            last = nc.tensor.matmul(ps[:, MISC_BANK, j * E1:(j + 1) * E1], cols(xtT[:, 0], j), wg[:],
                                                    start=True, stop=True)
                        last.then_inc(s["logit_mm"], 1)

                    def up(g):
                        pe.wait_ge(s["xhT"], g + 1)
                        for blk in range(NB1):
                            wait(pe, s["gelu"], 2 * (g - 1) + blk + 1)
                            nc.tensor.matmul(ps[:, UP_BANK + blk],
                                             w1s[:, 4 * blk:4 * blk + 4].rearrange("p e h -> p (e h)"), xhT[:, 0],
                                             start=True, stop=True).then_inc(s["up"], 1)

                    pe.wait_ge(s["w_in"], 16 * 8)
                    pe.wait_ge(s["w_folded"], 1)
                    for e in range(E1):
                        c = 32 * (e % 4)
                        last = nc.tensor.matmul(ps[c:c + 32, DOWN_BANK, e // 4:e // 4 + 1], w1[:, e], lnb[:, e:e + 1],
                                                start=True, stop=True, tile_position=(0, c))
                    last.then_inc(s["fold_mm"], 1)
                    transposes(0)
                    logits(0)
                    up(0)
                    pe.wait_ge(s["expand"], 1)
                    pe.wait_ge(s["bias"], 1)

                    def step(i, par):
                        g = 2 * i + par
                        if has_group(i, par, 1):
                            transposes(g + 1)
                        pe.wait_ge(s["mask"], g + 1)
                        for j in range(GB):
                            last = nc.tensor.transpose(ps[0:E1, MISC_BANK, j * P:(j + 1) * P], mask[:, j],
                                                       self.ident[:])
                        last.then_inc(s["mask_tr"], 1)
                        pe.wait_ge(s["mask16"], g + 1)
                        wait(pe, s["hm"], 2 * g)
                        for blk in range(NB1):
                            last = nc.tensor.matmul(ps[:, SPREAD_BANK + blk], expand16[:, blk * P:(blk + 1) * P],
                                                    mask16[:], start=True, stop=True)
                        last.then_inc(s["spread"], 1)
                        if has_group(i, par, 1):
                            logits(g + 1)
                            up(g + 1)
                        pe.wait_ge(s["hm"], 2 * g + 2)
                        wait(pe, s["out"], g)
                        for j in range(GB):
                            out = ps[:, DOWN_BANK, j * P:(j + 1) * P]
                            nc.tensor.matmul(out, cols(maskT, j), b2[:], start=True, stop=False)
                            for blk in range(NB1):
                                last = nc.tensor.matmul(out, cols(hm[:, blk], j), w2[:, blk], start=False,
                                                        stop=(blk == NB1 - 1))
                        last.then_inc(s["down"], 1)

                    group_steps(pe, step)


def program(nc, ins, out):
    Kernel(nc, ins, out).build()


def rope_tables():
    freqs = (np.float32(1.0) / np.float32(10000.0) ** (np.arange(0, P, 2, dtype=np.float32) / np.float32(P)))
    ang = np.outer(np.arange(P, dtype=np.float32), freqs.astype(np.float32)).astype(np.float32)
    cos, sin = np.cos(ang), np.sin(ang)
    order = channel_order()
    sign = np.where(order % 2 == 0, -1.0, 1.0).astype(np.float32)
    return np.stack([cos.T[order // 2], sin.T[order // 2] * sign[:, None]], axis=1).astype(np.float32)


def channel_order():
    return np.arange(P).reshape(2, BLK, D).transpose(0, 2, 1).reshape(-1)


def kernel(**inputs):
    import concourse.bacc as bacc
    from concourse.bass_utils import run_bass_kernel_spmd

    a = {k: np.asarray(v) for k, v in inputs.items()}
    order = channel_order()
    arrays = {
        "x": np.ascontiguousarray(a["x"].transpose(1, 0, 2)),
        "ctx": np.ascontiguousarray(a["ctx_1024"].transpose(1, 0, 2)),
        "rope": rope_tables(),
    }
    for l, (q, k, v, o) in enumerate((("L0_xattn_Wq", "L0_xattn_Wk", "L0_xattn_Wv", "L0_xattn_Wo"),
                                      ("L1_xattn_w_q", "L1_xattn_w_k", "L1_xattn_w_v", "L1_xattn_w_o"))):
        arrays[f"attn_w{l}"] = np.ascontiguousarray(np.stack(
            [a[q][order].T, a[q][order ^ 1].T, a[k][order].T, a[k][order ^ 1].T, a[v].T, a[o].T], axis=1))
    def cat(experts, shared):
        return np.concatenate([a[experts], a[shared][None]], axis=0)

    arrays |= {
        "f0_w1": np.ascontiguousarray(cat("L0_ffn_ew1", "L0_ffn_sw1").transpose(1, 0, 2)),
        "f0_b1": np.ascontiguousarray(cat("L0_ffn_eb1", "L0_ffn_sb1").reshape(NE * HB, P).T),
        "f0_w2": np.ascontiguousarray(cat("L0_ffn_ew2", "L0_ffn_sw2").reshape(NE, HB, P, P).transpose(2, 0, 1, 3)),
        "f0_b2": cat("L0_ffn_eb2", "L0_ffn_sb2"),
        "f0_rw": np.ascontiguousarray(a["L0_ffn_router_w"].T),
        "f0_nw": np.ascontiguousarray(a["L0_ffn_norm_weight"][:, None]),
        "f1_w1": np.ascontiguousarray(a["L1_ffn_W1"].transpose(1, 0, 2)),
        "f1_lns": np.ascontiguousarray(a["L1_ffn_ln_scale"].T),
        "f1_lnb": np.ascontiguousarray(a["L1_ffn_ln_bias"].T),
        "f1_b1": np.ascontiguousarray(a["L1_ffn_b1"].reshape(-1, P).T),
        "f1_w2": np.ascontiguousarray(a["L1_ffn_W2"].reshape(-1, P, P).transpose(1, 0, 2)),
        "f1_b2": np.ascontiguousarray(a["L1_ffn_b2"]),
        "f1_wg": np.ascontiguousarray(a["L1_ffn_Wg"].T),
        "f1_expand": np.repeat(np.eye(E1, dtype=np.float32), H1, axis=1),
    }
    nc = bacc.Bacc("TRN2", target_bir_lowering=False, num_devices=1)
    ins = {n: nc.dram_tensor(f"in_{n}", v.shape, mybir.dt.from_np(v.dtype), kind="ExternalInput").ap()
           for n, v in arrays.items()}
    out = nc.dram_tensor("out", (P, B, P), F32, kind="ExternalOutput").ap()
    program(nc, ins, out)
    got = run_bass_kernel_spmd(nc, [{f"in_{n}": v for n, v in arrays.items()}], core_ids=[0]).results[0]["out"]
    return np.ascontiguousarray(got.transpose(1, 0, 2))
```

```python
from contextlib import ExitStack

import numpy as np

import concourse.bass as bass
from concourse import mybir

P = 128
B = 32
H, D = 16, 8
BLK = 8
GB = 4
G = B // GB
GT = GB * P
E0, HID = 8, 512
NE = E0 + 1
HB = HID // P
E1, H1 = 8, 32
SLOTS = 2
BODY = SLOTS * GB
Q_TERMS = (0, 0, 0, 1, 1, 2)
K_TERMS = (0, 1, 2, 0, 1, 0)
TERM_ROWS = 8 * len(Q_TERMS)
STACKS = 4 * len(Q_TERMS)
MAX_ROWS = 2 * 3 * BLK
CONSTS = 10
SCALE = float(1.0 / np.sqrt(np.float32(D)))
EPS_LN, EPS_RMS, EPS_TOP = 1e-5, 1e-8, 1e-6

ALU = mybir.AluOpType
ACT = mybir.ActivationFunctionType
F32 = mybir.dt.float32
BF16 = mybir.dt.bfloat16
U32 = mybir.dt.uint32
AX = mybir.AxisListType.X


def wait(eng, sem, value):
    if not (isinstance(value, int) and value <= 0):
        eng.wait_ge(sem, value)


def group_steps(eng, step):
    step(0, 0)
    step(0, 1)
    with eng.Fori(1, G // 2 - 1) as i:
        step(i, 0)
        step(i, 1)
    step(G // 2 - 1, 0)
    step(G // 2 - 1, 1)


def has_group(i, par, ahead):
    return not isinstance(i, int) or 2 * i + par + ahead < G


def batch_steps(eng, step):
    for k in range(BODY):
        step(0, k)
    with eng.Fori(1, B // BODY - 1) as i:
        for k in range(BODY):
            step(i, k)
    for k in range(BODY + 4):
        step(B // BODY - 1 + k // BODY, k % BODY)


def has_batch(i, k, off):
    return not isinstance(i, int) or 0 <= BODY * i + k + off < B


class Kernel:
    def __init__(self, nc, ins, out):
        self.nc, self.ins, self.out = nc, ins, out
        self.ctx = ExitStack()
        self.open_sems = []

    def sb(self, name, shape, dtype=F32):
        return self.ctx.enter_context(self.nc.sbuf_tensor(name, shape, dtype))

    def sem(self, name):
        self.open_sems.append(self.nc.alloc_semaphore(name=name))
        return self.open_sems[-1]

    def renew_semaphores(self):
        self.nc.clear_and_free_semaphores(self.open_sems)
        self.open_sems = []
        self.nc.all_engine_barrier()

    def wait_apart(self, eng, *counts):
        counts = [(sem, value if isinstance(value, int) else eng.to_reg(value)) for sem, value in counts]
        eng.wait_ge(self.const_done, CONSTS)
        for sem, value in counts:
            wait(eng, sem, value)

    def sems(self, prefix, names):
        return {n: self.sem(f"{prefix}_{n}") for n in names.split()}

    def build(self):
        nc = self.nc
        with self.ctx:
            self.x = self.sb("x", [P, B, P])
            self.v = self.sb("v", [P, B, P])
            self.parts = [self.sb(f"{n}_parts", [P, 3, B * P], BF16) for n in "qk"]
            self.q_stack = self.sb("q_stack", [P, SLOTS, BLK * GT], BF16)
            self.k_stack = [self.sb(f"k_stack{par}", [P, SLOTS, BLK * GT], BF16) for par in range(2)]
            self.f0_w1 = self.sb("f0_w1", [P, NE, HID])
            self.f0_w2 = self.sb("f0_w2", [P, NE, HB, P])
            self.scratch = self.sb("scratch", [P, 8 * GT])
            sc = self.scratch[:]
            self.c_in = sc[:, 0:2 * GT].rearrange("p (r n) -> p r n", r=2)
            self.cT = sc[:, 2 * GT:4 * GT].rearrange("p (r n) -> p r n", r=2)
            self.xT = sc[:, 4 * GT:6 * GT].rearrange("p (r n) -> p r n", r=2)
            self.xn = sc[:, 6 * GT:7 * GT]
            self.hat = sc[:, 7 * GT:8 * GT]
            self.temp = self.sb("temp", [P, 4, GT])
            self.attn_w = self.sb("attn_w", [P, 6, P])
            self.rope_t = self.sb("rope_t", [P, 2, P])
            self.ident = self.sb("ident", [P, P])
            self.ident16 = self.sb("ident16", [P, P], BF16)
            self.select = self.sb("select", [MAX_ROWS, 2, BLK, P], BF16)
            self.half = self.sb("half", [P, 8])
            self.iota8 = self.sb("iota8", [P, 8])
            self.psum = self.ctx.enter_context(nc.psum_tensor("psum", [P, 8, 512], F32))
            self.experts_in = self.sem("experts_in")
            self.consts()
            self.attention(0)
            self.ffn0()
            self.renew_semaphores()
            self.attention(1)
            self.ffn1()

    def consts(self):
        nc = self.nc
        done = self.const_done = nc.alloc_semaphore(name="const_done")
        ii = self.sb("iota_int", [P, 8], mybir.dt.int32)
        with nc.Block() as block:
            @block.gpsimd
            def _(pool):
                nc.gpsimd.memset(self.ident[:], 0.0).then_inc(done, 1)
                pool.wait_ge(done, 1)
                nc.gpsimd.affine_select(out=self.ident[:], in_=self.ident[:], compare_op=ALU.not_equal, fill=1.0,
                                        base=0, pattern=[[-1, P]], channel_multiplier=1).then_inc(done, 1)
                nc.gpsimd.iota(ii[:], pattern=[[1, 8]], base=0, channel_multiplier=0).then_inc(done, 1)
                pool.wait_ge(done, 3)
                nc.gpsimd.tensor_copy(self.ident16[:], self.ident[:]).then_inc(done, 1)
                nc.gpsimd.tensor_copy(self.iota8[:], ii[:]).then_inc(done, 1)
                nc.gpsimd.memset(self.half[:], -0.5).then_inc(done, 1)
                nc.gpsimd.memset(self.select[:], 0.0).then_inc(done, 1)
                for part in range(3):
                    pool.wait_ge(done, 7 + part)
                    nc.gpsimd.affine_select(out=self.select[:], in_=self.select[:], compare_op=ALU.not_equal,
                                            fill=1.0, base=-BLK * part, pattern=[[-3 * BLK, 2], [-1, BLK], [0, P]],
                                            channel_multiplier=1).then_inc(done, 1)

    def transpose_in(self, pe, bank, src, **kw):
        for j in range(GB):
            last = self.nc.tensor.transpose(self.psum[:, bank, j * P:(j + 1) * P], src[:, j * P:(j + 1) * P],
                                            self.ident[:])
        return last

    def attention(self, l):
        nc, ps = self.nc, self.psum
        rope = l == 0
        s = self.sems(f"a{l}", """w_in cleared stats mv veps rstd xn xn_tr c_tr xT cT q_mm qs_mm k_mm ks_mm v_mm
            t1 t2 rot high rest mid low v_out stacked zeroed p1 negmax split_a split_b split_c split nm_tr nm_out
            p2 exps v_st pv u_out u_tr den y y_tr yT o_mm x_add""")
        x_in = [self.sem(f"a{l}_x_in{r}") for r in range(2)]
        c_in = [self.sem(f"a{l}_c_in{r}") for r in range(2)]

        with ExitStack() as local:
            def sb(name, shape, dtype=F32):
                return local.enter_context(nc.sbuf_tensor(f"a{l}_{name}", shape, dtype))

            bn = sb("bn", [P, GB, 6])
            mv = sb("mv", [P, GB, 2])
            veps = sb("veps", [P, GB])
            rstd = sb("rstd", [P, GB])
            negmax = sb("negmax", [P, 2, 2, BLK])
            nm_rest = sb("nm_rest", [P, 2, BLK])
            nm_parts = sb("nm_parts", [P, 2, 2, 3, BLK], BF16)
            nm_T = sb("nm_T", [MAX_ROWS, 2, P], BF16)
            v_st = sb("v_st", [P, 2, H, D + 1])
            u = sb("u", [P, 4, P])
            rden = sb("rden", [P, H])
            y = sb("y", [P, P])
            yT = sb("yT", [P, P])
            w_q, w_qs, w_k, w_ks, w_v, w_o = (self.attn_w[:, n] for n in range(6))
            t2, rot, rest = self.temp[:, 0], [self.temp[:, 1], self.temp[:, 2]], [self.temp[:, 3], self.hat]
            cos4 = self.rope_t[:, 0:1].to_broadcast([P, GB, P])
            sin4 = self.rope_t[:, 1:2].to_broadcast([P, GB, P])
            pt = self.temp[:].rearrange("p (r a) n -> p r (a n)", r=2).rearrange("p r (a b t) -> p r a b t", a=2, b=4)
            XN_BANK, C_BANK, Q_BANK, QS_BANK, K_BANK, KS_BANK, V_BANK = range(7)
            P1_BANK, P2_BANK, PV_BANK, TAIL_BANK = 0, 2, 6, 7
            nm_psum = ps[0:MAX_ROWS, TAIL_BANK].bitcast(BF16)[:, 4 * P:5 * P]

            def four(ap):
                return ap.rearrange("p (b t) -> p b t", b=GB)

            with nc.Block() as block:
                @block.sync
                def _(sp):
                    sp.dma_start(self.attn_w[:], self.ins[f"attn_w{l}"]).then_inc(s["w_in"], 16)
                    if rope:
                        sp.dma_start(self.rope_t[:], self.ins["rope"]).then_inc(s["w_in"], 16)

                    def stack(g, slot):
                        self.wait_apart(sp, (s["high"], 2 * g + 2), (s["mid"], 2 * g + 2), (s["low"], 2 * g + 2),
                                        (s["stacked"], 16 * STACKS * g))
                        if not isinstance(g, int):
                            self.wait_apart(sp, (s["p2"], 2 * GB * (g - SLOTS + 1)))
                        elif l == 0:
                            sp.wait_ge(s["cleared"], g + 1)
                        for par in range(2):
                            for dst, parts, terms in ((self.q_stack, self.parts[0], Q_TERMS),
                                                      (self.k_stack[par], self.parts[1], K_TERMS)):
                                for t, part in enumerate(terms):
                                    r0 = 64 * par + 8 * t
                                    sp.dma_start(dst[r0:r0 + 8, slot],
                                                 parts[64 * par:64 * par + 64, part, bass.ts(g, GT)],
                                                 ).then_inc(s["stacked"], 16)

                    for g in range(SLOTS):
                        stack(g, g)
                    if l == 0:
                        sp.dma_start(self.f0_w1[:], self.ins["f0_w1"]).then_inc(self.experts_in, 16)
                        sp.dma_start(self.f0_w2[:], self.ins["f0_w2"]).then_inc(self.experts_in, 16)
                    with sp.Fori(1, G // SLOTS) as i:
                        for slot in range(SLOTS):
                            stack(SLOTS * i + slot, slot)

                @block.gpsimd
                def _(pool):
                    def clear(slot):
                        for dst in (self.q_stack, *self.k_stack):
                            last = nc.gpsimd.memset(dst[:, slot].bitcast(F32), 0.0)
                        last.then_inc(s["cleared"], 1)

                    def inverse_std(g):
                        self.wait_apart(pool, (s["mv"], g + 1))
                        nc.gpsimd.tensor_scalar(veps[:], mv[:, :, 1], EPS_LN, None, ALU.add).then_inc(s["veps"], 1)
                        pool.wait_ge(s["veps"], g + 1)
                        nc.gpsimd.tensor_tensor(rstd[:], veps[:], self.half[:, 0:GB], ALU.pow).then_inc(s["rstd"], 1)

                    def low(n, w, g):
                        pool.wait_ge(s["mid"], n + 1)
                        nc.gpsimd.tensor_tensor(self.parts[w][:, 2, bass.ts(g, GT)], rest[w],
                                                self.parts[w][:, 1, bass.ts(g, GT)], ALU.subtract).then_inc(s["low"], 1)

                    inverse_std(0)
                    if l == 0:
                        for slot in range(SLOTS):
                            clear(slot)

                    def project(i, par):
                        g = 2 * i + par
                        if has_group(i, par, 1):
                            inverse_std(g + 1)
                        low(2 * g, 0, g)
                        low(2 * g + 1, 1, g)

                    group_steps(pool, project)
                    for r in range(2):
                        last = nc.gpsimd.memset(v_st[:, r, :, D:D + 1], 1.0)
                    last.then_inc(s["v_st"], 1)
                    pool.wait_ge(s["v_out"], G)

                    def step(i, k):
                        b = BODY * i + k
                        if has_batch(i, k, -1):
                            self.wait_apart(pool, (s["pv"], 2 * (b - 2)))
                            nc.gpsimd.tensor_copy(v_st[:, (k - 1) % 2, :, 0:D],
                                                  self.v[:, b - 1].rearrange("p (h d) -> p h d", h=H),
                                                  ).then_inc(s["v_st"], 1)
                        if has_batch(i, k, 0):
                            r = k % 2
                            self.wait_apart(pool, (s["negmax"], 4 * b + 4), (s["nm_tr"], b - 1))
                            nc.gpsimd.tensor_copy(nm_parts[:, r, :, 0], negmax[:, r]).then_inc(s["split_a"], 1)
                            pool.wait_ge(s["split_a"], b + 1)
                            nc.gpsimd.tensor_tensor(nm_rest[:], negmax[:, r], nm_parts[:, r, :, 0],
                                                    ALU.subtract).then_inc(s["split_b"], 1)
                            self.wait_apart(pool, (s["split_b"], b + 1))
                            nc.gpsimd.tensor_copy(nm_parts[:, r, :, 1], nm_rest[:]).then_inc(s["split_c"], 1)
                            pool.wait_ge(s["split_c"], b + 1)
                            nc.gpsimd.tensor_tensor(nm_parts[:, r, :, 2], nm_rest[:], nm_parts[:, r, :, 1],
                                                    ALU.subtract).then_inc(s["split"], 1)

                    batch_steps(pool, step)

                @block.scalar
                def _(act):
                    def load(g, par):
                        if l == 0:
                            act.dma_start(self.x[:, bass.ts(g, GB)], self.ins["x"][:, bass.ts(g, GB)],
                                          ).then_inc(x_in[par], 16)
                        act.dma_start(four(self.c_in[:, par]), self.ins["ctx"][:, bass.ts(g, GB)],
                                      ).then_inc(c_in[par], 16)

                    def copy_c(g, par):
                        act.wait_ge(s["c_tr"], g + 1)
                        wait(act, s["v_mm"], g - 1)
                        nc.scalar.activation(self.cT[:, par], ps[:, C_BANK], ACT.Copy).then_inc(s["cT"], 1)

                    def copy_x(g, par):
                        act.wait_ge(s["xn_tr"], g + 1)
                        wait(act, s["qs_mm" if rope else "q_mm"], g - 1)
                        nc.scalar.activation(self.xT[:, par], ps[:, XN_BANK], ACT.Copy).then_inc(s["xT"], 1)

                    def high(w, g):
                        if rope:
                            act.wait_ge(s["rot"], 2 * g + w + 1)
                        else:
                            act.wait_ge(s[("q_mm", "k_mm")[w]], g + 1)
                        nc.scalar.activation(self.parts[w][:, 0, bass.ts(g, GT)],
                                             rot[w] if rope else ps[:, (Q_BANK, K_BANK)[w]],
                                             ACT.Copy).then_inc(s["high"], 1)

                    def middle(w, g):
                        act.wait_ge(s["rest"], 2 * g + w + 1)
                        nc.scalar.activation(self.parts[w][:, 1, bass.ts(g, GT)], rest[w], ACT.Copy,
                                             ).then_inc(s["mid"], 1)

                    load(0, 0)
                    load(1, 1)
                    copy_c(0, 0)
                    copy_x(0, 0)

                    def project(i, par):
                        g = 2 * i + par
                        if has_group(i, par, 2):
                            act.wait_ge(s["c_tr"], g + 1)
                            load(g + 2, par)
                        high(0, g)
                        if has_group(i, par, 1):
                            copy_c(g + 1, 1 - par)
                            copy_x(g + 1, 1 - par)
                        high(1, g)
                        act.wait_ge(s["v_mm"], g + 1)
                        nc.scalar.activation(self.v[:, bass.ts(g, GB)], four(ps[:, V_BANK]), ACT.Copy,
                                             ).then_inc(s["v_out"], 1)
                        middle(0, g)
                        middle(1, g)

                    group_steps(act, project)

                    act.wait_ge(s["low"], 2 * G)
                    act.wait_ge(s["rest"], 2 * G)

                    def step(i, k):
                        b = BODY * i + k

                        def exp(unit):
                            n = 2 * (b - 2) + unit
                            act.wait_ge(s["p2"], n + 1)
                            wait(act, s["pv"], n - 1)
                            nc.scalar.activation(pt[:, unit].rearrange("p a b t -> p (a b t)"),
                                                 ps[:, P2_BANK + 2 * unit:P2_BANK + 2 * unit + 2]
                                                 .rearrange("p a n -> p (a n)"),
                                                 ACT.Exp, scale=SCALE).then_inc(s["exps"], 1)

                        if has_batch(i, k, -3):
                            act.wait_ge(s["pv"], 2 * (b - 3) + 2)
                            wait(act, s["u_tr"], b - 3)
                            nc.scalar.activation(u[:], four(ps[:, PV_BANK]), ACT.Copy).then_inc(s["u_out"], 1)
                        if has_batch(i, k, -2):
                            exp(0)
                            exp(1)
                        if has_batch(i, k, -1):
                            act.wait_ge(s["nm_tr"], b)
                            if has_batch(i, k, -3):
                                act.wait_ge(s["y_tr"], b - 2)
                            wait(act, s["p2"], 2 * (b - 3) + 2)
                            nc.scalar.activation(nm_T[:, (k - 1) % 2], nm_psum, ACT.Copy).then_inc(s["nm_out"], 1)
                        if has_batch(i, k, -3):
                            act.wait_ge(s["y_tr"], b - 2)
                            wait(act, s["o_mm"], b - 3)
                            nc.scalar.activation(yT[:], ps[:, TAIL_BANK, 0:P], ACT.Copy).then_inc(s["yT"], 1)

                    batch_steps(act, step)

                @block.vector
                def _(dve):
                    def statistics(g, par, loads):
                        if l == 0:
                            dve.wait_ge(x_in[par], 16 * loads)
                        for j in range(GB):
                            last = nc.vector.bn_stats(bn[:, j], self.x[:, 4 * g + j])
                        last.then_inc(s["stats"], 1)
                        self.wait_apart(dve, (s["stats"], g + 1), (s["rstd"], g))
                        for j in range(GB):
                            last = nc.vector.bn_aggr(mv[:, j], bn[:, j])
                        last.then_inc(s["mv"], 1)

                    def norm(g):
                        dve.wait_ge(s["mv"], g + 1)
                        dve.wait_ge(s["rstd"], g + 1)
                        wait(dve, s["xn_tr"], g)
                        for j in range(GB):
                            last = nc.vector.tensor_scalar(self.xn[:, j * P:(j + 1) * P], self.x[:, 4 * g + j],
                                                           mv[:, j, 0:1], rstd[:, j:j + 1], ALU.subtract, ALU.mult)
                        last.then_inc(s["xn"], 1)

                    def rotate(w, g):
                        n = 2 * g + w
                        dve.wait_ge(s[("q_mm", "k_mm")[w]], g + 1)
                        wait(dve, s["high"], n - 1)
                        wait(dve, s["rest"], n - 1)
                        nc.vector.tensor_tensor(four(rot[w]), four(ps[:, (Q_BANK, K_BANK)[w]]), cos4, ALU.mult,
                                                ).then_inc(s["t1"], 1)
                        dve.wait_ge(s[("qs_mm", "ks_mm")[w]], g + 1)
                        wait(dve, s["rot"], n)
                        nc.vector.tensor_tensor(four(t2), four(ps[:, (QS_BANK, KS_BANK)[w]]), sin4, ALU.mult,
                                                ).then_inc(s["t2"], 1)
                        dve.wait_ge(s["t1"], n + 1)
                        dve.wait_ge(s["t2"], n + 1)
                        nc.vector.tensor_tensor(rot[w], rot[w], t2, ALU.add).then_inc(s["rot"], 1)

                    def remainder(w, g):
                        n = 2 * g + w
                        if rope:
                            dve.wait_ge(s["rot"], n + 1)
                        dve.wait_ge(s["high"], n + 1)
                        wait(dve, s["low"], n - 1)
                        nc.vector.tensor_tensor(rest[w], rot[w] if rope else ps[:, (Q_BANK, K_BANK)[w]],
                                                self.parts[w][:, 0, bass.ts(g, GT)], ALU.subtract).then_inc(s["rest"], 1)

                    dve.wait_ge(s["w_in"], 32 if rope else 16)
                    statistics(0, 0, 1)
                    norm(0)

                    def project(i, par):
                        g = 2 * i + par
                        if has_group(i, par, 1):
                            statistics(g + 1, 1 - par, i + (par + 1) // 2 + 1)
                        if rope:
                            rotate(0, g)
                        if has_group(i, par, 1):
                            norm(g + 1)
                        if rope:
                            rotate(1, g)
                        remainder(0, g)
                        remainder(1, g)

                    group_steps(dve, project)
                    dve.wait_ge(s["v_out"], G)
                    nc.vector.memset(ps[:, PV_BANK], 0.0).then_inc(s["zeroed"], 1)

                    def step(i, k):
                        b = BODY * i + k
                        r = k % 2

                        def maxima(unit):
                            half, par = unit // 2, unit % 2
                            dve.wait_ge(s["p1"], 4 * b + unit + 1)
                            if unit == 0:
                                wait(dve, s["split"], b - 1)
                            nc.vector.tensor_reduce(negmax[:, r, par, 4 * half:4 * half + 4],
                                                    ps[:, P1_BANK + par].rearrange("p (b t) -> p b t", b=4),
                                                    AX, ALU.max, negate=True).then_inc(s["negmax"], 1)

                        if has_batch(i, k, 0):
                            maxima(0)
                            maxima(1)
                        if has_batch(i, k, -4):
                            dve.wait_ge(s["o_mm"], b - 3)
                            nc.vector.tensor_tensor(self.x[:, b - 4], ps[:, TAIL_BANK, P:2 * P], self.x[:, b - 4],
                                                    ALU.add).then_inc(s["x_add"], 1)
                        if has_batch(i, k, 0):
                            maxima(2)
                            maxima(3)
                        if has_batch(i, k, -3):
                            dve.wait_ge(s["u_tr"], b - 2)
                            sums = ps[:, TAIL_BANK].rearrange("p (h n) -> p h n", h=H)
                            nc.vector.reciprocal(rden[:], sums[:, :, D]).then_inc(s["den"], 1)
                            dve.wait_ge(s["den"], b - 2)
                            wait(dve, s["y_tr"], b - 3)
                            nc.vector.tensor_tensor(y[:].rearrange("p (h d) -> p h d", h=H), sums[:, :, 0:D],
                                                    rden[:].unsqueeze(2).to_broadcast([P, H, D]),
                                                    ALU.mult).then_inc(s["y"], 1)

                    batch_steps(dve, step)

                @block.tensor
                def _(pe):
                    def transpose_c(g, par, loads):
                        pe.wait_ge(c_in[par], 16 * loads)
                        wait(pe, s["cT"], g)
                        self.transpose_in(pe, C_BANK, self.c_in[:, par]).then_inc(s["c_tr"], 1)

                    def transpose_x(g):
                        pe.wait_ge(s["xn"], g + 1)
                        wait(pe, s["xT"], g)
                        self.transpose_in(pe, XN_BANK, self.xn).then_inc(s["xn_tr"], 1)

                    def product(w, weight, swapped, rhs, g):
                        wait(pe, s["t2" if rope else "rest"], 2 * (g - 1) + w + 1)
                        mm, mms = (("q_mm", "qs_mm"), ("k_mm", "ks_mm"))[w]
                        nc.tensor.matmul(ps[:, (Q_BANK, K_BANK)[w]], weight, rhs, start=True, stop=True,
                                         ).then_inc(s[mm], 1)
                        if rope:
                            nc.tensor.matmul(ps[:, (QS_BANK, KS_BANK)[w]], swapped, rhs, start=True, stop=True,
                                             ).then_inc(s[mms], 1)

                    pe.wait_ge(s["w_in"], 32 if rope else 16)
                    transpose_c(0, 0, 1)
                    transpose_x(0)

                    def project(i, par):
                        g = 2 * i + par
                        pe.wait_ge(s["xT"], g + 1)
                        product(0, w_q, w_qs, self.xT[:, par], g)
                        pe.wait_ge(s["cT"], g + 1)
                        product(1, w_k, w_ks, self.cT[:, par], g)
                        if has_group(i, par, 1):
                            transpose_c(g + 1, 1 - par, i + (par + 1) // 2 + 1)
                            transpose_x(g + 1)
                        wait(pe, s["v_out"], g)
                        for j in range(GB):
                            last = nc.tensor.matmul(ps[:, V_BANK, j * P:(j + 1) * P], self.cT[:, par, j * P:(j + 1) * P],
                                                    w_v, start=True, stop=True)
                        last.then_inc(s["v_mm"], 1)

                    group_steps(pe, project)
                    pe.wait_ge(s["rest"], 2 * G)
                    pe.wait_ge(s["zeroed"], 1)

                    def step(i, k):
                        b = BODY * i + k

                        def stacked(k, stack, blk):
                            return stack[:, k // GB, blk * GT + k % GB * P:blk * GT + (k % GB + 1) * P]

                        def p1(half):
                            if half == 0 and k % GB == 0:
                                pe.wait_ge(s["stacked"], 16 * STACKS * (SLOTS * i + k // GB + 1))
                            for par in range(2):
                                unit = 2 * half + par
                                wait(pe, s["negmax"], 4 * b + unit - 1)
                                for j in range(4):
                                    last = nc.tensor.matmul(ps[:, P1_BANK + par, j * P:(j + 1) * P],
                                                            stacked(k, self.q_stack, 4 * half + j),
                                                            stacked(k, self.k_stack[par], 4 * half + j),
                                                            start=True, stop=True)
                                last.then_inc(s["p1"], 1)

                        def p2(half):
                            if half == 0:
                                pe.wait_ge(s["nm_out"], b - 1)
                            wait(pe, s["exps"], 2 * (b - 3) + half + 1)
                            for par in range(2):
                                for j in range(4):
                                    blk, out = 4 * half + j, ps[:, P2_BANK + 2 * half + par, j * P:(j + 1) * P]
                                    nc.tensor.matmul(out, stacked((k - 2) % BODY, self.k_stack[par], blk),
                                                     stacked((k - 2) % BODY, self.q_stack, blk),
                                                     start=True, stop=False)
                                    last = nc.tensor.matmul(out, self.select[:, par, blk], nm_T[:, k % 2],
                                                            start=False, stop=True)
                            last.then_inc(s["p2"], 1)

                        def pv(half, c, r):
                            if half == 0:
                                pe.wait_ge(s["v_st"], c + 2)
                                wait(pe, s["u_out"], c)
                            pe.wait_ge(s["exps"], 2 * c + half + 1)
                            for par in range(2):
                                for j in range(4):
                                    last = nc.tensor.matmul(ps[32 * j:32 * j + D + 1, PV_BANK,
                                                               (2 * par + half) * P:(2 * par + half + 1) * P],
                                                            v_st[:, r, 8 * par + 4 * half + j],
                                                            pt[:, half, par, j], start=True, stop=True,
                                                            tile_position=(0, 32 * j))
                            last.then_inc(s["pv"], 1)

                        if has_batch(i, k, 0):
                            p1(0)
                        if has_batch(i, k, -3):
                            pv(1, b - 3, (k - 3) % 2)
                        if has_batch(i, k, -4):
                            pe.wait_ge(s["yT"], b - 3)
                            nc.tensor.matmul(ps[:, TAIL_BANK, P:2 * P], yT[:], w_o, start=True, stop=True
                                             ).then_inc(s["o_mm"], 1)
                        if has_batch(i, k, -2):
                            p2(0)
                        if has_batch(i, k, 0):
                            p1(1)
                        if has_batch(i, k, -3):
                            pe.wait_ge(s["u_out"], b - 2)
                            wait(pe, s["x_add"], b - 3)
                            if has_batch(i, k, -2):
                                wait(pe, s["nm_out"], b - 1)
                            for n in range(4):
                                last = nc.tensor.transpose(ps[:, TAIL_BANK, n * P:(n + 1) * P], u[:, n], self.ident[:])
                            last.then_inc(s["u_tr"], 1)
                        if has_batch(i, k, -2):
                            pv(0, b - 2, k % 2)
                            p2(1)
                        sums_read = [(s["y"], b - 2)] if has_batch(i, k, -3) else []
                        if has_batch(i, k, -1):
                            self.wait_apart(pe, (s["split"], b), (s["nm_out"], b - 1), *sums_read)
                            nc.tensor.transpose(nm_psum, nm_parts[:, (k - 1) % 2].rearrange("p a n b -> p (a n b)"),
                                                self.ident16[:]).then_inc(s["nm_tr"], 1)
                        if has_batch(i, k, -3):
                            pe.wait_ge(s["y"], b - 2)
                            nc.tensor.transpose(ps[:, TAIL_BANK, 0:P], y[:], self.ident[:]).then_inc(s["y_tr"], 1)

                    batch_steps(pe, step)

    def ffn0(self):
        nc, ps = self.nc, self.psum
        s = self.sems("f0", """small_in stats mv veps rstd hat sq sveps srstd xn xn_tr xT logit_mm prob
            top8 idx idxf m0 m1 mask picked total rtot comb comb_tr combT up relu down acc""")
        UP_BANK, DOWN_BANK, T_BANK, MISC_BANK = 0, 4, 6, 7
        w1, w2 = self.f0_w1, self.f0_w2
        hid = self.parts[0][:].rearrange("p a n -> p (a n)").bitcast(F32)[:, 0:2 * HB * GT].rearrange(
            "p (r b n) -> p r b n", r=2, b=HB)

        with ExitStack() as local:
            def sb(name, shape, dtype=F32):
                return local.enter_context(nc.sbuf_tensor(f"f0_{name}", shape, dtype))

            b1 = sb("b1", [P, NE * HB])
            b2 = sb("b2", [NE, P])
            rw = sb("rw", [P, E0])
            nw = sb("nw", [P, 1])
            bn = sb("bn", [P, GB, 6])
            mv = sb("mv", [P, GB, 2])
            veps = sb("veps", [P, GB])
            rstd = sb("rstd", [P, GB])
            sq = sb("sq", [P, GB])
            sveps = sb("sveps", [P, GB])
            srstd = sb("srstd", [P, GB])
            prob = sb("prob", [P, GB, E0])
            top8 = sb("top8", [P, GB, E0])
            idx = sb("idx", [P, GB, E0], U32)
            idxf = sb("idxf", [P, GB, 2])
            m0 = sb("m0", [P, GB, E0])
            m1 = sb("m1", [P, GB, E0])
            mask = sb("mask", [P, GB, E0])
            picked = sb("picked", [P, GB, E0])
            total = sb("total", [P, GB])
            rtot = sb("rtot", [P, GB])
            comb = sb("comb", [P, 2, GB, NE])
            combT = sb("combT", [NE, 2, GT])
            hat, xn, xT = self.hat, self.xn, self.xT

            def cols(ap, j):
                return ap[:, j * P:(j + 1) * P]

            def eight(ap):
                return ap.to_broadcast([P, GB, E0])

            with nc.Block() as block:
                @block.sync
                def _(sp):
                    for dst, name in ((b1, "f0_b1"), (b2, "f0_b2"), (rw, "f0_rw"), (nw, "f0_nw")):
                        sp.dma_start(dst[:], self.ins[name]).then_inc(s["small_in"], 16)

                @block.gpsimd
                def _(pool):
                    def roots(g):
                        self.wait_apart(pool, (s["mv"], g + 1))
                        nc.gpsimd.tensor_scalar(veps[:], mv[:, :, 1], EPS_LN, None, ALU.add).then_inc(s["veps"], 1)
                        pool.wait_ge(s["veps"], g + 1)
                        nc.gpsimd.tensor_tensor(rstd[:], veps[:], self.half[:, 0:GB], ALU.pow).then_inc(s["rstd"], 1)
                        self.wait_apart(pool, (s["sq"], g + 1))
                        nc.gpsimd.tensor_scalar(sveps[:], sq[:], 1.0 / P, EPS_RMS, ALU.mult, ALU.add,
                                                ).then_inc(s["sveps"], 1)
                        pool.wait_ge(s["sveps"], g + 1)
                        nc.gpsimd.tensor_tensor(srstd[:], sveps[:], self.half[:, 0:GB], ALU.pow,
                                                ).then_inc(s["srstd"], 1)

                    with pool.Fori(0, G) as g:
                        roots(g)

                @block.scalar
                def _(act):
                    def squares(g):
                        act.wait_ge(s["hat"], g + 1)
                        wait(act, s["srstd"], g)
                        for j in range(GB):
                            last = nc.scalar.activation(cols(xn, j), cols(hat, j), ACT.Square,
                                                        accum_out=sq[:, j:j + 1])
                        last.then_inc(s["sq"], 1)

                    def copy_xT(g, par):
                        act.wait_ge(s["xn_tr"], g + 1)
                        wait(act, s["up"], NE * HB * (g - 1))
                        nc.scalar.activation(xT[:, par], ps[:, T_BANK], ACT.Copy, scale=nw[:, 0:1]
                                             ).then_inc(s["xT"], 1)

                    def probs(g):
                        act.wait_ge(s["logit_mm"], g + 1)
                        wait(act, s["comb"], g)
                        nc.scalar.activation(prob[:], ps[:, MISC_BANK, 0:GB * E0].rearrange("p (j e) -> p j e", j=GB),
                                             ACT.Sigmoid).then_inc(s["prob"], 1)

                    def copy_combT(g, par):
                        act.wait_ge(s["comb_tr"], g + 1)
                        wait(act, s["down"], NE * (g - 1))
                        nc.scalar.activation(combT[:, par], ps[0:NE, MISC_BANK], ACT.Copy).then_inc(s["combT"], 1)

                    act.wait_ge(s["small_in"], 64)
                    squares(0)
                    copy_xT(0, 0)
                    probs(0)
                    copy_combT(0, 0)

                    def step(i, par):
                        g = 2 * i + par
                        for e in range(NE):
                            n = NE * g + e
                            for hb in range(HB):
                                act.wait_ge(s["up"], HB * n + hb + 1)
                                if hb == 0:
                                    wait(act, s["down"], n - 1)
                                nc.scalar.activation(hid[:, (par + e) % 2, hb], ps[:, UP_BANK + hb], ACT.Relu,
                                                     bias=b1[:, HB * e + hb:HB * e + hb + 1]).then_inc(s["relu"], 1)
                            if has_group(i, par, 1):
                                if e == 1:
                                    squares(g + 1)
                                if e == 4:
                                    copy_xT(g + 1, 1 - par)
                                if e == 6:
                                    probs(g + 1)
                                if e == 8:
                                    copy_combT(g + 1, 1 - par)

                    group_steps(act, step)

                @block.vector
                def _(dve):
                    def norm1(g):
                        for j in range(GB):
                            last = nc.vector.bn_stats(bn[:, j], self.x[:, 4 * g + j])
                        last.then_inc(s["stats"], 1)
                        self.wait_apart(dve, (s["stats"], g + 1), (s["rstd"], g))
                        for j in range(GB):
                            last = nc.vector.bn_aggr(mv[:, j], bn[:, j])
                        last.then_inc(s["mv"], 1)
                        dve.wait_ge(s["mv"], g + 1)
                        dve.wait_ge(s["rstd"], g + 1)
                        wait(dve, s["sq"], g)
                        for j in range(GB):
                            last = nc.vector.tensor_scalar(cols(hat, j), self.x[:, 4 * g + j], mv[:, j, 0:1],
                                                           rstd[:, j:j + 1], ALU.subtract, ALU.mult)
                        last.then_inc(s["hat"], 1)

                    def norm2(g):
                        dve.wait_ge(s["hat"], g + 1)
                        dve.wait_ge(s["sq"], g + 1)
                        dve.wait_ge(s["srstd"], g + 1)
                        wait(dve, s["xn_tr"], g)
                        for j in range(GB):
                            last = nc.vector.tensor_scalar(cols(xn, j), cols(hat, j), srstd[:, j:j + 1], None,
                                                           ALU.mult)
                        last.then_inc(s["xn"], 1)

                    def route(g, par):
                        self.wait_apart(dve, (s["prob"], g + 1))
                        for j in range(GB):
                            last = nc.vector.max(top8[:, j], prob[:, j])
                        last.then_inc(s["top8"], 1)
                        self.wait_apart(dve, (s["top8"], g + 1))
                        for j in range(GB):
                            last = nc.vector.max_index(idx[:, j], top8[:, j], prob[:, j])
                        last.then_inc(s["idx"], 1)
                        dve.wait_ge(s["idx"], g + 1)
                        nc.vector.tensor_copy(idxf[:], idx[:, :, 0:2]).then_inc(s["idxf"], 1)
                        dve.wait_ge(s["idxf"], g + 1)
                        iota = self.iota8[:].unsqueeze(1).to_broadcast([P, GB, E0])
                        nc.vector.tensor_tensor(m0[:], iota, eight(idxf[:, :, 0:1]), ALU.is_equal).then_inc(s["m0"], 1)
                        nc.vector.tensor_tensor(m1[:], iota, eight(idxf[:, :, 1:2]), ALU.is_equal).then_inc(s["m1"], 1)
                        dve.wait_ge(s["m0"], g + 1)
                        dve.wait_ge(s["m1"], g + 1)
                        nc.vector.tensor_tensor(mask[:], m0[:], m1[:], ALU.add).then_inc(s["mask"], 1)
                        dve.wait_ge(s["mask"], g + 1)
                        nc.vector.tensor_tensor(picked[:], mask[:], prob[:], ALU.mult).then_inc(s["picked"], 1)
                        nc.vector.scalar_tensor_tensor(total[:], top8[:, :, 0], EPS_TOP, top8[:, :, 1], ALU.add,
                                                       ALU.add).then_inc(s["total"], 1)
                        dve.wait_ge(s["total"], g + 1)
                        nc.vector.reciprocal(rtot[:], total[:]).then_inc(s["rtot"], 1)
                        dve.wait_ge(s["rtot"], g + 1)
                        dve.wait_ge(s["picked"], g + 1)
                        wait(dve, s["comb_tr"], g - 1)
                        nc.vector.tensor_tensor(comb[:, par, :, 0:E0], picked[:], eight(rtot[:].unsqueeze(2)),
                                                ALU.mult).then_inc(s["comb"], 1)

                    def accumulate(n, g, par, e):
                        dve.wait_ge(s["down"], n + 1)
                        bank = DOWN_BANK + (par + e) % 2
                        for j in range(GB):
                            if e < E0:
                                last = nc.vector.scalar_tensor_tensor(
                                    self.x[:, 4 * g + j], ps[:, bank, j * P:(j + 1) * P], comb[:, par, j, e:e + 1],
                                    self.x[:, 4 * g + j], ALU.mult, ALU.add)
                            else:
                                last = nc.vector.tensor_tensor(self.x[:, 4 * g + j], ps[:, bank, j * P:(j + 1) * P],
                                                               self.x[:, 4 * g + j], ALU.add)
                        last.then_inc(s["acc"], 1)

                    for r in range(2):
                        last = nc.vector.memset(comb[:, r, :, E0:NE], 1.0)
                    last.then_inc(s["comb"], 1)
                    dve.wait_ge(s["small_in"], 64)
                    norm1(0)
                    norm2(0)
                    route(0, 0)

                    def step(i, par):
                        g = 2 * i + par
                        for e in range(NE):
                            if has_group(i, par, 1):
                                if e == 0:
                                    norm1(g + 1)
                                if e == 2:
                                    norm2(g + 1)
                                if e == 7:
                                    route(g + 1, 1 - par)
                            wait(dve, s["acc"], NE * g + e)
                            accumulate(NE * g + e, g, par, e)

                    group_steps(dve, step)

                @block.tensor
                def _(pe):
                    def transposes(g):
                        pe.wait_ge(s["xn"], g + 1)
                        wait(pe, s["xT"], g)
                        self.transpose_in(pe, T_BANK, xn).then_inc(s["xn_tr"], 1)

                    def logits(g, par):
                        pe.wait_ge(s["xT"], g + 1)
                        wait(pe, s["combT"], g)
                        for j in range(GB):
                            last = nc.tensor.matmul(ps[:, MISC_BANK, j * E0:(j + 1) * E0], cols(xT[:, par], j), rw[:],
                                                    start=True, stop=True)
                        last.then_inc(s["logit_mm"], 1)

                    def comb_transpose(g, par):
                        pe.wait_ge(s["comb"], g + 2)
                        pe.wait_ge(s["prob"], g + 1)
                        for j in range(GB):
                            last = nc.tensor.transpose(ps[0:NE, MISC_BANK, j * P:(j + 1) * P], comb[:, par, j],
                                                       self.ident[:])
                        last.then_inc(s["comb_tr"], 1)

                    def up(n, par, e):
                        for hb in range(HB):
                            wait(pe, s["relu"], HB * (n - 1) + hb + 1)
                            nc.tensor.matmul(ps[:, UP_BANK + hb], w1[:, e, hb * P:(hb + 1) * P], xT[:, par],
                                             start=True, stop=True).then_inc(s["up"], 1)

                    def down(n, par, e, combT_ready=None):
                        wait(pe, s["acc"], n - 1)
                        if e == E0:
                            pe.wait_ge(s["combT"], combT_ready)
                        for j in range(GB):
                            out = ps[:, DOWN_BANK + (par + e) % 2, j * P:(j + 1) * P]
                            if e == E0:
                                nc.tensor.matmul(out, combT[:, par, j * P:(j + 1) * P], b2[:], start=True, stop=False)
                            for hb in range(HB):
                                if j == 0:
                                    pe.wait_ge(s["relu"], HB * n + hb + 1)
                                last = nc.tensor.matmul(out, hid[:, (par + e) % 2, hb, j * P:(j + 1) * P],
                                                        w2[:, e, hb], start=(e < E0 and hb == 0), stop=(hb == HB - 1))
                        last.then_inc(s["down"], 1)

                    pe.wait_ge(s["small_in"], 64)
                    transposes(0)
                    logits(0, 0)
                    comb_transpose(0, 0)
                    pe.wait_ge(self.experts_in, 32)

                    def step(i, par):
                        g = 2 * i + par
                        for e in range(NE):
                            n = NE * g + e
                            up(n, par, e)
                            if has_group(i, par, 1):
                                if e == 4:
                                    transposes(g + 1)
                                if e == 6:
                                    logits(g + 1, 1 - par)
                                if e == 8:
                                    comb_transpose(g + 1, 1 - par)
                            if e > 0:
                                down(n - 1, par, e - 1)
                        down(NE * g + NE - 1, par, E0, g + 1)

                    group_steps(pe, step)

    def ffn1(self):
        nc, ps = self.nc, self.psum
        s = self.sems("f1", """w_in w_folded fold_mm bias expand stats mv veps rstd xt xstats xmv xveps xrstd xh
            xt_tr xh_tr xtT xhT logit_mm logit top8 idx idxf mask mask_tr maskT mask16 up gelu spread hm down out
            out_dma""")
        XT_BANK, XH_BANK, UP_BANK, SPREAD_BANK, DOWN_BANK, MISC_BANK = 0, 1, 2, 4, 6, 7
        NB1 = E1 * H1 // P
        xt, xh = self.xn, self.hat
        xtT, xhT = self.xT, self.cT

        with ExitStack() as local:
            def sb(name, shape, dtype=F32):
                return local.enter_context(nc.sbuf_tensor(f"f1_{name}", shape, dtype))

            w1 = sb("w1", [P, E1, H1])
            w1s = sb("w1s", [P, E1, H1])
            lns = sb("lns", [P, E1])
            lnb = sb("lnb", [P, E1])
            b1 = sb("b1", [P, NB1])
            b1e = sb("b1e", [P, NB1])
            w2 = sb("w2", [P, NB1, P])
            b2 = sb("b2", [E1, P])
            wg = sb("wg", [P, E1])
            expand = sb("expand", [E1, NB1 * P])
            expand16 = sb("expand16", [E1, NB1 * P], BF16)
            bn = sb("bn", [P, 2, GB, 6])
            mv = sb("mv", [P, 2, GB, 2])
            veps = sb("veps", [P, 2, GB])
            rstd = sb("rstd", [P, 2, GB])
            logit = sb("logit", [P, GB, E1])
            top8 = sb("top8", [P, GB, E1])
            idx = sb("idx", [P, GB, E1], U32)
            idxf = sb("idxf", [P, GB, 1])
            mask = sb("mask", [P, GB, E1])
            maskT = sb("maskT", [E1, GT])
            mask16 = sb("mask16", [E1, GT], BF16)
            free = self.parts[0][:].rearrange("p a n -> p (a n)").bitcast(F32)
            hg = free[:, 0:2 * NB1 * GT].rearrange("p (r b n) -> p r b n", r=2, b=NB1)
            hm = free[:, 2 * NB1 * GT:3 * NB1 * GT].rearrange("p (b n) -> p b n", b=NB1)

            def cols(ap, j):
                return ap[:, j * P:(j + 1) * P]

            with nc.Block() as block:
                @block.sync
                def _(sp):
                    pairs = ((w1, "f1_w1"), (lns, "f1_lns"), (lnb, "f1_lnb"), (b1, "f1_b1"), (w2, "f1_w2"),
                             (b2, "f1_b2"), (wg, "f1_wg"), (expand, "f1_expand"))
                    for dst, name in pairs:
                        sp.dma_start(dst[:], self.ins[name]).then_inc(s["w_in"], 16)
                    with sp.Fori(0, G) as g:
                        sp.wait_ge(s["out"], g + 1)
                        sp.dma_start(self.out[:, bass.ts(g, GB)], self.x[:, bass.ts(g, GB)]).then_inc(s["out_dma"], 16)
                    sp.wait_ge(s["out_dma"], 16 * G)

                @block.gpsimd
                def _(pool):
                    def inverse_std(g, which, ready, add, done):
                        self.wait_apart(pool, (s[ready], g + 1))
                        nc.gpsimd.tensor_scalar(veps[:, which], mv[:, which, :, 1], EPS_LN, None, ALU.add,
                                                ).then_inc(s[add], 1)
                        pool.wait_ge(s[add], g + 1)
                        nc.gpsimd.tensor_tensor(rstd[:, which], veps[:, which], self.half[:, 0:GB], ALU.pow,
                                                ).then_inc(s[done], 1)

                    with pool.Fori(0, G) as g:
                        inverse_std(g, 0, "mv", "veps", "rstd")
                        inverse_std(g, 1, "xmv", "xveps", "xrstd")

                @block.scalar
                def _(act):
                    def inputs(g):
                        act.wait_ge(s["xt_tr"], g + 1)
                        wait(act, s["logit_mm"], g)
                        nc.scalar.activation(xtT[:, 0], ps[:, XT_BANK], ACT.Copy).then_inc(s["xtT"], 1)
                        act.wait_ge(s["xh_tr"], g + 1)
                        wait(act, s["up"], 2 * g)
                        nc.scalar.activation(xhT[:, 0], ps[:, XH_BANK], ACT.Copy).then_inc(s["xhT"], 1)

                    def gelu(g, par):
                        wait(act, s["hm"], 2 * (g - 1))
                        for blk in range(NB1):
                            act.wait_ge(s["up"], 2 * g + blk + 1)
                            nc.scalar.activation(hg[:, par, blk], ps[:, UP_BANK + blk], ACT.Gelu,
                                                 bias=b1e[:, blk:blk + 1]).then_inc(s["gelu"], 1)

                    def masks(g):
                        act.wait_ge(s["mask_tr"], g + 1)
                        wait(act, s["down"], g)
                        nc.scalar.activation(maskT[:], ps[0:E1, MISC_BANK], ACT.Copy).then_inc(s["maskT"], 1)
                        wait(act, s["spread"], g)
                        nc.scalar.activation(mask16[:], ps[0:E1, MISC_BANK], ACT.Copy).then_inc(s["mask16"], 1)

                    act.wait_ge(s["w_in"], 16 * 8)
                    nc.scalar.activation(expand16[:], expand[:], ACT.Copy).then_inc(s["expand"], 1)
                    inputs(0)
                    act.wait_ge(s["bias"], 1)
                    gelu(0, 0)

                    def step(i, par):
                        g = 2 * i + par
                        if has_group(i, par, 1):
                            inputs(g + 1)
                        masks(g)
                        if has_group(i, par, 1):
                            gelu(g + 1, 1 - par)

                    group_steps(act, step)

                @block.vector
                def _(dve):
                    def norm(g, which, src, dst, stats, mvs, ready, read, done):
                        for j in range(GB):
                            last = nc.vector.bn_stats(bn[:, which, j], src[j])
                        last.then_inc(s[stats], 1)
                        self.wait_apart(dve, (s[stats], g + 1), (s[ready], g))
                        for j in range(GB):
                            last = nc.vector.bn_aggr(mv[:, which, j], bn[:, which, j])
                        last.then_inc(s[mvs], 1)
                        dve.wait_ge(s[mvs], g + 1)
                        dve.wait_ge(s[ready], g + 1)
                        wait(dve, s[read], g)
                        for j in range(GB):
                            last = nc.vector.tensor_scalar(cols(dst, j), src[j], mv[:, which, j, 0:1],
                                                           rstd[:, which, j:j + 1], ALU.subtract, ALU.mult)
                        last.then_inc(s[done], 1)

                    def norms(g):
                        norm(g, 0, [self.x[:, 4 * g + j] for j in range(GB)], xt, "stats", "mv", "rstd", "xt_tr", "xt")
                        dve.wait_ge(s["xt"], g + 1)
                        norm(g, 1, [cols(xt, j) for j in range(GB)], xh, "xstats", "xmv", "xrstd", "xh_tr", "xh")

                    def route(g):
                        dve.wait_ge(s["logit_mm"], g + 1)
                        nc.vector.tensor_copy(logit[:], ps[:, MISC_BANK, 0:GB * E1].rearrange("p (j e) -> p j e", j=GB),
                                              ).then_inc(s["logit"], 1)
                        self.wait_apart(dve, (s["logit"], g + 1))
                        for j in range(GB):
                            last = nc.vector.max(top8[:, j], logit[:, j])
                        last.then_inc(s["top8"], 1)
                        self.wait_apart(dve, (s["top8"], g + 1))
                        for j in range(GB):
                            last = nc.vector.max_index(idx[:, j], top8[:, j], logit[:, j])
                        last.then_inc(s["idx"], 1)
                        dve.wait_ge(s["idx"], g + 1)
                        nc.vector.tensor_copy(idxf[:], idx[:, :, 0:1]).then_inc(s["idxf"], 1)
                        dve.wait_ge(s["idxf"], g + 1)
                        wait(dve, s["mask_tr"], g)
                        nc.vector.tensor_tensor(mask[:], self.iota8[:].unsqueeze(1).to_broadcast([P, GB, E1]),
                                                idxf[:].to_broadcast([P, GB, E1]), ALU.is_equal).then_inc(s["mask"], 1)

                    dve.wait_ge(s["w_in"], 16 * 8)
                    for e in range(E1):
                        last = nc.vector.tensor_scalar(w1s[:, e], w1[:, e], lns[:, e:e + 1], None, ALU.mult)
                    last.then_inc(s["w_folded"], 1)
                    norms(0)
                    dve.wait_ge(s["fold_mm"], 1)
                    nc.vector.tensor_tensor(b1e[:], ps[:, DOWN_BANK, 0:NB1], b1[:], ALU.add).then_inc(s["bias"], 1)
                    route(0)
                    norms(1)

                    def step(i, par):
                        g = 2 * i + par
                        dve.wait_ge(s["spread"], g + 1)
                        wait(dve, s["down"], g)
                        for blk in range(NB1):
                            dve.wait_ge(s["gelu"], 2 * g + blk + 1)
                            nc.vector.tensor_tensor(hm[:, blk], hg[:, par, blk], ps[:, SPREAD_BANK + blk],
                                                    ALU.mult).then_inc(s["hm"], 1)
                        if has_group(i, par, 1):
                            route(g + 1)
                        if has_group(i, par, 2):
                            norms(g + 2)
                        dve.wait_ge(s["down"], g + 1)
                        nc.vector.tensor_tensor(self.x[:, bass.ts(g, GB)],
                                                ps[:, DOWN_BANK].rearrange("p (j n) -> p j n", j=GB),
                                                self.x[:, bass.ts(g, GB)], ALU.add).then_inc(s["out"], 1)

                    group_steps(dve, step)

                @block.tensor
                def _(pe):
                    def transposes(g):
                        pe.wait_ge(s["xt"], g + 1)
                        wait(pe, s["xtT"], g)
                        self.transpose_in(pe, XT_BANK, xt).then_inc(s["xt_tr"], 1)
                        pe.wait_ge(s["xh"], g + 1)
                        wait(pe, s["xhT"], g)
                        self.transpose_in(pe, XH_BANK, xh).then_inc(s["xh_tr"], 1)

                    def logits(g):
                        pe.wait_ge(s["xtT"], g + 1)
                        wait(pe, s["mask16"], g)
                        for j in range(GB):
                            last = nc.tensor.matmul(ps[:, MISC_BANK, j * E1:(j + 1) * E1], cols(xtT[:, 0], j), wg[:],
                                                    start=True, stop=True)
                        last.then_inc(s["logit_mm"], 1)

                    def up(g):
                        pe.wait_ge(s["xhT"], g + 1)
                        for blk in range(NB1):
                            wait(pe, s["gelu"], 2 * (g - 1) + blk + 1)
                            nc.tensor.matmul(ps[:, UP_BANK + blk],
                                             w1s[:, 4 * blk:4 * blk + 4].rearrange("p e h -> p (e h)"), xhT[:, 0],
                                             start=True, stop=True).then_inc(s["up"], 1)

                    pe.wait_ge(s["w_in"], 16 * 8)
                    pe.wait_ge(s["w_folded"], 1)
                    for e in range(E1):
                        c = 32 * (e % 4)
                        last = nc.tensor.matmul(ps[c:c + 32, DOWN_BANK, e // 4:e // 4 + 1], w1[:, e], lnb[:, e:e + 1],
                                                start=True, stop=True, tile_position=(0, c))
                    last.then_inc(s["fold_mm"], 1)
                    transposes(0)
                    logits(0)
                    up(0)
                    pe.wait_ge(s["expand"], 1)
                    pe.wait_ge(s["bias"], 1)

                    def step(i, par):
                        g = 2 * i + par
                        if has_group(i, par, 1):
                            transposes(g + 1)
                        pe.wait_ge(s["mask"], g + 1)
                        for j in range(GB):
                            last = nc.tensor.transpose(ps[0:E1, MISC_BANK, j * P:(j + 1) * P], mask[:, j],
                                                       self.ident[:])
                        last.then_inc(s["mask_tr"], 1)
                        pe.wait_ge(s["mask16"], g + 1)
                        wait(pe, s["hm"], 2 * g)
                        for blk in range(NB1):
                            last = nc.tensor.matmul(ps[:, SPREAD_BANK + blk], expand16[:, blk * P:(blk + 1) * P],
                                                    mask16[:], start=True, stop=True)
                        last.then_inc(s["spread"], 1)
                        if has_group(i, par, 1):
                            logits(g + 1)
                            up(g + 1)
                        pe.wait_ge(s["hm"], 2 * g + 2)
                        wait(pe, s["out"], g)
                        for j in range(GB):
                            out = ps[:, DOWN_BANK, j * P:(j + 1) * P]
                            nc.tensor.matmul(out, cols(maskT, j), b2[:], start=True, stop=False)
                            for blk in range(NB1):
                                last = nc.tensor.matmul(out, cols(hm[:, blk], j), w2[:, blk], start=False,
                                                        stop=(blk == NB1 - 1))
                        last.then_inc(s["down"], 1)

                    group_steps(pe, step)


def program(nc, ins, out):
    Kernel(nc, ins, out).build()


def rope_tables():
    freqs = (np.float32(1.0) / np.float32(10000.0) ** (np.arange(0, P, 2, dtype=np.float32) / np.float32(P)))
    ang = np.outer(np.arange(P, dtype=np.float32), freqs.astype(np.float32)).astype(np.float32)
    cos, sin = np.cos(ang), np.sin(ang)
    order = channel_order()
    sign = np.where(order % 2 == 0, -1.0, 1.0).astype(np.float32)
    return np.stack([cos.T[order // 2], sin.T[order // 2] * sign[:, None]], axis=1).astype(np.float32)


def channel_order():
    return np.arange(P).reshape(2, BLK, D).transpose(0, 2, 1).reshape(-1)


def kernel(**inputs):
    import concourse.bacc as bacc
    from concourse.bass_utils import run_bass_kernel_spmd

    a = {k: np.asarray(v) for k, v in inputs.items()}
    order = channel_order()
    arrays = {
        "x": np.ascontiguousarray(a["x"].transpose(1, 0, 2)),
        "ctx": np.ascontiguousarray(a["ctx_1024"].transpose(1, 0, 2)),
        "rope": rope_tables(),
    }
    for l, (q, k, v, o) in enumerate((("L0_xattn_Wq", "L0_xattn_Wk", "L0_xattn_Wv", "L0_xattn_Wo"),
                                      ("L1_xattn_w_q", "L1_xattn_w_k", "L1_xattn_w_v", "L1_xattn_w_o"))):
        arrays[f"attn_w{l}"] = np.ascontiguousarray(np.stack(
            [a[q][order].T, a[q][order ^ 1].T, a[k][order].T, a[k][order ^ 1].T, a[v].T, a[o].T], axis=1))
    def cat(experts, shared):
        return np.concatenate([a[experts], a[shared][None]], axis=0)

    arrays |= {
        "f0_w1": np.ascontiguousarray(cat("L0_ffn_ew1", "L0_ffn_sw1").transpose(1, 0, 2)),
        "f0_b1": np.ascontiguousarray(cat("L0_ffn_eb1", "L0_ffn_sb1").reshape(NE * HB, P).T),
        "f0_w2": np.ascontiguousarray(cat("L0_ffn_ew2", "L0_ffn_sw2").reshape(NE, HB, P, P).transpose(2, 0, 1, 3)),
        "f0_b2": cat("L0_ffn_eb2", "L0_ffn_sb2"),
        "f0_rw": np.ascontiguousarray(a["L0_ffn_router_w"].T),
        "f0_nw": np.ascontiguousarray(a["L0_ffn_norm_weight"][:, None]),
        "f1_w1": np.ascontiguousarray(a["L1_ffn_W1"].transpose(1, 0, 2)),
        "f1_lns": np.ascontiguousarray(a["L1_ffn_ln_scale"].T),
        "f1_lnb": np.ascontiguousarray(a["L1_ffn_ln_bias"].T),
        "f1_b1": np.ascontiguousarray(a["L1_ffn_b1"].reshape(-1, P).T),
        "f1_w2": np.ascontiguousarray(a["L1_ffn_W2"].reshape(-1, P, P).transpose(1, 0, 2)),
        "f1_b2": np.ascontiguousarray(a["L1_ffn_b2"]),
        "f1_wg": np.ascontiguousarray(a["L1_ffn_Wg"].T),
        "f1_expand": np.repeat(np.eye(E1, dtype=np.float32), H1, axis=1),
    }
    nc = bacc.Bacc("TRN2", target_bir_lowering=False, num_devices=1)
    ins = {n: nc.dram_tensor(f"in_{n}", v.shape, mybir.dt.from_np(v.dtype), kind="ExternalInput").ap()
           for n, v in arrays.items()}
    out = nc.dram_tensor("out", (P, B, P), F32, kind="ExternalOutput").ap()
    program(nc, ins, out)
    got = run_bass_kernel_spmd(nc, [{f"in_{n}": v for n, v in arrays.items()}], core_ids=[0]).results[0]["out"]
    return np.ascontiguousarray(got.transpose(1, 0, 2))
```

```python
from contextlib import ExitStack

import numpy as np

import concourse.bass as bass
from concourse import mybir

P = 128
B = 32
H, D = 16, 8
BLK = 8
GB = 4
G = B // GB
GT = GB * P
E0, HID = 8, 512
NE = E0 + 1
HB = HID // P
E1, H1 = 8, 32
SLOTS = 2
BODY = SLOTS * GB
Q_TERMS = (0, 0, 0, 1, 1, 2)
K_TERMS = (0, 1, 2, 0, 1, 0)
STACK_ROWS = 16 * len(Q_TERMS)
STACKS = 3 * len(Q_TERMS)
POOL_STACKS = 4
MAX_ROWS = 2 * 2 * BLK
PARTS_C = 3
CONSTS = 7
SCALE = float(1.0 / np.sqrt(np.float32(D)))
EPS_LN, EPS_RMS, EPS_TOP = 1e-5, 1e-8, 1e-6

ALU = mybir.AluOpType
ACT = mybir.ActivationFunctionType
F32 = mybir.dt.float32
BF16 = mybir.dt.bfloat16
F32R = mybir.dt.float32r
U32 = mybir.dt.uint32
AX = mybir.AxisListType.X


def wait(eng, sem, value):
    if not (isinstance(value, int) and value <= 0):
        eng.wait_ge(sem, value)


def group_steps(eng, step):
    step(0, 0)
    step(0, 1)
    with eng.Fori(1, G // 2 - 1) as i:
        step(i, 0)
        step(i, 1)
    step(G // 2 - 1, 0)
    step(G // 2 - 1, 1)


def has_group(i, par, ahead):
    return not isinstance(i, int) or 0 <= 2 * i + par + ahead < G


def batch_steps(eng, step):
    for k in range(BODY):
        step(0, k)
    with eng.Fori(1, B // BODY - 1) as i:
        for k in range(BODY):
            step(i, k)
    for k in range(BODY + 4):
        step(B // BODY - 1 + k // BODY, k % BODY)


def has_batch(i, k, off):
    return not isinstance(i, int) or 0 <= BODY * i + k + off < B


def stacked_count(g):
    if isinstance(g, int) and g <= SLOTS:
        return 16 * STACKS * g
    return 16 * (STACKS - POOL_STACKS) * g + 16 * POOL_STACKS * SLOTS


class Kernel:
    def __init__(self, nc, ins, out):
        self.nc, self.ins, self.out = nc, ins, out
        self.ctx = ExitStack()
        self.open_sems = []

    def sb(self, name, shape, dtype=F32):
        return self.ctx.enter_context(self.nc.sbuf_tensor(name, shape, dtype))

    def sem(self, name):
        self.open_sems.append(self.nc.alloc_semaphore(name=name))
        return self.open_sems[-1]

    def renew_semaphores(self):
        self.nc.clear_and_free_semaphores(self.open_sems)
        self.open_sems = []
        self.nc.all_engine_barrier()

    def wait_apart(self, eng, *counts):
        counts = [(sem, value if isinstance(value, int) else eng.to_reg(value)) for sem, value in counts]
        eng.wait_ge(self.const_done, CONSTS)
        for sem, value in counts:
            wait(eng, sem, value)

    def sems(self, prefix, names):
        return {n: self.sem(f"{prefix}_{n}") for n in names.split()}

    def build(self):
        nc = self.nc
        with self.ctx:
            self.x = self.sb("x", [P, B, P])
            sc = self.sb("scratch", [P, 8 * GT])[:]
            self.c_in = sc[:, 0:2 * GT].rearrange("p (r n) -> p r n", r=2)
            self.cT = sc[:, 2 * GT:4 * GT].rearrange("p (r n) -> p r n", r=2)
            self.xT = sc[:, 4 * GT:6 * GT].rearrange("p (r n) -> p r n", r=2)
            self.xn = sc[:, 6 * GT:7 * GT]
            self.hat = sc[:, 7 * GT:8 * GT]
            self.temp = self.sb("temp", [P, 4, GT])
            self.attn_w = self.sb("attn_w", [P, 6, P])
            self.rope_t = self.sb("rope_t", [P, 2, P])
            self.ident = self.sb("ident", [P, P])
            self.ident16 = self.sb("ident16", [P, P], BF16)
            self.head_rows = self.sb("head_rows", [P, 2, BLK, P], BF16)
            self.expert_rows = self.sb("expert_rows", [PARTS_C * E0, E0, P], BF16)
            self.half = self.sb("half", [P, 8])
            self.zero = self.sb("zero", [P, 1])
            self.iota8 = self.sb("iota8", [P, 8])
            self.psum = self.ctx.enter_context(nc.psum_tensor("psum", [P, 8, 512], F32))
            self.consts()
            self.attention(0)
            self.ffn0()
            self.renew_semaphores()
            self.attention(1)
            self.ffn1()

    def stack_copies(self, g, slot, parts, q_stack, k_stack):
        copies = [(q_stack[16 * t:16 * t + 16, slot], parts[0][:, part, bass.ts(g, GT)])
                  for t, part in enumerate(Q_TERMS)]
        for par in range(2):
            for t, part in enumerate(K_TERMS):
                r0 = 16 * t + 8 * par
                copies.append((k_stack[par][r0:r0 + 8, slot],
                               parts[1][64 * par:64 * par + 64, part, bass.ts(g, GT)]))
        return copies

    def consts(self):
        nc = self.nc
        done = self.const_done = nc.alloc_semaphore(name="const_done")
        ii = self.sb("iota_int", [P, 8], mybir.dt.int32)
        with nc.Block() as block:
            @block.gpsimd
            def _(pool):
                nc.gpsimd.memset(self.ident[:], 0.0).then_inc(done, 1)
                pool.wait_ge(done, 1)
                nc.gpsimd.affine_select(out=self.ident[:], in_=self.ident[:], compare_op=ALU.not_equal, fill=1.0,
                                        base=0, pattern=[[-1, P]], channel_multiplier=1).then_inc(done, 1)
                nc.gpsimd.iota(ii[:], pattern=[[1, 8]], base=0, channel_multiplier=0).then_inc(done, 1)
                pool.wait_ge(done, 3)
                nc.gpsimd.tensor_copy(self.ident16[:], self.ident[:]).then_inc(done, 1)
                nc.gpsimd.tensor_copy(self.iota8[:], ii[:]).then_inc(done, 1)
                nc.gpsimd.memset(self.half[:], -0.5).then_inc(done, 1)
                nc.gpsimd.memset(self.zero[:], 0.0).then_inc(done, 1)

    def make_head_rows(self, pool, done, part):
        nc = self.nc
        if part == 0:
            nc.gpsimd.memset(self.head_rows[:], 0.0).then_inc(done, 1)
        pool.wait_ge(done, 1 + part)
        nc.gpsimd.affine_select(out=self.head_rows[:], in_=self.head_rows[:], compare_op=ALU.not_equal, fill=1.0,
                                base=-STACK_ROWS - BLK * part, pattern=[[-2 * BLK, 2], [-1, BLK], [0, P]],
                                channel_multiplier=1).then_inc(done, 1)

    def make_expert_rows(self, pool, done):
        nc = self.nc
        nc.gpsimd.memset(self.expert_rows[:], 0.0).then_inc(done, 1)
        for part in range(PARTS_C):
            pool.wait_ge(done, 1 + part)
            nc.gpsimd.affine_select(out=self.expert_rows[:], in_=self.expert_rows[:], compare_op=ALU.not_equal,
                                    fill=1.0, base=-E0 * part, pattern=[[-1, E0], [0, P]],
                                    channel_multiplier=1).then_inc(done, 1)

    def transpose_in(self, pe, bank, src, **kw):
        for j in range(GB):
            last = self.nc.tensor.transpose(self.psum[:, bank, j * P:(j + 1) * P], src[:, j * P:(j + 1) * P],
                                            self.ident[:])
        return last

    def attention(self, l):
        nc, ps = self.nc, self.psum
        rope = l == 0
        s = self.sems(f"a{l}", """w_in cleared stats mv veps rstd xn xn_tr c_tr xT cT q_mm qs_mm k_mm ks_mm v_mm
            t1 t2 rot high rest mid low v_out stacked stacked_rest zeroed head_rows p1 negmax expert_rows head_rows_in
            nm_zero split_high split nm_tr nm_out
            p2 exps v_st pv u_out u_tr den y y_tr yT o_mm x_add""")
        x_in = [self.sem(f"a{l}_x_in_{n}") for n in ("group0", "group1", "rest")]
        c_in = [self.sem(f"a{l}_c_in{r}") for r in range(2)]

        with ExitStack() as local:
            def sb(name, shape, dtype=F32):
                return local.enter_context(nc.sbuf_tensor(f"a{l}_{name}", shape, dtype))

            v_all = sb("v", [P, B, P])
            parts = [sb(f"{n}_parts", [P, 3, B * P], BF16) for n in "qk"]
            q_stack = sb("q_stack", [P, SLOTS, BLK * GT], BF16)
            k_stack = [sb(f"k_stack{par}", [P, SLOTS, BLK * GT], BF16) for par in range(2)]
            bn = sb("bn", [P, GB, 6])
            mv = sb("mv", [P, GB, 2])
            veps = sb("veps", [P, GB])
            rstd = sb("rstd", [P, GB])
            negmax = sb("negmax", [P, 2, 2, BLK])
            nm_cols = sb("nm_cols", [P, 2, P], BF16)
            nm_parts = nm_cols[:, :, STACK_ROWS:P].rearrange("p r (a n b) -> p r a n b", a=2, n=2)
            v_st = sb("v_st", [P, 2, H, D + 1])
            u = sb("u", [P, 4, P])
            rden = sb("rden", [P, H])
            y = sb("y", [P, P])
            yT = sb("yT", [P, P])
            w_q, w_qs, w_k, w_ks, w_v, w_o = (self.attn_w[:, n] for n in range(6))
            t2_k = sb("t2_k", [P, GT])
            t2, rot, rest = [self.temp[:, 0], t2_k[:]], [self.temp[:, 1], self.temp[:, 2]], [self.temp[:, 3], self.hat]
            cos4 = self.rope_t[:, 0:1].to_broadcast([P, GB, P])
            sin4 = self.rope_t[:, 1:2].to_broadcast([P, GB, P])
            pt = self.temp[:].rearrange("p (r a) n -> p r (a n)", r=2).rearrange("p r (a b t) -> p r a b t", a=2, b=4)
            XN_BANK, C_BANK, Q_BANK, QS_BANK, K_BANK, KS_BANK, V_BANK = range(7)
            P1_BANK, P2_BANK, PV_BANK, TAIL_BANK = 0, 2, 6, 7
            nm_psum = ps[:, TAIL_BANK].bitcast(BF16)[:, 4 * P:5 * P]

            def four(ap):
                return ap.rearrange("p (b t) -> p b t", b=GB)

            with nc.Block() as block:
                @block.sync
                def _(sp):
                    if l == 0:
                        sp.dma_start(self.x[:, 0:GB], self.ins["x"][:, 0:GB]).then_inc(x_in[0], 16)
                    sp.dma_start(self.attn_w[:], self.ins[f"attn_w{l}"]).then_inc(s["w_in"], 16)
                    if rope:
                        sp.dma_start(self.rope_t[:], self.ins["rope"]).then_inc(s["w_in"], 16)
                    if l == 0:
                        for g in range(1, G):
                            sp.dma_start(self.x[:, bass.ts(g, GB)], self.ins["x"][:, bass.ts(g, GB)],
                                         ).then_inc(x_in[min(g, 2)], 16)

                    def stack(g, slot):
                        self.wait_apart(sp, (s["high"], 2 * g + 2), (s["mid"], 2 * g + 2), (s["low"], 2 * g + 2),
                                        (s["stacked"], stacked_count(g)))
                        if not isinstance(g, int):
                            self.wait_apart(sp, (s["p2"], 2 * GB * (g - SLOTS + 1)))
                        else:
                            sp.wait_ge(s["cleared"], 2 * g + 2)
                        copies = self.stack_copies(g, slot, parts, q_stack, k_stack)
                        for dst, src in copies if isinstance(g, int) else copies[:-POOL_STACKS]:
                            sp.dma_start(dst, src).then_inc(s["stacked"], 16)

                    if l == 0:
                        sp.wait_ge(s["head_rows"], 3)
                    for slot in range(SLOTS):
                        for par in range(2):
                            for j in range(GB):
                                rows = k_stack[par][STACK_ROWS:P, slot].rearrange("p (b j t) -> p j b t", b=BLK, j=GB)
                                sp.dma_start(rows[:, j], self.head_rows[STACK_ROWS:P, par]
                                             ).then_inc(s["head_rows_in"], 16)
                    for g in range(SLOTS):
                        stack(g, g)
                    with sp.Fori(1, G // SLOTS) as i:
                        for slot in range(SLOTS):
                            stack(SLOTS * i + slot, slot)

                @block.gpsimd
                def _(pool):
                    def inverse_std(g):
                        self.wait_apart(pool, (s["mv"], g + 1))
                        nc.gpsimd.tensor_scalar(veps[:], mv[:, :, 1], EPS_LN, None, ALU.add).then_inc(s["veps"], 1)
                        pool.wait_ge(s["veps"], g + 1)
                        nc.gpsimd.tensor_tensor(rstd[:], veps[:], self.half[:, 0:GB], ALU.pow).then_inc(s["rstd"], 1)

                    def low(n, w, g):
                        pool.wait_ge(s["mid"], n + 1)
                        nc.gpsimd.tensor_tensor(parts[w][:, 2, bass.ts(g, GT)], rest[w],
                                                parts[w][:, 1, bass.ts(g, GT)], ALU.subtract).then_inc(s["low"], 1)

                    if l == 0:
                        for part in range(2):
                            self.make_head_rows(pool, s["head_rows"], part)
                    inverse_std(0)
                    inverse_std(1)

                    def project(i, par):
                        g = 2 * i + par
                        if rope:
                            for w in range(2):
                                pool.wait_ge(s["t1"], 2 * g + w + 1)
                                pool.wait_ge(s["t2"], 2 * g + w + 1)
                                nc.gpsimd.tensor_tensor(rot[w], rot[w], t2[w], ALU.add).then_inc(s["rot"], 1)
                        if has_group(i, par, 2):
                            inverse_std(g + 2)
                        low(2 * g, 0, g)
                        low(2 * g + 1, 1, g)

                    group_steps(pool, project)
                    nc.gpsimd.memset(nm_cols[:], 0.0).then_inc(s["nm_zero"], 1)
                    pool.wait_ge(s["nm_zero"], 1)
                    for r in range(2):
                        last = nc.gpsimd.memset(v_st[:, r, :, D:D + 1], 1.0)
                    last.then_inc(s["v_st"], 1)
                    pool.wait_ge(s["v_out"], G)

                    def step(i, k):
                        b = BODY * i + k
                        if has_batch(i, k, -1):
                            self.wait_apart(pool, (s["pv"], 2 * (b - 2)))
                            nc.gpsimd.tensor_copy(v_st[:, (k - 1) % 2, :, 0:D],
                                                  v_all[:, b - 1].rearrange("p (h d) -> p h d", h=H),
                                                  ).then_inc(s["v_st"], 1)
                        if has_batch(i, k, 0):
                            r = k % 2
                            self.wait_apart(pool, (s["negmax"], 4 * b + 4), (s["nm_tr"], b - 1))
                            nc.gpsimd.tensor_copy(nm_parts[:, r, :, 0], negmax[:, r]).then_inc(s["split_high"], 1)
                            pool.wait_ge(s["split_high"], b + 1)
                            nc.gpsimd.tensor_tensor(nm_parts[:, r, :, 1], negmax[:, r], nm_parts[:, r, :, 0],
                                                    ALU.subtract).then_inc(s["split"], 1)
                        g = SLOTS * i + k // GB + 1
                        if k % GB == 1 and not (isinstance(g, int) and not SLOTS <= g < G):
                            self.wait_apart(pool, (s["p2"], 2 * GB * (g - SLOTS + 1)))
                            copies = self.stack_copies(g, (k // GB + 1) % SLOTS, parts, q_stack, k_stack)
                            for dst, src in copies[-POOL_STACKS:]:
                                pool.dma_start(dst, src).then_inc(s["stacked_rest"], 16)

                    batch_steps(pool, step)
                    if l == 0:
                        self.make_expert_rows(pool, s["expert_rows"])

                @block.scalar
                def _(act):
                    def load(g, par):
                        act.dma_start(four(self.c_in[:, par]), self.ins["ctx"][:, bass.ts(g, GB)],
                                      ).then_inc(c_in[par], 16)

                    def copy_c(g, par):
                        act.wait_ge(s["c_tr"], g + 1)
                        wait(act, s["v_mm"], g - 1)
                        nc.scalar.activation(self.cT[:, par], ps[:, C_BANK], ACT.Copy).then_inc(s["cT"], 1)

                    def copy_x(g, par):
                        act.wait_ge(s["xn_tr"], g + 1)
                        wait(act, s["qs_mm" if rope else "q_mm"], g - 1)
                        nc.scalar.activation(self.xT[:, par], ps[:, XN_BANK], ACT.Copy).then_inc(s["xT"], 1)

                    def high(w, g):
                        if rope:
                            act.wait_ge(s["rot"], 2 * g + w + 1)
                        else:
                            act.wait_ge(s[("q_mm", "k_mm")[w]], g + 1)
                        nc.scalar.activation(parts[w][:, 0, bass.ts(g, GT)],
                                             rot[w] if rope else ps[:, (Q_BANK, K_BANK)[w]],
                                             ACT.Copy).then_inc(s["high"], 1)

                    def middle(w, g):
                        act.wait_ge(s["rest"], 2 * g + w + 1)
                        nc.scalar.activation(parts[w][:, 1, bass.ts(g, GT)], rest[w], ACT.Copy,
                                             ).then_inc(s["mid"], 1)

                    load(0, 0)
                    load(1, 1)
                    copy_c(0, 0)
                    copy_x(0, 0)

                    def project(i, par):
                        g = 2 * i + par
                        if has_group(i, par, 2):
                            act.wait_ge(s["c_tr"], g + 1)
                            load(g + 2, par)
                        high(0, g)
                        if has_group(i, par, 1):
                            copy_c(g + 1, 1 - par)
                            copy_x(g + 1, 1 - par)
                        high(1, g)
                        act.wait_ge(s["v_mm"], g + 1)
                        nc.scalar.activation(v_all[:, bass.ts(g, GB)], four(ps[:, V_BANK]), ACT.Copy,
                                             ).then_inc(s["v_out"], 1)
                        middle(0, g)
                        middle(1, g)
                        if isinstance(i, int) and i == 0:
                            for stack in k_stack:
                                words = stack[0:STACK_ROWS, par].bitcast(F32)
                                nc.scalar.activation(words, self.zero[0:STACK_ROWS].to_broadcast(
                                    [STACK_ROWS, BLK * GT // 2]), ACT.Copy,
                                                     ).then_inc(s["cleared"], 1)

                    group_steps(act, project)

                    act.wait_ge(s["low"], 2 * G)
                    act.wait_ge(s["rest"], 2 * G)

                    def step(i, k):
                        b = BODY * i + k

                        def exp(unit):
                            n = 2 * (b - 2) + unit
                            act.wait_ge(s["p2"], n + 1)
                            wait(act, s["pv"], n - 1)
                            nc.scalar.activation(pt[:, unit].rearrange("p a b t -> p (a b t)"),
                                                 ps[:, P2_BANK + 2 * unit:P2_BANK + 2 * unit + 2]
                                                 .rearrange("p a n -> p (a n)"),
                                                 ACT.Exp, scale=SCALE).then_inc(s["exps"], 1)

                        if has_batch(i, k, -3):
                            act.wait_ge(s["pv"], 2 * (b - 3) + 2)
                            wait(act, s["u_tr"], b - 3)
                            nc.scalar.activation(u[:], four(ps[:, PV_BANK]), ACT.Copy).then_inc(s["u_out"], 1)
                        if has_batch(i, k, -2):
                            exp(0)
                            exp(1)
                        if has_batch(i, k, -3):
                            act.wait_ge(s["y_tr"], b - 2)
                            wait(act, s["o_mm"], b - 3)
                            nc.scalar.activation(yT[:], ps[:, TAIL_BANK, 0:P], ACT.Copy).then_inc(s["yT"], 1)
                        if has_batch(i, k, -1):
                            act.wait_ge(s["nm_tr"], b)
                            if has_batch(i, k, -3):
                                act.wait_ge(s["y_tr"], b - 2)
                            wait(act, s["p2"], 2 * (b - 3) + 2)
                            rows = q_stack[STACK_ROWS:P, (k - 1) % BODY // GB].rearrange(
                                "p (b j t) -> p b j t", b=BLK, j=GB)[:, :, (k - 1) % GB]
                            nc.scalar.activation(rows, nm_psum[STACK_ROWS:P].unsqueeze(1).to_broadcast(
                                [MAX_ROWS, BLK, P]), ACT.Copy).then_inc(s["nm_out"], 1)

                    batch_steps(act, step)

                @block.vector
                def _(dve):
                    def statistics(g):
                        if l == 0:
                            first = isinstance(g, int) and g < 2
                            dve.wait_ge(x_in[g if first else 2], 16 if first else 16 * (G - 2))
                        wait(dve, s["xn"], g)
                        for j in range(GB):
                            last = nc.vector.bn_stats(bn[:, j], self.x[:, 4 * g + j])
                        last.then_inc(s["stats"], 1)
                        self.wait_apart(dve, (s["stats"], g + 1), (s["rstd"], g))
                        for j in range(GB):
                            last = nc.vector.bn_aggr(mv[:, j], bn[:, j])
                        last.then_inc(s["mv"], 1)

                    def norm(g):
                        dve.wait_ge(s["mv"], g + 1)
                        dve.wait_ge(s["rstd"], g + 1)
                        wait(dve, s["xn_tr"], g)
                        for j in range(GB):
                            last = nc.vector.tensor_scalar(self.xn[:, j * P:(j + 1) * P], self.x[:, 4 * g + j],
                                                           mv[:, j, 0:1], rstd[:, j:j + 1], ALU.subtract, ALU.mult)
                        last.then_inc(s["xn"], 1)

                    def rotate(w, g):
                        n = 2 * g + w
                        dve.wait_ge(s[("q_mm", "k_mm")[w]], g + 1)
                        wait(dve, s["high"], n - 1)
                        wait(dve, s["rest"], n - 1)
                        nc.vector.tensor_tensor(four(rot[w]), four(ps[:, (Q_BANK, K_BANK)[w]]), cos4, ALU.mult,
                                                ).then_inc(s["t1"], 1)
                        dve.wait_ge(s[("qs_mm", "ks_mm")[w]], g + 1)
                        wait(dve, s["rot"], n - 1)
                        nc.vector.tensor_tensor(four(t2[w]), four(ps[:, (QS_BANK, KS_BANK)[w]]), sin4, ALU.mult,
                                                ).then_inc(s["t2"], 1)

                    def remainder(w, g):
                        n = 2 * g + w
                        if rope:
                            dve.wait_ge(s["rot"], n + 1)
                        dve.wait_ge(s["high"], n + 1)
                        wait(dve, s["low"], n - 1)
                        nc.vector.tensor_tensor(rest[w], rot[w] if rope else ps[:, (Q_BANK, K_BANK)[w]],
                                                parts[w][:, 0, bass.ts(g, GT)], ALU.subtract).then_inc(s["rest"], 1)

                    statistics(0)
                    norm(0)
                    statistics(1)
                    dve.wait_ge(s["w_in"], 32 if rope else 16)

                    def project(i, par):
                        g = 2 * i + par
                        if rope:
                            rotate(0, g)
                        if has_group(i, par, 1):
                            norm(g + 1)
                        if rope:
                            rotate(1, g)
                        if has_group(i, par, 2):
                            statistics(g + 2)
                        remainder(0, g)
                        remainder(1, g)

                    group_steps(dve, project)
                    dve.wait_ge(s["v_out"], G)
                    nc.vector.memset(ps[:, PV_BANK], 0.0).then_inc(s["zeroed"], 1)

                    def step(i, k):
                        b = BODY * i + k
                        r = k % 2

                        def maxima(unit):
                            half, par = unit // 2, unit % 2
                            dve.wait_ge(s["p1"], 4 * b + unit + 1)
                            if unit == 0:
                                wait(dve, s["split"], b - 1)
                            nc.vector.tensor_reduce(negmax[:, r, par, 4 * half:4 * half + 4],
                                                    ps[:, P1_BANK + par].rearrange("p (b t) -> p b t", b=4),
                                                    AX, ALU.max, negate=True).then_inc(s["negmax"], 1)

                        if has_batch(i, k, 0):
                            maxima(0)
                            maxima(1)
                            maxima(2)
                        if has_batch(i, k, -4):
                            dve.wait_ge(s["o_mm"], b - 3)
                            nc.vector.tensor_tensor(self.x[:, b - 4], ps[:, TAIL_BANK, P:2 * P], self.x[:, b - 4],
                                                    ALU.add).then_inc(s["x_add"], 1)
                        if has_batch(i, k, 0):
                            maxima(3)
                        if has_batch(i, k, -3):
                            dve.wait_ge(s["u_tr"], b - 2)
                            sums = ps[:, TAIL_BANK].rearrange("p (h n) -> p h n", h=H)
                            nc.vector.reciprocal(rden[:], sums[:, :, D]).then_inc(s["den"], 1)
                            dve.wait_ge(s["den"], b - 2)
                            wait(dve, s["y_tr"], b - 3)
                            nc.vector.tensor_tensor(y[:].rearrange("p (h d) -> p h d", h=H), sums[:, :, 0:D],
                                                    rden[:].unsqueeze(2).to_broadcast([P, H, D]),
                                                    ALU.mult).then_inc(s["y"], 1)

                    batch_steps(dve, step)

                @block.tensor
                def _(pe):
                    def transpose_c(g, par, loads):
                        pe.wait_ge(c_in[par], 16 * loads)
                        wait(pe, s["cT"], g)
                        self.transpose_in(pe, C_BANK, self.c_in[:, par]).then_inc(s["c_tr"], 1)

                    def transpose_x(g):
                        pe.wait_ge(s["xn"], g + 1)
                        wait(pe, s["xT"], g)
                        self.transpose_in(pe, XN_BANK, self.xn).then_inc(s["xn_tr"], 1)

                    def product(w, weight, swapped, rhs, g):
                        wait(pe, s["t2" if rope else "rest"], 2 * (g - 1) + w + 1)
                        mm, mms = (("q_mm", "qs_mm"), ("k_mm", "ks_mm"))[w]
                        nc.tensor.matmul(ps[:, (Q_BANK, K_BANK)[w]], weight, rhs, start=True, stop=True,
                                         ).then_inc(s[mm], 1)
                        if rope:
                            nc.tensor.matmul(ps[:, (QS_BANK, KS_BANK)[w]], swapped, rhs, start=True, stop=True,
                                             ).then_inc(s[mms], 1)

                    pe.wait_ge(s["w_in"], 32 if rope else 16)
                    transpose_c(0, 0, 1)
                    transpose_x(0)

                    def project(i, par):
                        g = 2 * i + par
                        pe.wait_ge(s["xT"], g + 1)
                        product(0, w_q, w_qs, self.xT[:, par], g)
                        pe.wait_ge(s["cT"], g + 1)
                        product(1, w_k, w_ks, self.cT[:, par], g)
                        if has_group(i, par, 1):
                            transpose_c(g + 1, 1 - par, i + (par + 1) // 2 + 1)
                            transpose_x(g + 1)
                        wait(pe, s["v_out"], g)
                        for j in range(GB):
                            cols = slice(j * P, (j + 1) * P)
                            last = nc.tensor.matmul(ps[:, V_BANK, cols], self.cT[:, par, cols], w_v,
                                                    start=True, stop=True)
                        last.then_inc(s["v_mm"], 1)

                    group_steps(pe, project)
                    pe.wait_ge(s["rest"], 2 * G)
                    pe.wait_ge(s["zeroed"], 1)
                    pe.wait_ge(s["head_rows_in"], 16 * 2 * SLOTS * GB)

                    def step(i, k):
                        b = BODY * i + k

                        def stacked(k, stack, blk, rows=STACK_ROWS):
                            return stack[0:rows, k // GB, blk * GT + k % GB * P:blk * GT + (k % GB + 1) * P]

                        def p1(half):
                            if half == 0 and k % GB == 0:
                                g = SLOTS * i + k // GB
                                pe.wait_ge(s["stacked"], stacked_count(g + 1))
                                wait(pe, s["stacked_rest"], 16 * POOL_STACKS * (g + 1 - SLOTS))
                            for par in range(2):
                                unit = 2 * half + par
                                wait(pe, s["negmax"], 4 * b + unit - 1)
                                for j in range(4):
                                    last = nc.tensor.matmul(ps[:, P1_BANK + par, j * P:(j + 1) * P],
                                                            stacked(k, q_stack, 4 * half + j),
                                                            stacked(k, k_stack[par], 4 * half + j),
                                                            start=True, stop=True)
                                last.then_inc(s["p1"], 1)

                        def p2(half):
                            if half == 0:
                                pe.wait_ge(s["nm_out"], b - 1)
                            wait(pe, s["exps"], 2 * (b - 3) + half + 1)
                            for par in range(2):
                                for j in range(4):
                                    blk, out = 4 * half + j, ps[:, P2_BANK + 2 * half + par, j * P:(j + 1) * P]
                                    last = nc.tensor.matmul(out, stacked((k - 2) % BODY, k_stack[par], blk, P),
                                                            stacked((k - 2) % BODY, q_stack, blk, P),
                                                            start=True, stop=True)
                            last.then_inc(s["p2"], 1)

                        def pv(half, c, r):
                            if half == 0:
                                pe.wait_ge(s["v_st"], c + 2)
                                wait(pe, s["u_out"], c)
                            pe.wait_ge(s["exps"], 2 * c + half + 1)
                            for par in range(2):
                                for j in range(4):
                                    last = nc.tensor.matmul(ps[32 * j:32 * j + D + 1, PV_BANK,
                                                               (2 * par + half) * P:(2 * par + half + 1) * P],
                                                            v_st[:, r, 8 * par + 4 * half + j],
                                                            pt[:, half, par, j], start=True, stop=True,
                                                            tile_position=(0, 32 * j))
                            last.then_inc(s["pv"], 1)

                        if has_batch(i, k, 0):
                            p1(0)
                        if has_batch(i, k, -3):
                            pv(1, b - 3, (k - 3) % 2)
                        if has_batch(i, k, -4):
                            pe.wait_ge(s["yT"], b - 3)
                            if has_batch(i, k, -2):
                                pe.wait_ge(s["nm_out"], b - 1)
                            nc.tensor.matmul(ps[:, TAIL_BANK, P:2 * P], yT[:], w_o, start=True, stop=True
                                             ).then_inc(s["o_mm"], 1)
                        if has_batch(i, k, 0):
                            p1(1)
                        if has_batch(i, k, -2):
                            p2(0)
                        if has_batch(i, k, -2):
                            p2(1)
                        if has_batch(i, k, -3):
                            pe.wait_ge(s["u_out"], b - 2)
                            wait(pe, s["x_add"], b - 3)
                            if has_batch(i, k, -2):
                                wait(pe, s["nm_out"], b - 1)
                            for n in range(4):
                                last = nc.tensor.transpose(ps[:, TAIL_BANK, n * P:(n + 1) * P], u[:, n], self.ident[:])
                            last.then_inc(s["u_tr"], 1)
                        if has_batch(i, k, -2):
                            pv(0, b - 2, k % 2)
                        sums_read = [(s["y"], b - 2)] if has_batch(i, k, -3) else []
                        if has_batch(i, k, -1):
                            self.wait_apart(pe, (s["split"], b), (s["nm_out"], b - 1), *sums_read)
                            nc.tensor.transpose(nm_psum, nm_cols[:, (k - 1) % 2], self.ident16[:]).then_inc(s["nm_tr"], 1)
                        if has_batch(i, k, -3):
                            pe.wait_ge(s["y"], b - 2)
                            nc.tensor.transpose(ps[:, TAIL_BANK, 0:P], y[:], self.ident[:]).then_inc(s["y_tr"], 1)

                    batch_steps(pe, step)

    def ffn0(self):
        nc, ps = self.nc, self.psum
        s = self.sems("f0", """small_in w_hi w_lo stats mv veps rstd hat sq sveps srstd xn xn_tr xT x_hi x_lo logit_mm
            prob top8 idx idxf m0 m1 mask picked total rtot comb c_hi c_rest c_mid c_low comb_tr combT parts_tr
            parts_out up spread relu weighted h_hi h_lo down out_copy out_tr acc""")
        experts_in = [self.sem(f"f0_experts_in{r}") for r in range(2)]
        UP_BANK, OUT_BANK, SPREAD_BANK, T_BANK, MISC_BANK = 0, 4, 5, 6, 7
        NC = PARTS_C * E0
        parts_psum = ps[0:NC, T_BANK].bitcast(BF16)[:, 0:GT]
        outT = self.c_in[:, 0]

        with ExitStack() as local:
            def sb(name, shape, dtype=F32):
                return local.enter_context(nc.sbuf_tensor(f"f0_{name}", shape, dtype))

            b1 = sb("b1", [P, NE * HB])
            b2 = sb("b2", [NE, P])
            rw = sb("rw", [P, E0])
            nw = sb("nw", [P, 1])
            bn = sb("bn", [P, GB, 6])
            mv = sb("mv", [P, GB, 2])
            veps = sb("veps", [P, GB])
            rstd = sb("rstd", [P, GB])
            sq = sb("sq", [P, GB])
            sveps = sb("sveps", [P, GB])
            srstd = sb("srstd", [P, GB])
            prob = sb("prob", [P, GB, E0])
            top8 = sb("top8", [P, GB, E0])
            idx = sb("idx", [P, GB, E0], U32)
            idxf = sb("idxf", [P, GB, 2])
            m0 = sb("m0", [P, GB, E0])
            m1 = sb("m1", [P, GB, E0])
            mask = sb("mask", [P, GB, E0])
            picked = sb("picked", [P, GB, E0])
            total = sb("total", [P, GB])
            rtot = sb("rtot", [P, GB])
            comb = sb("comb", [P, 2, GB, NE])
            w_in = sb("w_in", [P, 2, 2, HID])
            w1_hi, w1_lo = (sb(f"w1_{n}", [P, NE, HID], F32R) for n in ("hi", "lo"))
            w2_hi, w2_lo = (sb(f"w2_{n}", [P, NE, HB, P], F32R) for n in ("hi", "lo"))
            x_hi, x_lo = (sb(f"x_{n}", [P, 2, GT], F32R) for n in ("hi", "lo"))
            h_hi, h_lo = (sb(f"h_{n}", [P, 2, HB, GT], F32R) for n in ("hi", "lo"))
            hid = sb("hid", [P, 2, HB, GT])
            c_rest = sb("c_rest", [P, GB, E0])
            c_parts = sb("c_parts", [P, GB, 3, E0], BF16)
            combT = self.temp[0:NE, 0:2]
            partsT = self.temp[0:NC, 2].bitcast(BF16).rearrange("p (r n) -> p r n", r=2)
            hat, xn, xT = self.hat, self.xn, self.xT

            def cols(ap, j):
                return ap[:, j * P:(j + 1) * P]

            def eight(ap):
                return ap.to_broadcast([P, GB, E0])

            with nc.Block() as block:
                @block.sync
                def _(sp):
                    for dst, name in ((b1, "f0_b1"), (b2, "f0_b2"), (rw, "f0_rw"), (nw, "f0_nw")):
                        sp.dma_start(dst[:], self.ins[name]).then_inc(s["small_in"], 16)
                    for e in range(NE):
                        if e >= 2:
                            sp.wait_ge(s["w_lo"], 2 * e - 2)
                        for k, name in enumerate(("f0_w1", "f0_w2")):
                            sp.dma_start(w_in[:, e % 2, k], self.ins[name][:, e]).then_inc(experts_in[e % 2], 16)

                @block.gpsimd
                def _(pool):
                    def roots(g):
                        self.wait_apart(pool, (s["mv"], g + 1))
                        nc.gpsimd.tensor_scalar(veps[:], mv[:, :, 1], EPS_LN, None, ALU.add).then_inc(s["veps"], 1)
                        pool.wait_ge(s["veps"], g + 1)
                        nc.gpsimd.tensor_tensor(rstd[:], veps[:], self.half[:, 0:GB], ALU.pow).then_inc(s["rstd"], 1)

                    def square_roots(g):
                        self.wait_apart(pool, (s["sq"], g + 1))
                        nc.gpsimd.tensor_scalar(sveps[:], sq[:], 1.0 / P, EPS_RMS, ALU.mult, ALU.add,
                                                ).then_inc(s["sveps"], 1)
                        pool.wait_ge(s["sveps"], g + 1)
                        nc.gpsimd.tensor_tensor(srstd[:], sveps[:], self.half[:, 0:GB], ALU.pow,
                                                ).then_inc(s["srstd"], 1)

                    def x_low(g, par):
                        pool.wait_ge(s["x_hi"], g + 1)
                        nc.gpsimd.tensor_tensor(x_lo[:, par], xT[:, par], x_hi[:, par], ALU.subtract,
                                                ).then_inc(s["x_lo"], 1)

                    def split_comb(g, par):
                        w = comb[:, par, :, 0:E0]
                        self.wait_apart(pool, (s["comb"], g + 2), (s["parts_tr"], g))
                        nc.gpsimd.tensor_copy(c_parts[:, :, 0], w).then_inc(s["c_hi"], 1)
                        pool.wait_ge(s["c_hi"], g + 1)
                        nc.gpsimd.tensor_tensor(c_rest[:], w, c_parts[:, :, 0], ALU.subtract).then_inc(s["c_rest"], 1)
                        self.wait_apart(pool, (s["c_rest"], g + 1))
                        nc.gpsimd.tensor_copy(c_parts[:, :, 1], c_rest[:]).then_inc(s["c_mid"], 1)
                        pool.wait_ge(s["c_mid"], g + 1)
                        nc.gpsimd.tensor_tensor(c_parts[:, :, 2], c_rest[:], c_parts[:, :, 1], ALU.subtract,
                                                ).then_inc(s["c_low"], 1)

                    roots(0)
                    square_roots(0)
                    x_low(0, 0)
                    split_comb(0, 0)

                    def step(i, par):
                        g = 2 * i + par
                        for e in range(NE):
                            if has_group(i, par, 1):
                                if e == 0:
                                    roots(g + 1)
                                if e == 2:
                                    square_roots(g + 1)
                                if e == 4:
                                    x_low(g + 1, 1 - par)
                                if e == 7:
                                    split_comb(g + 1, 1 - par)
                            n, r = NE * g + e, (par + e) % 2
                            for hb in range(HB):
                                pool.wait_ge(s["h_hi"], HB * n + hb + 1)
                                nc.gpsimd.tensor_tensor(h_lo[:, r, hb], hid[:, r, hb], h_hi[:, r, hb],
                                                        ALU.subtract).then_inc(s["h_lo"], 1)

                    group_steps(pool, step)

                @block.scalar
                def _(act):
                    def squares(g):
                        act.wait_ge(s["hat"], g + 1)
                        wait(act, s["srstd"], g)
                        for j in range(GB):
                            last = nc.scalar.activation(cols(xn, j), cols(hat, j), ACT.Square,
                                                        accum_out=sq[:, j:j + 1])
                        last.then_inc(s["sq"], 1)

                    def copy_xT(g, par):
                        act.wait_ge(s["xn_tr"], g + 1)
                        wait(act, s["logit_mm"], g - 1)
                        wait(act, s["x_lo"], g - 1)
                        nc.scalar.activation(xT[:, par], ps[:, T_BANK], ACT.Copy, scale=nw[:, 0:1]
                                             ).then_inc(s["xT"], 1)
                        act.wait_ge(s["xT"], g + 1)
                        wait(act, s["up"], NE * HB * (g - 1))
                        nc.scalar.activation(x_hi[:, par], xT[:, par], ACT.Copy).then_inc(s["x_hi"], 1)

                    def probs(g):
                        act.wait_ge(s["logit_mm"], g + 1)
                        wait(act, s["comb"], g + 1)
                        nc.scalar.activation(prob[:], ps[:, MISC_BANK, 0:GB * E0].rearrange("p (j e) -> p j e", j=GB),
                                             ACT.Sigmoid).then_inc(s["prob"], 1)

                    def copy_comb(g, par):
                        act.wait_ge(s["comb_tr"], g + 1)
                        wait(act, s["down"], NE * (g - 1))
                        nc.scalar.activation(combT[:, par], ps[0:NE, MISC_BANK], ACT.Copy).then_inc(s["combT"], 1)
                        act.wait_ge(s["parts_tr"], g + 1)
                        wait(act, s["spread"], E0 * (g - 1))
                        nc.scalar.activation(partsT[:, par], parts_psum, ACT.Copy).then_inc(s["parts_out"], 1)

                    def split_weights(e):
                        act.wait_ge(experts_in[e % 2], 32 * (e // 2 + 1))
                        for k, hi in enumerate((w1_hi[:, e], w2_hi[:, e].rearrange("p b n -> p (b n)"))):
                            nc.scalar.activation(hi, w_in[:, e % 2, k], ACT.Copy).then_inc(s["w_hi"], 1)

                    def relu(n, e, r, hb):
                        act.wait_ge(s["up"], HB * n + hb + 1)
                        wait(act, s["h_lo"], HB * (n - 2) + hb + 1)
                        nc.scalar.activation(hid[:, r, hb], ps[:, UP_BANK + hb], ACT.Relu,
                                             bias=b1[:, HB * e + hb:HB * e + hb + 1]).then_inc(s["relu"], 1)

                    def high(n, g, e, r, hb):
                        if e < E0:
                            act.wait_ge(s["weighted"], HB * (E0 * g + e) + hb + 1)
                        else:
                            act.wait_ge(s["relu"], HB * n + hb + 1)
                        if hb == 0:
                            wait(act, s["down"], n - 1)
                        nc.scalar.activation(h_hi[:, r, hb], hid[:, r, hb], ACT.Copy,
                                             ).then_inc(s["h_hi"], 1)

                    def copy_out(g):
                        act.wait_ge(s["down"], NE * (g + 1))
                        wait(act, s["out_tr"], g)
                        nc.scalar.activation(outT, ps[:, OUT_BANK], ACT.Copy).then_inc(s["out_copy"], 1)

                    squares(0)
                    split_weights(0)
                    act.wait_ge(s["small_in"], 64)
                    copy_xT(0, 0)
                    probs(0)
                    copy_comb(0, 0)

                    def step(i, par):
                        g = 2 * i + par
                        for e in range(NE):
                            n, r = NE * g + e, (par + e) % 2
                            if isinstance(i, int) and i == 0 and par == 0 and e < E0:
                                split_weights(e + 1)
                            relu(n, e, r, 0)
                            relu(n, e, r, 1)
                            high(n, g, e, r, 0)
                            relu(n, e, r, 2)
                            high(n, g, e, r, 1)
                            relu(n, e, r, 3)
                            high(n, g, e, r, 2)
                            high(n, g, e, r, 3)
                            if e == 0 and has_group(i, par, -1):
                                copy_out(g - 1)
                            if has_group(i, par, 1):
                                if e == 1:
                                    squares(g + 1)
                                if e == 3:
                                    copy_xT(g + 1, 1 - par)
                                if e == 5:
                                    probs(g + 1)
                                if e == 8:
                                    copy_comb(g + 1, 1 - par)

                    group_steps(act, step)
                    copy_out(G - 1)

                @block.vector
                def _(dve):
                    def norm1(g):
                        for j in range(GB):
                            last = nc.vector.bn_stats(bn[:, j], self.x[:, 4 * g + j])
                        last.then_inc(s["stats"], 1)
                        self.wait_apart(dve, (s["stats"], g + 1), (s["rstd"], g))
                        for j in range(GB):
                            last = nc.vector.bn_aggr(mv[:, j], bn[:, j])
                        last.then_inc(s["mv"], 1)

                    def hats(g):
                        dve.wait_ge(s["mv"], g + 1)
                        dve.wait_ge(s["rstd"], g + 1)
                        wait(dve, s["sq"], g)
                        for j in range(GB):
                            last = nc.vector.tensor_scalar(cols(hat, j), self.x[:, 4 * g + j], mv[:, j, 0:1],
                                                           rstd[:, j:j + 1], ALU.subtract, ALU.mult)
                        last.then_inc(s["hat"], 1)

                    def norm2(g):
                        dve.wait_ge(s["hat"], g + 1)
                        dve.wait_ge(s["sq"], g + 1)
                        dve.wait_ge(s["srstd"], g + 1)
                        wait(dve, s["xn_tr"], g)
                        for j in range(GB):
                            last = nc.vector.tensor_scalar(cols(xn, j), cols(hat, j), srstd[:, j:j + 1], None,
                                                           ALU.mult)
                        last.then_inc(s["xn"], 1)

                    def route(g, par):
                        self.wait_apart(dve, (s["prob"], g + 1))
                        for j in range(GB):
                            last = nc.vector.max(top8[:, j], prob[:, j])
                        last.then_inc(s["top8"], 1)
                        self.wait_apart(dve, (s["top8"], g + 1))
                        for j in range(GB):
                            last = nc.vector.max_index(idx[:, j], top8[:, j], prob[:, j])
                        last.then_inc(s["idx"], 1)
                        dve.wait_ge(s["idx"], g + 1)
                        nc.vector.tensor_copy(idxf[:], idx[:, :, 0:2]).then_inc(s["idxf"], 1)
                        dve.wait_ge(s["idxf"], g + 1)
                        iota = self.iota8[:].unsqueeze(1).to_broadcast([P, GB, E0])
                        nc.vector.tensor_tensor(m0[:], iota, eight(idxf[:, :, 0:1]), ALU.is_equal).then_inc(s["m0"], 1)
                        nc.vector.tensor_tensor(m1[:], iota, eight(idxf[:, :, 1:2]), ALU.is_equal).then_inc(s["m1"], 1)
                        dve.wait_ge(s["m0"], g + 1)
                        dve.wait_ge(s["m1"], g + 1)
                        nc.vector.tensor_tensor(mask[:], m0[:], m1[:], ALU.add).then_inc(s["mask"], 1)
                        dve.wait_ge(s["mask"], g + 1)
                        nc.vector.tensor_tensor(picked[:], mask[:], prob[:], ALU.mult).then_inc(s["picked"], 1)
                        nc.vector.scalar_tensor_tensor(total[:], top8[:, :, 0], EPS_TOP, top8[:, :, 1], ALU.add,
                                                       ALU.add).then_inc(s["total"], 1)
                        dve.wait_ge(s["total"], g + 1)
                        nc.vector.reciprocal(rtot[:], total[:]).then_inc(s["rtot"], 1)
                        dve.wait_ge(s["rtot"], g + 1)
                        dve.wait_ge(s["picked"], g + 1)
                        wait(dve, s["comb_tr"], g - 1)
                        wait(dve, s["c_low"], g - 1)
                        nc.vector.tensor_tensor(comb[:, par, :, 0:E0], picked[:], eight(rtot[:].unsqueeze(2)),
                                                ALU.mult).then_inc(s["comb"], 1)

                    def split_weights(e):
                        for k, (hi, lo) in enumerate(((w1_hi, w1_lo), (w2_hi, w2_lo))):
                            hi, lo = (t[:, e] if k == 0 else t[:, e].rearrange("p b n -> p (b n)") for t in (hi, lo))
                            dve.wait_ge(s["w_hi"], 2 * e + k + 1)
                            nc.vector.tensor_tensor(lo, w_in[:, e % 2, k], hi, ALU.subtract).then_inc(s["w_lo"], 1)

                    def accumulate(g):
                        dve.wait_ge(s["out_tr"], g + 1)
                        nc.vector.tensor_tensor(self.x[:, bass.ts(g, GB)],
                                                ps[:, T_BANK].rearrange("p (j n) -> p j n", j=GB),
                                                self.x[:, bass.ts(g, GB)], ALU.add).then_inc(s["acc"], 1)

                    for r in range(2):
                        last = nc.vector.memset(comb[:, r, :, E0:NE], 1.0)
                    last.then_inc(s["comb"], 1)
                    norm1(0)
                    hats(0)
                    norm2(0)
                    split_weights(0)
                    route(0, 0)

                    def step(i, par):
                        g = 2 * i + par
                        for e in range(NE):
                            n, r = NE * g + e, (par + e) % 2
                            if has_group(i, par, 1):
                                if e == 0:
                                    norm1(g + 1)
                                if e == 1:
                                    hats(g + 1)
                                if e == 3:
                                    norm2(g + 1)
                                if e == 6:
                                    route(g + 1, 1 - par)
                            if isinstance(i, int) and i == 0 and par == 0 and e < E0:
                                split_weights(e + 1)
                            if e < E0:
                                dve.wait_ge(s["spread"], E0 * g + e + 1)
                                for hb in range(HB):
                                    dve.wait_ge(s["relu"], HB * n + hb + 1)
                                    nc.vector.tensor_tensor(hid[:, r, hb], hid[:, r, hb], ps[:, SPREAD_BANK],
                                                            ALU.mult).then_inc(s["weighted"], 1)
                            if e == 1 and has_group(i, par, -1):
                                accumulate(g - 1)

                    group_steps(dve, step)
                    accumulate(G - 1)

                @block.tensor
                def _(pe):
                    def transposes(g):
                        pe.wait_ge(s["xn"], g + 1)
                        wait(pe, s["parts_out"], g)
                        wait(pe, s["acc"], g - 1)
                        self.transpose_in(pe, T_BANK, xn).then_inc(s["xn_tr"], 1)

                    def logits(g, par):
                        pe.wait_ge(s["xT"], g + 1)
                        wait(pe, s["combT"], g)
                        for j in range(GB):
                            last = nc.tensor.matmul(ps[:, MISC_BANK, j * E0:(j + 1) * E0], cols(xT[:, par], j), rw[:],
                                                    start=True, stop=True)
                        last.then_inc(s["logit_mm"], 1)

                    def comb_transpose(g, par):
                        pe.wait_ge(s["comb"], g + 2)
                        pe.wait_ge(s["prob"], g + 1)
                        for j in range(GB):
                            last = nc.tensor.transpose(ps[0:NE, MISC_BANK, j * P:(j + 1) * P], comb[:, par, j],
                                                       self.ident[:])
                        last.then_inc(s["comb_tr"], 1)
                        pe.wait_ge(s["c_low"], g + 1)
                        pe.wait_ge(s["xT"], g + 1)
                        for j in range(GB):
                            last = nc.tensor.transpose(parts_psum[:, j * P:(j + 1) * P],
                                                       c_parts[:, j].rearrange("p n e -> p (n e)"), self.ident16[:])
                        last.then_inc(s["parts_tr"], 1)

                    def exact(out, w_hi, w_lo, x_hi, x_lo, start, stop):
                        terms = ((w_hi, x_hi), (w_lo, x_hi), (w_hi, x_lo))
                        for t, (w, x) in enumerate(terms):
                            last = nc.tensor.matmul(out, w, x, start=start and t == 0,
                                                    stop=stop and t == len(terms) - 1)
                        return last

                    def up(n, g, e, par, first):
                        pe.wait_ge(s["x_lo"], g + 1)
                        if first:
                            pe.wait_ge(s["w_lo"], 2 * e + 1)
                        for hb in range(HB):
                            wait(pe, s["relu"], HB * (n - 1) + hb + 1)
                            exact(ps[:, UP_BANK + hb], w1_hi[:, e, hb * P:(hb + 1) * P], w1_lo[:, e, hb * P:(hb + 1) * P],
                                  x_hi[:, par], x_lo[:, par], True, True).then_inc(s["up"], 1)

                    def spread(g, e, par):
                        pe.wait_ge(s["parts_out"], g + 1)
                        wait(pe, s["weighted"], HB * (E0 * g + e))
                        nc.tensor.matmul(ps[:, SPREAD_BANK], self.expert_rows[:, e], partsT[:, par],
                                         start=True, stop=True).then_inc(s["spread"], 1)

                    def down(n, g, e, par, first):
                        r = (par + e) % 2
                        if first:
                            pe.wait_ge(s["w_lo"], 2 * e + 2)
                        if e == 0:
                            pe.wait_ge(s["combT"], g + 1)
                            wait(pe, s["out_copy"], g)
                            nc.tensor.matmul(ps[:, OUT_BANK], b2[:], combT[:, par], start=True, stop=False)
                        for hb in range(HB):
                            pe.wait_ge(s["h_lo"], HB * n + hb + 1)
                            last = exact(ps[:, OUT_BANK], w2_hi[:, e, hb], w2_lo[:, e, hb], h_hi[:, r, hb],
                                         h_lo[:, r, hb], False, e == NE - 1 and hb == HB - 1)
                        last.then_inc(s["down"], 1)

                    def transpose_out(g, more):
                        pe.wait_ge(s["out_copy"], g + 1)
                        if more:
                            pe.wait_ge(s["parts_out"], g + 2)
                        self.transpose_in(pe, T_BANK, outT).then_inc(s["out_tr"], 1)

                    pe.wait_ge(s["small_in"], 64)
                    transposes(0)
                    logits(0, 0)
                    comb_transpose(0, 0)

                    def step(i, par):
                        g = 2 * i + par
                        first = isinstance(i, int) and i == 0 and par == 0
                        for e in range(NE):
                            n = NE * g + e
                            up(n, g, e, par, first)
                            if e < E0:
                                spread(g, e, par)
                            if e == 1 and has_group(i, par, -1):
                                transpose_out(g - 1, True)
                            if has_group(i, par, 1):
                                if e == 3:
                                    transposes(g + 1)
                                if e == 5:
                                    logits(g + 1, 1 - par)
                                if e == 8:
                                    comb_transpose(g + 1, 1 - par)
                            if e > 0:
                                down(n - 1, g, e - 1, par, first)
                            elif has_group(i, par, -1):
                                down(n - 1, g - 1, NE - 1, 1 - par, False)

                    group_steps(pe, step)
                    down(NE * G - 1, G - 1, NE - 1, 1, False)
                    transpose_out(G - 1, False)

    def ffn1(self):
        nc, ps = self.nc, self.psum
        s = self.sems("f1", """w_in w_folded fold_mm bias expand stats mv veps rstd xt xstats xmv xveps xrstd xh
            xt_tr xh_tr xtT xhT logit_mm logit top8 idx idxf mask mask_tr maskT mask16 up gelu spread hm down out
            out_dma""")
        XT_BANK, XH_BANK, UP_BANK, SPREAD_BANK, DOWN_BANK, MISC_BANK = 0, 1, 2, 4, 6, 7
        NB1 = E1 * H1 // P
        xt, xh = self.xn, self.hat
        xtT, xhT = self.xT, self.cT

        with ExitStack() as local:
            def sb(name, shape, dtype=F32):
                return local.enter_context(nc.sbuf_tensor(f"f1_{name}", shape, dtype))

            w1 = sb("w1", [P, E1, H1])
            w1s = sb("w1s", [P, E1, H1])
            lns = sb("lns", [P, E1])
            lnb = sb("lnb", [P, E1])
            b1 = sb("b1", [P, NB1])
            b1e = sb("b1e", [P, NB1])
            w2 = sb("w2", [P, NB1, P])
            b2 = sb("b2", [E1, P])
            wg = sb("wg", [P, E1])
            expand = sb("expand", [E1, NB1 * P])
            expand16 = sb("expand16", [E1, NB1 * P], BF16)
            bn = sb("bn", [P, 2, GB, 6])
            mv = sb("mv", [P, 2, GB, 2])
            veps = sb("veps", [P, 2, GB])
            rstd = sb("rstd", [P, 2, GB])
            logit = sb("logit", [P, GB, E1])
            top8 = sb("top8", [P, GB, E1])
            idx = sb("idx", [P, GB, E1], U32)
            idxf = sb("idxf", [P, GB, 1])
            mask = sb("mask", [P, GB, E1])
            maskT = sb("maskT", [E1, GT])
            mask16 = sb("mask16", [E1, GT], BF16)
            hg = sb("hg", [P, 2, NB1, GT])
            hm = sb("hm", [P, NB1, GT])

            def cols(ap, j):
                return ap[:, j * P:(j + 1) * P]

            with nc.Block() as block:
                @block.sync
                def _(sp):
                    pairs = ((w1, "f1_w1"), (lns, "f1_lns"), (lnb, "f1_lnb"), (b1, "f1_b1"), (w2, "f1_w2"),
                             (b2, "f1_b2"), (wg, "f1_wg"), (expand, "f1_expand"))
                    for dst, name in pairs:
                        sp.dma_start(dst[:], self.ins[name]).then_inc(s["w_in"], 16)
                    with sp.Fori(0, G) as g:
                        sp.wait_ge(s["out"], g + 1)
                        sp.dma_start(self.out[:, bass.ts(g, GB)], self.x[:, bass.ts(g, GB)]).then_inc(s["out_dma"], 16)
                    sp.wait_ge(s["out_dma"], 16 * G)

                @block.gpsimd
                def _(pool):
                    def inverse_std(g, which, ready, add, done):
                        self.wait_apart(pool, (s[ready], g + 1))
                        nc.gpsimd.tensor_scalar(veps[:, which], mv[:, which, :, 1], EPS_LN, None, ALU.add,
                                                ).then_inc(s[add], 1)
                        pool.wait_ge(s[add], g + 1)
                        nc.gpsimd.tensor_tensor(rstd[:, which], veps[:, which], self.half[:, 0:GB], ALU.pow,
                                                ).then_inc(s[done], 1)

                    with pool.Fori(0, G) as g:
                        inverse_std(g, 0, "mv", "veps", "rstd")
                        inverse_std(g, 1, "xmv", "xveps", "xrstd")

                @block.scalar
                def _(act):
                    def inputs(g):
                        act.wait_ge(s["xt_tr"], g + 1)
                        wait(act, s["logit_mm"], g)
                        nc.scalar.activation(xtT[:, 0], ps[:, XT_BANK], ACT.Copy).then_inc(s["xtT"], 1)
                        act.wait_ge(s["xh_tr"], g + 1)
                        wait(act, s["up"], 2 * g)
                        nc.scalar.activation(xhT[:, 0], ps[:, XH_BANK], ACT.Copy).then_inc(s["xhT"], 1)

                    def gelu(g, par):
                        wait(act, s["hm"], 2 * (g - 1))
                        for blk in range(NB1):
                            act.wait_ge(s["up"], 2 * g + blk + 1)
                            nc.scalar.activation(hg[:, par, blk], ps[:, UP_BANK + blk], ACT.Gelu,
                                                 bias=b1e[:, blk:blk + 1]).then_inc(s["gelu"], 1)

                    def masks(g):
                        act.wait_ge(s["mask_tr"], g + 1)
                        wait(act, s["down"], g)
                        nc.scalar.activation(maskT[:], ps[0:E1, MISC_BANK], ACT.Copy).then_inc(s["maskT"], 1)
                        wait(act, s["spread"], g)
                        nc.scalar.activation(mask16[:], ps[0:E1, MISC_BANK], ACT.Copy).then_inc(s["mask16"], 1)

                    inputs(0)
                    act.wait_ge(s["w_in"], 16 * 8)
                    nc.scalar.activation(expand16[:], expand[:], ACT.Copy).then_inc(s["expand"], 1)
                    act.wait_ge(s["bias"], 1)
                    gelu(0, 0)

                    def step(i, par):
                        g = 2 * i + par
                        masks(g)
                        if has_group(i, par, 1):
                            inputs(g + 1)
                        if has_group(i, par, 1):
                            gelu(g + 1, 1 - par)

                    group_steps(act, step)

                @block.vector
                def _(dve):
                    def statistics(g, which, src, stats, mvs, ready):
                        for j in range(GB):
                            last = nc.vector.bn_stats(bn[:, which, j], src[j])
                        last.then_inc(s[stats], 1)
                        self.wait_apart(dve, (s[stats], g + 1), (s[ready], g))
                        for j in range(GB):
                            last = nc.vector.bn_aggr(mv[:, which, j], bn[:, which, j])
                        last.then_inc(s[mvs], 1)

                    def norm(g, which, src, dst, mvs, ready, read, done):
                        dve.wait_ge(s[mvs], g + 1)
                        dve.wait_ge(s[ready], g + 1)
                        wait(dve, s[read], g)
                        for j in range(GB):
                            last = nc.vector.tensor_scalar(cols(dst, j), src[j], mv[:, which, j, 0:1],
                                                           rstd[:, which, j:j + 1], ALU.subtract, ALU.mult)
                        last.then_inc(s[done], 1)

                    def norm_parts(g):
                        x = [self.x[:, 4 * g + j] for j in range(GB)]
                        y = [cols(xt, j) for j in range(GB)]
                        return (lambda: statistics(g, 0, x, "stats", "mv", "rstd"),
                                lambda: norm(g, 0, x, xt, "mv", "rstd", "xt_tr", "xt"),
                                lambda: (dve.wait_ge(s["xt"], g + 1), statistics(g, 1, y, "xstats", "xmv", "xrstd")),
                                lambda: norm(g, 1, y, xh, "xmv", "xrstd", "xh_tr", "xh"))

                    def norms(g):
                        for part in norm_parts(g):
                            part()

                    def route(g):
                        dve.wait_ge(s["logit_mm"], g + 1)
                        nc.vector.tensor_copy(logit[:], ps[:, MISC_BANK, 0:GB * E1].rearrange("p (j e) -> p j e", j=GB),
                                              ).then_inc(s["logit"], 1)
                        self.wait_apart(dve, (s["logit"], g + 1))
                        for j in range(GB):
                            last = nc.vector.max(top8[:, j], logit[:, j])
                        last.then_inc(s["top8"], 1)
                        self.wait_apart(dve, (s["top8"], g + 1))
                        for j in range(GB):
                            last = nc.vector.max_index(idx[:, j], top8[:, j], logit[:, j])
                        last.then_inc(s["idx"], 1)
                        dve.wait_ge(s["idx"], g + 1)
                        nc.vector.tensor_copy(idxf[:], idx[:, :, 0:1]).then_inc(s["idxf"], 1)
                        dve.wait_ge(s["idxf"], g + 1)
                        wait(dve, s["mask_tr"], g)
                        nc.vector.tensor_tensor(mask[:], self.iota8[:].unsqueeze(1).to_broadcast([P, GB, E1]),
                                                idxf[:].to_broadcast([P, GB, E1]), ALU.is_equal).then_inc(s["mask"], 1)

                    norms(0)
                    dve.wait_ge(s["w_in"], 16 * 8)
                    for e in range(E1):
                        last = nc.vector.tensor_scalar(w1s[:, e], w1[:, e], lns[:, e:e + 1], None, ALU.mult)
                    last.then_inc(s["w_folded"], 1)
                    dve.wait_ge(s["fold_mm"], 1)
                    nc.vector.tensor_tensor(b1e[:], ps[:, DOWN_BANK, 0:NB1], b1[:], ALU.add).then_inc(s["bias"], 1)
                    route(0)
                    norms(1)

                    def step(i, par):
                        g = 2 * i + par
                        ahead = has_group(i, par, 2)
                        if ahead:
                            norm0, norm1, norm2, norm3 = norm_parts(g + 2)
                            norm0()
                        dve.wait_ge(s["spread"], g + 1)
                        wait(dve, s["down"], g)
                        for blk in range(NB1):
                            dve.wait_ge(s["gelu"], 2 * g + blk + 1)
                            nc.vector.tensor_tensor(hm[:, blk], hg[:, par, blk], ps[:, SPREAD_BANK + blk],
                                                    ALU.mult).then_inc(s["hm"], 1)
                        if ahead:
                            norm1()
                            norm2()
                        if has_group(i, par, 1):
                            route(g + 1)
                        if ahead:
                            norm3()
                        dve.wait_ge(s["down"], g + 1)
                        nc.vector.tensor_tensor(self.x[:, bass.ts(g, GB)],
                                                ps[:, DOWN_BANK].rearrange("p (j n) -> p j n", j=GB),
                                                self.x[:, bass.ts(g, GB)], ALU.add).then_inc(s["out"], 1)

                    group_steps(dve, step)

                @block.tensor
                def _(pe):
                    def transposes(g):
                        pe.wait_ge(s["xt"], g + 1)
                        wait(pe, s["xtT"], g)
                        self.transpose_in(pe, XT_BANK, xt).then_inc(s["xt_tr"], 1)
                        pe.wait_ge(s["xh"], g + 1)
                        wait(pe, s["xhT"], g)
                        self.transpose_in(pe, XH_BANK, xh).then_inc(s["xh_tr"], 1)

                    def logits(g):
                        pe.wait_ge(s["xtT"], g + 1)
                        wait(pe, s["mask16"], g)
                        for j in range(GB):
                            last = nc.tensor.matmul(ps[:, MISC_BANK, j * E1:(j + 1) * E1], cols(xtT[:, 0], j), wg[:],
                                                    start=True, stop=True)
                        last.then_inc(s["logit_mm"], 1)

                    def up(g):
                        pe.wait_ge(s["xhT"], g + 1)
                        for blk in range(NB1):
                            wait(pe, s["gelu"], 2 * (g - 1) + blk + 1)
                            nc.tensor.matmul(ps[:, UP_BANK + blk],
                                             w1s[:, 4 * blk:4 * blk + 4].rearrange("p e h -> p (e h)"), xhT[:, 0],
                                             start=True, stop=True).then_inc(s["up"], 1)

                    transposes(0)
                    pe.wait_ge(s["w_in"], 16 * 8)
                    for e in range(E1):
                        c = 32 * (e % 4)
                        last = nc.tensor.matmul(ps[c:c + 32, DOWN_BANK, e // 4:e // 4 + 1], w1[:, e], lnb[:, e:e + 1],
                                                start=True, stop=True, tile_position=(0, c))
                    last.then_inc(s["fold_mm"], 1)
                    logits(0)
                    pe.wait_ge(s["w_folded"], 1)
                    up(0)
                    pe.wait_ge(s["expand"], 1)
                    pe.wait_ge(s["bias"], 1)

                    def step(i, par):
                        g = 2 * i + par
                        pe.wait_ge(s["mask"], g + 1)
                        for j in range(GB):
                            last = nc.tensor.transpose(ps[0:E1, MISC_BANK, j * P:(j + 1) * P], mask[:, j],
                                                       self.ident[:])
                        last.then_inc(s["mask_tr"], 1)
                        if has_group(i, par, 1):
                            transposes(g + 1)
                        pe.wait_ge(s["mask16"], g + 1)
                        wait(pe, s["hm"], 2 * g)
                        for blk in range(NB1):
                            last = nc.tensor.matmul(ps[:, SPREAD_BANK + blk], expand16[:, blk * P:(blk + 1) * P],
                                                    mask16[:], start=True, stop=True)
                        last.then_inc(s["spread"], 1)
                        if has_group(i, par, 1):
                            logits(g + 1)
                            up(g + 1)
                        pe.wait_ge(s["hm"], 2 * g + 2)
                        wait(pe, s["out"], g)
                        for j in range(GB):
                            out = ps[:, DOWN_BANK, j * P:(j + 1) * P]
                            nc.tensor.matmul(out, cols(maskT, j), b2[:], start=True, stop=False)
                            for blk in range(NB1):
                                last = nc.tensor.matmul(out, cols(hm[:, blk], j), w2[:, blk], start=False,
                                                        stop=(blk == NB1 - 1))
                        last.then_inc(s["down"], 1)

                    group_steps(pe, step)


def program(nc, ins, out):
    Kernel(nc, ins, out).build()


def rope_tables():
    freqs = (np.float32(1.0) / np.float32(10000.0) ** (np.arange(0, P, 2, dtype=np.float32) / np.float32(P)))
    ang = np.outer(np.arange(P, dtype=np.float32), freqs.astype(np.float32)).astype(np.float32)
    cos, sin = np.cos(ang), np.sin(ang)
    order = channel_order()
    sign = np.where(order % 2 == 0, -1.0, 1.0).astype(np.float32)
    return np.stack([cos.T[order // 2], sin.T[order // 2] * sign[:, None]], axis=1).astype(np.float32)


def channel_order():
    return np.arange(P).reshape(2, BLK, D).transpose(0, 2, 1).reshape(-1)


def kernel(**inputs):
    import concourse.bacc as bacc
    from concourse.bass_utils import run_bass_kernel_spmd

    a = {k: np.asarray(v) for k, v in inputs.items()}
    order = channel_order()
    arrays = {
        "x": np.ascontiguousarray(a["x"].transpose(1, 0, 2)),
        "ctx": np.ascontiguousarray(a["ctx_1024"].transpose(1, 0, 2)),
        "rope": rope_tables(),
    }
    for l, (q, k, v, o) in enumerate((("L0_xattn_Wq", "L0_xattn_Wk", "L0_xattn_Wv", "L0_xattn_Wo"),
                                      ("L1_xattn_w_q", "L1_xattn_w_k", "L1_xattn_w_v", "L1_xattn_w_o"))):
        arrays[f"attn_w{l}"] = np.ascontiguousarray(np.stack(
            [a[q][order].T, a[q][order ^ 1].T, a[k][order].T, a[k][order ^ 1].T, a[v].T, a[o].T], axis=1))
    def cat(experts, shared):
        return np.concatenate([a[experts], a[shared][None]], axis=0)

    arrays |= {
        "f0_w1": np.ascontiguousarray(cat("L0_ffn_ew1", "L0_ffn_sw1").transpose(1, 0, 2)),
        "f0_b1": np.ascontiguousarray(cat("L0_ffn_eb1", "L0_ffn_sb1").reshape(NE * HB, P).T),
        "f0_w2": np.ascontiguousarray(
            cat("L0_ffn_ew2", "L0_ffn_sw2").reshape(NE, HB, P, P).transpose(2, 0, 1, 3).reshape(P, NE, HID)),
        "f0_b2": cat("L0_ffn_eb2", "L0_ffn_sb2"),
        "f0_rw": np.ascontiguousarray(a["L0_ffn_router_w"].T),
        "f0_nw": np.ascontiguousarray(a["L0_ffn_norm_weight"][:, None]),
        "f1_w1": np.ascontiguousarray(a["L1_ffn_W1"].transpose(1, 0, 2)),
        "f1_lns": np.ascontiguousarray(a["L1_ffn_ln_scale"].T),
        "f1_lnb": np.ascontiguousarray(a["L1_ffn_ln_bias"].T),
        "f1_b1": np.ascontiguousarray(a["L1_ffn_b1"].reshape(-1, P).T),
        "f1_w2": np.ascontiguousarray(a["L1_ffn_W2"].reshape(-1, P, P).transpose(1, 0, 2)),
        "f1_b2": np.ascontiguousarray(a["L1_ffn_b2"]),
        "f1_wg": np.ascontiguousarray(a["L1_ffn_Wg"].T),
        "f1_expand": np.repeat(np.eye(E1, dtype=np.float32), H1, axis=1),
    }
    nc = bacc.Bacc("TRN2", target_bir_lowering=False, num_devices=1)
    ins = {n: nc.dram_tensor(f"in_{n}", v.shape, mybir.dt.from_np(v.dtype), kind="ExternalInput").ap()
           for n, v in arrays.items()}
    out = nc.dram_tensor("out", (P, B, P), F32, kind="ExternalOutput").ap()
    program(nc, ins, out)
    got = run_bass_kernel_spmd(nc, [{f"in_{n}": v for n, v in arrays.items()}], core_ids=[0]).results[0]["out"]
    return np.ascontiguousarray(got.transpose(1, 0, 2))
```
